# Optimizing a Trainium2 kernel written in Bass

```python
import numpy as np
import jax
import jax.numpy as jnp

def _softmax(x, axis=-1):
    return jax.nn.softmax(x, axis=axis)

def _gelu(x):
    return jax.nn.gelu(x, approximate=True)

def _silu(x):
    return jax.nn.silu(x)

def _sigmoid(x):
    return jax.nn.sigmoid(x)

def _layernorm(x, axis=-1, eps=1e-05):
    m = jnp.mean(x, axis=axis, keepdims=True)
    v = jnp.var(x, axis=axis, keepdims=True)
    return (x - m) / jnp.sqrt(v + eps)

def _scatter_add(tgt, idx, src, axis=0):
    return tgt.at[idx].add(src)

def _segment_sum(src, seg, n):
    return jax.ops.segment_sum(src, seg, n)
kernel_name = 'mk_gnn_ffn_d1_gnn_r8_4796fd'

def setup_inputs(seed: int=0):
    np.random.seed(seed)
    _w = jnp.asarray

    def _rec_inputs():
        import jax
        import jax.numpy as jnp
        _gk = jax.random.key(seed)
        x = -8.776e-05 + 1 * jax.random.normal(jax.random.fold_in(_gk, 1), (6250, 512), jnp.float32)
        src = jax.random.randint(jax.random.fold_in(_gk, 2), (100000,), 0, 6250, jnp.int32)
        dst = jax.random.randint(jax.random.fold_in(_gk, 3), (100000,), 0, 6250, jnp.int32)
        _o = jnp.argsort(dst, stable=True)
        src = src[_o]
        dst = dst[_o]
        return (x, src, dst)
    x, src, dst = _rec_inputs()

    def _L0_gnn_setup():
        import jax, jax.numpy as jnp
        import numpy as np
        N, E, D = (1250, 20000, 512)

        def _sage_layer(h, src, dst, W_self, W_neigh, b, n_nodes):
            agg = jax.ops.segment_sum(h[src], dst, num_segments=n_nodes)
            deg = jax.ops.segment_sum(jnp.ones_like(dst, dtype=h.dtype), dst, num_segments=n_nodes)
            h_neigh = agg / jnp.maximum(deg, 1.0)[:, None]
            return jax.nn.relu(h @ W_self + h_neigh @ W_neigh + b)
        key = jax.random.key(seed)
        ks = jax.random.split(key, 8)
        scale = 1.0 / np.sqrt(D)
        return {'feats': jax.random.normal(ks[0], (N, D), dtype=jnp.float32), 'src': jax.random.randint(ks[1], (E,), 0, N, dtype=jnp.int32), 'dst': jax.random.randint(ks[2], (E,), 0, N, dtype=jnp.int32), 'W_self1': jax.random.normal(ks[3], (D, D), dtype=jnp.float32) * scale, 'W_neigh1': jax.random.normal(ks[4], (D, D), dtype=jnp.float32) * scale, 'b1': jnp.zeros((D,), dtype=jnp.float32), 'W_self2': jax.random.normal(ks[5], (D, D), dtype=jnp.float32) * scale, 'W_neigh2': jax.random.normal(ks[6], (D, D), dtype=jnp.float32) * scale, 'b2': jnp.zeros((D,), dtype=jnp.float32)}
    _L0_gnn_all = _L0_gnn_setup()
    _L0_gnn_in = {k: v for k, v in _L0_gnn_all.items() if k in ('W_self1', 'W_neigh1', 'b1', 'W_self2', 'W_neigh2', 'b2')}
    del _L0_gnn_all

    def _L0_ffn_setup():
        import jax, jax.numpy as jnp
        import numpy as np
        EPS = 1e-05
        TOP_K = 2

        def _moe_forward(x, Wg, W1, b1, W2, b2, gamma, beta):
            B, S, D = x.shape
            xf = x.reshape(-1, D)
            logits = xf @ Wg
            topv, topi = jax.lax.top_k(logits, TOP_K)
            gate_w = jax.nn.softmax(topv, axis=-1)
            h = jax.nn.relu(jnp.einsum('td,edh->teh', xf, W1) + b1[None])
            y = jnp.einsum('teh,ehd->ted', h, W2) + b2[None]
            mu = jnp.mean(y, axis=-1, keepdims=True)
            var = jnp.mean((y - mu) ** 2, axis=-1, keepdims=True)
            y = (y - mu) / jnp.sqrt(var + EPS) * gamma[None] + beta[None]
            y_sel = jnp.take_along_axis(y, topi[:, :, None], axis=1)
            out = jnp.sum(gate_w[:, :, None] * y_sel, axis=1)
            return out.reshape(B, S, D)
        key = jax.random.key(seed)
        ks = jax.random.split(key, 8)
        B, S, D, H, E = (4, 256, 512, 512, 8)
        sd = lambda fan_in: 1.0 / np.sqrt(fan_in)
        x = jax.random.normal(ks[0], (B, S, D), dtype=jnp.float32)
        Wg = jax.random.uniform(ks[1], (D, E), jnp.float32, -sd(D), sd(D))
        W1 = jax.random.uniform(ks[2], (E, D, H), jnp.float32, -sd(D), sd(D))
        b1 = jax.random.uniform(ks[3], (E, H), jnp.float32, -sd(D), sd(D))
        W2 = jax.random.uniform(ks[4], (E, H, D), jnp.float32, -sd(H), sd(H))
        b2 = jax.random.uniform(ks[5], (E, D), jnp.float32, -sd(H), sd(H))
        gamma = jnp.ones((E, D), jnp.float32)
        beta = jnp.zeros((E, D), jnp.float32)
        return {'x': x, 'Wg': Wg, 'W1': W1, 'b1': b1, 'W2': W2, 'b2': b2, 'gamma': gamma, 'beta': beta}
    _L0_ffn_all = _L0_ffn_setup()
    _L0_ffn_in = {k: v for k, v in _L0_ffn_all.items() if k in ('Wg', 'W1', 'b1', 'W2', 'b2', 'gamma', 'beta')}
    del _L0_ffn_all
    return {'x': x, 'src': src, 'dst': dst, 'L0_gnn_W_self1': _L0_gnn_in['W_self1'], 'L0_gnn_W_neigh1': _L0_gnn_in['W_neigh1'], 'L0_gnn_b1': _L0_gnn_in['b1'], 'L0_gnn_W_self2': _L0_gnn_in['W_self2'], 'L0_gnn_W_neigh2': _L0_gnn_in['W_neigh2'], 'L0_gnn_b2': _L0_gnn_in['b2'], 'L0_ffn_Wg': _L0_ffn_in['Wg'], 'L0_ffn_W1': _L0_ffn_in['W1'], 'L0_ffn_b1': _L0_ffn_in['b1'], 'L0_ffn_W2': _L0_ffn_in['W2'], 'L0_ffn_b2': _L0_ffn_in['b2'], 'L0_ffn_gamma': _L0_ffn_in['gamma'], 'L0_ffn_beta': _L0_ffn_in['beta']}

def reference(x, src, dst, L0_gnn_W_self1, L0_gnn_W_neigh1, L0_gnn_b1, L0_gnn_W_self2, L0_gnn_W_neigh2, L0_gnn_b2, L0_ffn_Wg, L0_ffn_W1, L0_ffn_b1, L0_ffn_W2, L0_ffn_b2, L0_ffn_gamma, L0_ffn_beta):
    import jax
    import jax.numpy as jnp

    def _L0_gnn_ref(feats, src, dst, W_self1, W_neigh1, b1, W_self2, W_neigh2, b2):
        import jax, jax.numpy as jnp
        import numpy as np
        N, E, D = (1250, 20000, 512)

        def _sage_layer(h, src, dst, W_self, W_neigh, b, n_nodes):
            agg = jax.ops.segment_sum(h[src], dst, num_segments=n_nodes)
            deg = jax.ops.segment_sum(jnp.ones_like(dst, dtype=h.dtype), dst, num_segments=n_nodes)
            h_neigh = agg / jnp.maximum(deg, 1.0)[:, None]
            return jax.nn.relu(h @ W_self + h_neigh @ W_neigh + b)
        n_nodes = feats.shape[0]
        h = _sage_layer(feats, src, dst, W_self1, W_neigh1, b1, n_nodes)
        h = _sage_layer(h, src, dst, W_self2, W_neigh2, b2, n_nodes)
        return h

    def _L0_ffn_ref(x, Wg, W1, b1, W2, b2, gamma, beta):
        import jax, jax.numpy as jnp
        import numpy as np
        EPS = 1e-05
        TOP_K = 2

        def _moe_forward(x, Wg, W1, b1, W2, b2, gamma, beta):
            B, S, D = x.shape
            xf = x.reshape(-1, D)
            logits = xf @ Wg
            topv, topi = jax.lax.top_k(logits, TOP_K)
            gate_w = jax.nn.softmax(topv, axis=-1)
            h = jax.nn.relu(jnp.einsum('td,edh->teh', xf, W1) + b1[None])
            y = jnp.einsum('teh,ehd->ted', h, W2) + b2[None]
            mu = jnp.mean(y, axis=-1, keepdims=True)
            var = jnp.mean((y - mu) ** 2, axis=-1, keepdims=True)
            y = (y - mu) / jnp.sqrt(var + EPS) * gamma[None] + beta[None]
            y_sel = jnp.take_along_axis(y, topi[:, :, None], axis=1)
            out = jnp.sum(gate_w[:, :, None] * y_sel, axis=1)
            return out.reshape(B, S, D)
        return _moe_forward(x, Wg, W1, b1, W2, b2, gamma, beta)
    x = x + _L0_gnn_ref(_layernorm(x, axis=-1), src, dst, L0_gnn_W_self1, L0_gnn_W_neigh1, L0_gnn_b1, L0_gnn_W_self2, L0_gnn_W_neigh2, L0_gnn_b2)
    x = x + _L0_ffn_ref(_layernorm(x, axis=-1)[None], L0_ffn_Wg, L0_ffn_W1, L0_ffn_b1, L0_ffn_W2, L0_ffn_b2, L0_ffn_gamma, L0_ffn_beta)[0]
    return x

_drawn_inputs = setup_inputs


def setup_inputs(seed=0):
    import zlib

    import numpy as np

    out = dict(_drawn_inputs(seed))
    spreads = {'L0_gnn_b1': (0.0, 0.1),
     'L0_gnn_b2': (0.0, 0.1),
     'L0_ffn_gamma': (1.0, 0.2),
     'L0_ffn_beta': (0.0, 0.1)}
    factors = {}
    for name, (base, spread) in spreads.items():
        noise = np.random.default_rng([zlib.crc32(name.encode()), seed]).standard_normal(out[name].shape)
        drawn = base * np.exp(spread * noise) if base else spread * noise
        out[name] = jnp.asarray(drawn.astype(out[name].dtype))
    for name, factor in factors.items():
        out[name] = (out[name] * factor).astype(out[name].dtype)
    return out
```

```python
from contextlib import ExitStack

import numpy as np

import concourse.bass as bass
from concourse import mybir

F32 = mybir.dt.float32
F32R = mybir.dt.float32r
I32 = mybir.dt.int32
U32 = mybir.dt.uint32
ALU = mybir.AluOpType
ACT = mybir.ActivationFunctionType
AX = mybir.AxisListType

P = 128
N, D, E = 6250, 512, 100000
NE = 8
KC = D // P
NT = -(-N // P)
LAST = N - P
EPS = 1e-5

G = 9
EB, EP = 7, 112
ET = EB * EP
ETP = ET + 2 * G
FAR = 1.0e6
MAXG = -(-ET // G)
IDX_AT = {0: 5, 5: 4}
SELW = 3

LN_ROWS = 4
LN_CH = -(-N // (P * LN_ROWS))

WSPLIT_AT = (6, 10)
MIN_TILES = 3
REGION = NT * P + MIN_TILES * P
YT = 2 * NT + NE * MIN_TILES + 1
CB = 7


def start_of(g):
    return min(g * P, LAST)


def build(nc, x, src, dst, w_self1, w_neigh1, b1, w_self2, w_neigh2, b2, Wg, W1, eb1, W2, eb2, gamma, beta, out):
    xn_d = nc.dram_tensor("xn_scratch", (N, D), F32, kind="Internal").ap()
    h1_d = nc.dram_tensor("h1_scratch", (N, D), F32, kind="Internal").ap()
    x2_d = nc.dram_tensor("x2_scratch", (N, D), F32, kind="Internal").ap()
    disp_d = nc.dram_tensor("dispatch_scratch", (NE * REGION, D), F32, kind="Internal").ap()
    y_d = nc.dram_tensor("expert_out_scratch", (YT * P, D), F32, kind="Internal").ap()

    with ExitStack() as ctx:
        def sem(name):
            return ctx.enter_context(nc.semaphore(name))

        def sbc(c, name, shape, dt=F32):
            return c.enter_context(nc.sbuf_tensor(name, shape, dt))

        def sb(name, shape, dt=F32):
            return sbc(ctx, name, shape, dt)

        ident = sb("ident", [P, P])
        upper = sb("upper", [P, P])
        onesq = sb("onesq", [P, P])
        iota = sb("iota", [P, P])
        srcT = sb("srcT", [P, ETP], I32)
        dstT = sb("dstT", [P, ETP])
        start_col = sb("start_col", [P, NT])
        iota_g = sb("iota_g", [P, P])
        rdeg = sb("rdeg", [P, NT])
        zero2 = sb("zero2", [2, P], F32R)
        zero_row = sb("zero_row", [2, D], F32R)
        one2 = sb("one2", [2, P], F32R)
        ones_col = sb("ones_col", [P, 2], F32R)
        eps_col = sb("eps_col", [P, 1])
        rsel = sb("rsel", [2, 2])
        rseli = sb("rseli", [2, 2], I32)
        tab_first = sb("tab_first", [1, NT], I32)
        tab_group = sb("tab_group", [1, NT + 1], I32)
        tab_tiles = sb("tab_tiles", [1, NE + 1], I32)
        tab_last = sb("tab_last", [1, NE], I32)
        tab_rows = sb("tab_rows", [1, NE], I32)
        wts = [sb(f"wts{i}", [P, 2, 2, KC, D], F32R) for i in range(2)]
        w_raw = sb("w_raw", [P, 2, KC, D])
        bias_raw = sb("bias_raw", [2, 2, D])
        bias_t = sb("bias_t", [2, D])
        bias_u = sb("bias_u", [2, D])
        bias = [sb(f"bias{i}", [2, 2, D], F32R) for i in range(2)]
        wg_s = sb("wg_s", [P, KC, NE])
        top2 = sb("top2", [P, 2, NT])
        posf = sb("posf", [P, NT, 2])
        posi = sb("posi", [P, NT, 2], I32)
        gate = sb("gate", [P, 2, NT])
        gate_e = sb("gate_e", [P, NT])
        gate_d = sb("gate_d", [P, NT])
        run = sb("run", [P, NE])

        with ExitStack() as c1:
            ln_in = [sbc(c1, f"ln_in{i}", [P, LN_ROWS, D]) for i in range(3)]
            ln_out = [sbc(c1, f"ln_out{i}", [P, LN_ROWS, D]) for i in range(3)]
            ln_bst = [sbc(c1, f"ln_bst{i}", [P, LN_ROWS, 6]) for i in range(2)]
            ln_mv = [sbc(c1, f"ln_mv{i}", [P, LN_ROWS, 2]) for i in range(2)]
            ln_std = [sbc(c1, f"ln_std{i}", [P, LN_ROWS]) for i in range(2)]
            ln_r = [sbc(c1, f"ln_r{i}", [P, LN_ROWS]) for i in range(2)]
            ln_b = [sbc(c1, f"ln_b{i}", [P, LN_ROWS]) for i in range(2)]
            ed_i = sbc(c1, "ed_i", [EP, 2, EB, P], I32)
            ed_f = sbc(c1, "ed_f", [EP, 2, EB, P])
            t_max = sbc(c1, "t_max", [EP, EB])
            t_min = sbc(c1, "t_min", [EP, EB])
            tid_i = sbc(c1, "tid_i", [EP, EB], I32)
            tid = sbc(c1, "tid", [EP, EB])
            thr_i = sbc(c1, "thr_i", [P, NT], I32)
            thr = sbc(c1, "thr", [P, NT])
            thr_hi = sbc(c1, "thr_hi", [P, NT])
            iota_i = sbc(c1, "iota_i", [P, P], I32)
            cmp_m = sbc(c1, "cmp_m", [EP, NT, EB])
            cmp_v = sbc(c1, "cmp_v", [EP, NT, EB])
            first_c = sbc(c1, "first_c", [EP, NT])
            end_c = sbc(c1, "end_c", [EP, NT])
            first_g = sbc(c1, "first_g", [NT, 1])
            end_g = sbc(c1, "end_g", [NT, 1])
            span_g = sbc(c1, "span_g", [NT, 1])
            gi_i = sbc(c1, "gi_i", [NT, MAXG], I32)
            gi = sbc(c1, "gi", [NT, MAXG])
            cmp_g = sbc(c1, "cmp_g", [NT, MAXG])
            n_g = sbc(c1, "n_g", [NT, 1])
            n_g2 = sbc(c1, "n_g2", [NT, 1])

        with ExitStack() as c2:
            rows = sbc(c2, "rows", [P, G, D])
            r_hi = sbc(c2, "r_hi", [P, G, D], F32R)
            r_lo = sbc(c2, "r_lo", [P, G, D], F32R)
            sel = sbc(c2, "sel", [P, G, P], F32R)
            idx = sbc(c2, "idx", [P, G], I32)
            agg_s = sbc(c2, "agg_s", [P, D])
            self_t = sbc(c2, "self_t", [P, D])
            aT = sbc(c2, "aT", [P, 2, KC, P], F32R)
            sT = sbc(c2, "sT", [P, 2, KC, P], F32R)
            h_t = sbc(c2, "h_t", [P, D])
            x_t = sbc(c2, "x_t", [P, D])
            x2_t = sbc(c2, "x2_t", [P, D])
            xn2_t = sbc(c2, "xn2_t", [P, D])
            xT = sbc(c2, "xT", [P, KC, P])
            deg_m = sbc(c2, "deg_m", [P, 1])
            bst = sbc(c2, "bst", [P, 6])
            mv = sbc(c2, "mv", [P, 2])
            std = sbc(c2, "std", [P, 1])
            rstd = sbc(c2, "rstd", [P, 1])
            nmr = sbc(c2, "nmr", [P, 1])
            lg = sbc(c2, "lg", [P, NE])
            mx8 = sbc(c2, "mx8", [P, NE])
            ix8 = sbc(c2, "ix8", [P, NE], U32)
            e01 = sbc(c2, "e01", [P, 2])
            mask = sbc(c2, "mask", [P, 2, NE])
            mask_s = sbc(c2, "mask_s", [P, NE])
            place = sbc(c2, "place", [P, NE])
            prod = sbc(c2, "prod", [P, 2, NE])
            pos_now = sbc(c2, "pos_now", [P, 2], I32)
            nrow = sbc(c2, "nrow", [P, NE])
            ti_i = sbc(c2, "ti_i", [P, NE, NT], I32)
            ti = sbc(c2, "ti", [P, NE, NT])
            ti_c = sbc(c2, "ti_c", [P, NE, NT])
            ntile = sbc(c2, "ntile", [P, NE])
            ntile2 = sbc(c2, "ntile2", [P, NE])
            shift = sbc(c2, "shift", [P, NE])
            pos_c = sbc(c2, "pos_c", [P, 2 * NT, NE - 1])
            pos_s = sbc(c2, "pos_s", [P, 2 * NT])
            tcum = sbc(c2, "tcum", [1, NE + 1])
            ebase_i = sbc(c2, "ebase_i", [P, NE], I32)
            ebase = sbc(c2, "ebase", [P, NE])
            zrow = sbc(c2, "zrow", [P, D])

        with ExitStack() as c3:
            m_x = sbc(c3, "m_x", [P, D])
            m_xT = sbc(c3, "m_xT", [P, 2, KC, P], F32R)
            m_h = sbc(c3, "m_h", [P, D])
            m_hT = sbc(c3, "m_hT", [P, 2, KC, P], F32R)
            m_n = sbc(c3, "m_n", [P, D])
            m_ng = sbc(c3, "m_ng", [P, D])
            m_y = sbc(c3, "m_y", [P, D])
            m_bst = sbc(c3, "m_bst", [P, 6])
            m_mv = sbc(c3, "m_mv", [P, 2])
            m_std = sbc(c3, "m_std", [P, 1])
            m_r = sbc(c3, "m_r", [P, 1])
            m_b = sbc(c3, "m_b", [P, 1])
            gam = [sbc(c3, f"gam{i}", [P, D]) for i in range(2)]
            bet = [sbc(c3, f"bet{i}", [P, D]) for i in range(2)]

        with ExitStack() as c4:
            c_y = sbc(c4, "c_y", [P, CB, 2, D])
            c_x = sbc(c4, "c_x", [P, CB, D])
            c_t = sbc(c4, "c_t", [P, CB, D])
            c_idx = sbc(c4, "c_idx", [P, CB, 2], I32)

        ps = ctx.enter_context(nc.psum_tensor("ps", [P, 8, 512], F32))
        agg_p, deg_p, aT_p, sT_p, dense_p, xT_p, lg_p, pre_p = (ps[:, i, :] for i in range(8))
        mxT_p, mh_p, mhT_p, my_p = (ps[:, i, :] for i in range(4))

        s_const = sem("s_const")
        s_constv = sem("s_constv")
        s_ln_in = [sem(f"s_ln_in{i}") for i in range(3)]
        s_ln_st = sem("s_ln_st")
        s_ln_mv = sem("s_ln_mv")
        s_ln_std = sem("s_ln_std")
        s_ln_r = sem("s_ln_r")
        s_ln_b = sem("s_ln_b")
        s_ln_out = sem("s_ln_out")
        s_xn = sem("s_xn")
        s_pad = sem("s_pad")
        s_edges = sem("s_edges")
        s_tab = sem("s_tab")
        s_tabT = sem("s_tabT")
        s_raw = sem("s_raw")
        s_brow = sem("s_brow")
        s_split = sem("s_split")
        s_wset = sem("s_wset")
        s_wg = sem("s_wg")
        s_whi = sem("s_whi")
        s_wlo = sem("s_wlo")
        s_passed = sem("s_passed")
        s_bset = sem("s_bset")
        s_const2 = sem("s_const2")
        s_cv2 = sem("s_cv2")
        s_gate = sem("s_gate")
        s_place = sem("s_place")
        s_yzero = sem("s_yzero")

        names = ("iota idx hi lo seg node rdeg0 rdeg evac aggT aggHi aggLo self selfT selfHi "
                 "selfLo dense res store xt bst mv std rstd nmr xn2 xT xTc logit lg mx ix e01 m0 m1 msum pref "
                 "place run prod pos posi scat").split()
        L = [{n: sem(f"s{l + 1}_{n}") for n in names if l == 1 or n not in
              ("xt bst mv std rstd nmr xn2 xT xTc logit lg mx ix e01 m0 m1 msum pref place run prod pos "
               "posi scat").split()} for l in range(2)]
        L_rows = [[sem(f"s{l + 1}_rows{k}") for k in range(G)] for l in range(2)]

        s_cnt = sem("s_cnt")
        s_gexp = sem("s_gexp")
        s_zero = sem("s_zero")
        M = {n: sem(f"m_{n}") for n in ("x xT xHi xLo h relu hT hHi hLo y bst mv std r b norm gam out "
                                        "store aff").split()}
        s_cidx = sem("s_cidx")
        s_cy = [sem(f"s_cy{j}") for j in range(CB)]
        s_cx = [sem(f"s_cx{j}") for j in range(CB)]
        s_ct = sem("s_ct")
        s_cacc = sem("s_cacc")
        s_cout = sem("s_cout")
        s_out = sem("s_out")

        CONST, CONSTV = 17, 11
        TAB_DONE = 23
        CNT_DONE = 17

        block = ctx.enter_context(nc.Block())

        def value(eng, cell, top):
            return eng.value_load(cell, min_val=0, max_val=top)

        def weights_hi(act, n, par):
            act.wait_ge(s_raw, n * 32 + 32)
            for m in range(2):
                act.activation(wts[par][:, m, 0], w_raw[:, m], ACT.Copy).then_inc(s_whi, 1)

        def weights_lo(dve, n, par):
            for m in range(2):
                dve.wait_ge(s_whi, n * 2 + m + 1)
                dve.tensor_tensor(wts[par][:, m, 1], w_raw[:, m], wts[par][:, m, 0].bitcast(F32),
                                  ALU.subtract).then_inc(s_wlo, 1)

        def alone(eng, semaphore, v):
            eng.wait_ge(semaphore, v)
            eng.sem_inc(s_passed, 1)

        def within(v, top):
            return v if isinstance(v, int) else v.with_bounds(min_val=0, max_val=top)

        def layer(eng, group, hooks, opening=None, tail=None, lag=1):
            def tile(g, prev):
                at = (lambda t, i: t[0:1, i:i + 1]) if isinstance(g, int) else (lambda t, i: t[0:1, bass.ds(i, 1)])
                c0 = value(eng, at(tab_group, g), NT * MAXG)
                c1 = value(eng, at(tab_group, g + 1), NT * MAXG)
                t0 = value(eng, at(tab_first, g), ET)
                steps = {k: [(f, prev) for f in fs] for k, fs in hooks.items()} if prev is not None else {}
                if opening:
                    opening(g, c0)
                group(g, c0, t0, {k: f for k, f in steps.items() if k < G})
                group(g, c0 + 1, t0 + G, {k - G: f for k, f in steps.items() if k >= G})
                with eng.If_lt(eng.to_reg(c0 + 2), eng.to_reg(c1)):
                    with eng.Fori(c0 + 2, c1) as c:
                        group(g, c, within(t0 + (c - c0) * G, ETP - G), {})
                if tail:
                    tail(g)

            for g in range(lag):
                tile(g, None)
            with eng.Fori(lag, NT) as g:
                tile(g, g - lag)
            for n in range(NT - lag, NT):
                for k in sorted(hooks):
                    for f in hooks[k]:
                        f(n)

        def run_hooks(hooks, k):
            for f, n in hooks.get(k, []):
                f(n)

        def rows_at(t, n):
            return t[start_of(n):start_of(n) + P, :] if isinstance(n, int) else t[bass.ds(n * P, P), :]

        @block.sync
        def _(sp):
            def load_chunk(c):
                r0 = min(c * P * LN_ROWS, N - P * LN_ROWS)
                sp.dma_start(ln_in[c % 3][:], x[r0:r0 + P * LN_ROWS, :].rearrange("(p j) d -> p j d", p=P)) \
                    .then_inc(s_ln_in[c % 3], 16)

            def store_chunk(c):
                r0 = min(c * P * LN_ROWS, N - P * LN_ROWS)
                sp.wait_ge(s_ln_out, c + 1)
                if c == LN_CH - 1:
                    sp.wait_ge(s_xn, 16 * c)
                sp.dma_start(xn_d[r0:r0 + P * LN_ROWS, :].rearrange("(p j) d -> p j d", p=P),
                             ln_out[c % 3][:]).then_inc(s_xn, 16)

            def load_set(n, wa, wb, ba, bb):
                if not (isinstance(n, int) and n == 0):
                    sp.wait_ge(s_wset, n)
                sp.dma_start(w_raw[:, 0], wa.rearrange("(k p) n -> p k n", p=P)).then_inc(s_raw, 16)
                sp.dma_start(w_raw[:, 1], wb.rearrange("(k p) n -> p k n", p=P)).then_inc(s_raw, 16)
                for j, b in enumerate((ba, bb)):
                    for q in range(2):
                        sp.dma_start(bias_raw[q:q + 1, j, :], b).then_inc(s_brow, 16)

            load_chunk(0)
            sp.wait_ge(s_pad, 2)
            full = (EB - 1) * EP * P
            tail_rows = (E - full) // P
            for j, lst in enumerate((src, dst)):
                sp.dma_start(ed_i[:, j, 0:EB - 1, :],
                             lst[0:full].rearrange("(b p e) -> p b e", p=EP, e=P)).then_inc(s_edges, 16)
                sp.dma_start(ed_i[0:tail_rows, j, EB - 1, :],
                             lst[full:full + tail_rows * P].rearrange("(p e) -> p e", e=P)).then_inc(s_edges, 16)
                sp.dma_start(ed_i[tail_rows:tail_rows + 1, j, EB - 1, 0:E - full - tail_rows * P],
                             lst[full + tail_rows * P:E].rearrange("(a e) -> a e", a=1)).then_inc(s_edges, 16)
            load_chunk(1)
            load_chunk(2)
            sp.dma_start(wg_s[:], Wg.rearrange("(k p) e -> p k e", p=P)).then_inc(s_wg, 16)
            brow = lambda b: b.rearrange("(a n) -> a n", a=1)
            for c in range(LN_CH):
                store_chunk(c)
                if c + 3 < LN_CH:
                    load_chunk(c + 3)
                if c == 2:
                    load_set(0, w_neigh1, w_self1, brow(b1), brow(b1))
                if c == 7:
                    load_set(1, w_neigh2, w_self2, brow(b2), brow(b2))

            for l, own, res_d, res in ((0, xn_d, h1_d, h_t), (1, h1_d, x2_d, x2_t)):
                S = L[l]
                if l == 0:
                    sp.wait_ge(s_xn, 16 * LN_CH)
                else:
                    load_set(2, W1[0], W2[0], eb1[0:1], eb2[0:1])
                    sp.wait_ge(L[0]["store"], 16 * NT)

                def load_tile(n):
                    if not (isinstance(n, int) and n == 0):
                        alone(sp, S["selfT"], n)
                        sp.wait_ge(S["self"], n * 16)
                    elif l == 1:
                        sp.wait_ge(L[0]["selfT"], NT)
                    sp.dma_start(self_t[:], rows_at(own, n)).then_inc(S["self"], 16)
                    if l == 1:
                        if not (isinstance(n, int) and n == 0):
                            sp.wait_ge(S["res"], n)
                            sp.wait_ge(S["xt"], n * 16)
                        sp.dma_start(x_t[:], rows_at(x, n)).then_inc(S["xt"], 16)

                def store_tile(n):
                    sp.wait_ge(S["res"], n + 1)
                    if isinstance(n, int):
                        sp.wait_ge(S["store"], 16 * n)
                    sp.dma_start(rows_at(res_d, n), res[:]).then_inc(S["store"], 16)

                load_tile(0)
                with sp.Fori(0, NT - 2) as n:
                    load_tile(n + 1)
                    store_tile(n)
                load_tile(NT - 1)
                sp.wait_ge(S["res"], NT - 1)
                sp.dma_start(res_d[(NT - 2) * P:(NT - 1) * P, :], res[:]).then_inc(S["store"], 16)
                store_tile(NT - 1)

            def expert_set(n, e, par):
                at = (lambda t: t[e:e + 1]) if isinstance(e, int) else (lambda t: t[bass.ds(e, 1)])
                if not (isinstance(n, int) and n == 2):
                    load_set(n, at(W1).rearrange("a k n -> (a k) n"), at(W2).rearrange("a k n -> (a k) n"),
                             at(eb1), at(eb2))
                for t, d in ((gam[par], gamma), (bet[par], beta)):
                    sp.dma_start(t[:], at(d).to_broadcast([P, D])).then_inc(M["aff"], 16)

            sp.wait_ge(L[1]["scat"], 32 * NT)
            sp.wait_ge(s_cnt, CNT_DONE)
            for e in range(NE):
                r = value(sp, tab_rows[0:1, e:e + 1], (NE - 1) * REGION + NT * P)
                for j in range(MIN_TILES):
                    sp.dma_start(disp_d[bass.ds(r + j * P, P), :], zrow[:]).then_inc(s_zero, 16)
            expert_set(2, 0, 0)
            sp.wait_ge(s_zero, 16 * MIN_TILES * NE)
            sp.wait_ge(s_place, 5)

            def load_x(q, row):
                if not (isinstance(q, int) and q == 0):
                    sp.wait_ge(M["xT"], q)
                sp.dma_start(m_x[:], disp_d[bass.ds(row, P), :]).then_inc(M["x"], 16)

            with sp.Fori(0, NE // 2) as e2:
                for par in range(2):
                    e = e2 * 2 + par
                    q0 = value(sp, tab_tiles[0:1, bass.ds(e, 1)], YT - 1)
                    q1 = value(sp, tab_tiles[0:1, bass.ds(e + 1, 1)], YT - 1)
                    load_x(q0, e * REGION)
                    load_x(q0 + 1, e * REGION + P)
                    nxt = within(e + 1 - ((e + 1) // NE), NE - 1)
                    alone(sp, M["out"], q0)
                    expert_set(e + 3, nxt, 1 - par)
                    with sp.Fori(q0 + 2, q1) as q:
                        load_x(q, within(e * REGION + (q - q0) * P, NE * REGION - P))
            qT = value(sp, tab_tiles[0:1, NE:NE + 1], YT - 1)
            load_x(qT, 0)
            alone(sp, M["store"], qT * 16)
            alone(sp, M["xLo"], qT + 1)
            sp.wait_ge(M["aff"], 32 * (NE + 1))

            def combine_loads(a):
                for j in range(CB):
                    n = a * CB + j
                    if not (isinstance(a, int) and a == 0):
                        alone(sp, s_ct, n - CB + 1)
                        alone(sp, s_cx[j], 16 * a)
                    sp.dma_start(c_x[:, j, :], rows_at(x2_d, n)).then_inc(s_cx[j], 16)

            def combine_stores(a):
                for j in range(CB):
                    n = a * CB + j
                    sp.wait_ge(s_cacc, n + 1)
                    if isinstance(n, int) and n == NT - 1:
                        sp.wait_ge(s_out, 16 * n)
                    sp.dma_start(rows_at(out, n), c_t[:, j, :]).then_inc(s_out, 16)

            combine_loads(0)
            with sp.Fori(0, NT // CB - 2) as a:
                combine_stores(a)
                combine_loads(a + 1)
            combine_stores(NT // CB - 2)
            combine_loads(NT // CB - 1)
            combine_stores(NT // CB - 1)
            sp.wait_ge(s_out, 16 * NT)

        @block.gpsimd
        def _(pool):
            k = [0]

            def did(ins, wait=False):
                k[0] += 1
                ins.then_inc(s_const, 1)
                if wait:
                    pool.wait_ge(s_const, k[0])

            pool.memset(ed_i[:, 1, EB - 1, :], int(FAR)).then_inc(s_pad, 1)
            pool.memset(ed_i[:, 0, EB - 1, :], 0).then_inc(s_pad, 1)
            did(pool.iota(iota_i[:], pattern=[[1, P]], base=0, channel_multiplier=0))
            did(pool.iota(thr_i[:], pattern=[[P, NT]], base=0, channel_multiplier=0))
            did(pool.iota(tid_i[:], pattern=[[EP, EB]], base=0, channel_multiplier=1))
            did(pool.iota(gi_i[:], pattern=[[G, MAXG]], base=0, channel_multiplier=0))
            did(pool.iota(rseli[:], pattern=[[1, 2]], base=0, channel_multiplier=1))
            did(pool.memset(eps_col[:], EPS))
            did(pool.memset(zero2[:].bitcast(F32), 0.0))
            did(pool.memset(one2[:].bitcast(F32), 1.0))
            did(pool.memset(ones_col[:].bitcast(F32), 1.0))
            did(pool.memset(onesq[:], 1.0))
            did(pool.memset(ident[:], 0.0), wait=True)
            did(pool.affine_select(out=ident[:], in_=ident[:], compare_op=ALU.not_equal, fill=1.0, base=0,
                                   pattern=[[-1, P]], channel_multiplier=1))
            did(pool.memset(upper[:], 1.0), wait=True)
            did(pool.affine_select(out=upper[:], in_=upper[:], compare_op=ALU.is_ge, fill=0.0, base=-1,
                                   pattern=[[1, P]], channel_multiplier=-1))
            did(pool.memset(srcT[:, ET:ETP], 0))
            did(pool.memset(dstT[:, ET:ETP], FAR))
            did(pool.memset(zero_row[:].bitcast(F32), 0.0))
            assert k[0] == CONST

            def split_set(n, par):
                pool.wait_ge(s_raw, n * 32 + 32)
                alone(pool, s_brow, n * 64 + 64)
                base = n * 10
                for m in range(2):
                    if isinstance(n, int) and n < 3:
                        pool.wait_ge(s_wlo, n * 2 + m + 1)
                        pool.sem_inc(s_split, 2)
                    else:
                        pool.tensor_copy(wts[par][:, m, 0], w_raw[:, m]).then_inc(s_split, 1)
                        alone(pool, s_split, base + 5 * m + 1)
                        pool.tensor_tensor(wts[par][:, m, 1], w_raw[:, m], wts[par][:, m, 0].bitcast(F32),
                                           ALU.subtract).then_inc(s_split, 1)
                    pool.tensor_copy(bias[par][:, m, :], bias_raw[:, m, :]).then_inc(s_split, 1)
                    alone(pool, s_split, base + 5 * m + 3)
                    pool.tensor_scalar(bias_t[:], bias[par][:, m, :].bitcast(F32), rsel[:, 1:2], None,
                                       ALU.mult).then_inc(s_split, 1)
                    pool.tensor_scalar(bias_u[:], bias_raw[:, m, :], rsel[:, 0:1], None,
                                       ALU.mult).then_inc(s_split, 1)
                    alone(pool, s_split, base + 5 * m + 5)
                    pool.tensor_tensor(bias[par][:, m, :], bias_t[:], bias_u[:], ALU.add) \
                        .then_inc(s_wset if m else s_bset, 1)
                    if not m:
                        alone(pool, s_bset, n + 1)

            pool.wait_ge(s_constv, CONSTV)
            split_set(0, 0)
            split_set(1, 1)

            pool.wait_ge(s_tab, TAB_DONE)
            for l, rows_d in ((0, xn_d), (1, h1_d)):
                S = L[l]
                if l == 0:
                    pool.wait_ge(s_xn, 16 * LN_CH)
                else:
                    pool.wait_ge(L[0]["store"], 16 * NT)
                    pool.iota(ebase_i[:], pattern=[[REGION, NE]], base=0, channel_multiplier=0).then_inc(s_const2, 1)
                    pool.iota(ti_i[:], pattern=[[0, NE], [P, NT]], base=0, channel_multiplier=0).then_inc(s_const2, 1)

                def gathers(g, c, t, hooks):
                    for k in range(G):
                        run_hooks(hooks, k)
                        if k in IDX_AT:
                            w = IDX_AT[k]
                            alone(pool, S["hi"], c * G + (k + w))
                            alone(pool, S["lo"], c * G + (k + w))
                            pool.tensor_copy(idx[:, k:k + w], srcT[:, bass.ds(t + k, w)]).then_inc(S["idx"], 1)
                            alone(pool, S["idx"], c * len(IDX_AT) + (1 + (k > 0)))
                        pool.indirect_dma_start(
                            rows[:, k, :], None, rows_d,
                            bass.IndirectOffsetOnAxis(ap=idx[:, k:k + 1], axis=0)).then_inc(L_rows[l][k], 16)
                    run_hooks(hooks, G)

                def scatter(n):
                    alone(pool, S["posi"], n + 1)
                    for j in range(2):
                        pool.indirect_dma_start(
                            disp_d, bass.IndirectOffsetOnAxis(ap=pos_now[:, j:j + 1], axis=0),
                            xn2_t[:], None) \
                            .then_inc(S["scat"], 16)

                layer(pool, gathers, {3: [scatter]} if l == 1 else {}, lag=2)

            pool.wait_ge(L[1]["dense"], NT)
            pool.wait_ge(s_cnt, CNT_DONE)
            split_set(2, 0)
            split_set(3, 1)
            qT = value(pool, tab_tiles[0:1, NE:NE + 1], YT - 1)
            with pool.Fori(1, YT - qT + 1) as j:
                pool.dma_start(y_d[bass.ds(within((qT + j - 1) * P, (YT - 1) * P), P), :], zrow[:]) \
                    .then_inc(s_yzero, 16)
                alone(pool, s_yzero, j * 16)
            with pool.Fori(1, NE // 2) as e2:
                for par in range(2):
                    e = e2 * 2 + par
                    q = value(pool, tab_tiles[0:1, bass.ds(within(e - 1, NE), 1)], YT - 1)
                    alone(pool, M["y"], q)
                    split_set(e + 2, par)
            split_last = NE + 2
            pool.wait_ge(s_raw, split_last * 32 + 32)
            pool.wait_ge(s_brow, split_last * 64 + 64)

            qT = value(pool, tab_tiles[0:1, NE:NE + 1], YT - 1)
            alone(pool, M["store"], qT * 16)
            alone(pool, M["xLo"], qT + 1)
            pool.wait_ge(s_place, 5)

            def combine_gathers(a):
                for j in range(CB):
                    n = a * CB + j
                    if not (isinstance(a, int) and a == 0):
                        alone(pool, s_cacc, n - CB + 1)
                        alone(pool, s_cy[j], 32 * a)
                    pool.tensor_copy(c_idx[:, j, :], posi[:, n, :] if isinstance(n, int) else
                                     posi[:, bass.ds(n, 1), :].rearrange("p a j -> p (a j)")).then_inc(s_cidx, 1)
                    alone(pool, s_cidx, n + 1)
                    for i in range(2):
                        pool.indirect_dma_start(
                            c_y[:, j, i, :], None, y_d,
                            bass.IndirectOffsetOnAxis(ap=c_idx[:, j, i:i + 1], axis=0)).then_inc(s_cy[j], 16)

            combine_gathers(0)
            with pool.Fori(1, NT // CB) as a:
                combine_gathers(a)

        @block.scalar
        def _(act):
            act.wait_ge(s_const, CONST)

            def ln_sqrt(c):
                act.wait_ge(s_ln_mv, c + 1)
                act.activation(ln_std[c % 2][:], ln_mv[c % 2][:, :, 1], ACT.Sqrt, bias=eps_col[:, 0:1],
                               scale=1.0).then_inc(s_ln_std, 1)

            def ln_norm(c):
                act.wait_ge(s_ln_b, c + 1)
                if c >= 3:
                    act.wait_ge(s_xn, 16 * (c - 2))
                for j in range(LN_ROWS):
                    i = act.activation(ln_out[c % 3][:, j, :], ln_in[c % 3][:, j, :], ACT.Identity,
                                       bias=ln_b[c % 2][:, j:j + 1], scale=ln_r[c % 2][:, j:j + 1])
                i.then_inc(s_ln_out, 1)

            ln_sqrt(0)
            for c in range(LN_CH):
                if c + 1 < LN_CH:
                    ln_sqrt(c + 1)
                ln_norm(c)
                if c in WSPLIT_AT:
                    weights_hi(act, WSPLIT_AT.index(c), WSPLIT_AT.index(c))

            act.wait_ge(s_tab, TAB_DONE)
            for l in range(2):
                S = L[l]
                act.wait_ge(s_ln_out, LN_CH)
                if l == 1:
                    weights_hi(act, 2, 0)
                act.sem_inc(S["hi"], G)

                def halves(g, c, t, hooks):
                    for k in range(G):
                        run_hooks(hooks, k)
                        act.wait_ge(L_rows[l][k], c * 16 + 16)
                        act.wait_ge(S["seg"], c * G + (k + 1))
                        act.activation(r_hi[:, k, :], rows[:, k, :], ACT.Copy).then_inc(S["hi"], 1)
                    run_hooks(hooks, G)

                def evac(g):
                    act.wait_ge(S["node"], g + 1)
                    if l == 0:
                        act.wait_ge(S["rdeg"], g + 1)
                    act.wait_ge(S["aggT"], g)
                    act.activation(agg_s[:], agg_p, ACT.Identity,
                                   scale=rdeg[:, g:g + 1] if isinstance(g, int) else
                                   rdeg[:, bass.ds(g, 1)]).then_inc(S["evac"], 1)

                def self_hi(n):
                    act.wait_ge(S["selfT"], n + 1)
                    act.wait_ge(S["dense"], n)
                    act.activation(sT[:, 0].rearrange("p k n -> p (k n)"), sT_p, ACT.Copy).then_inc(S["selfHi"], 1)

                def agg_hi(n):
                    act.wait_ge(S["aggT"], n + 1)
                    act.activation(aT[:, 0].rearrange("p k n -> p (k n)"), aT_p, ACT.Copy).then_inc(S["aggHi"], 1)

                def relu(n):
                    act.wait_ge(S["dense"], n + 1)
                    act.wait_ge(S["store"], n * 16)
                    act.activation(h_t[:], dense_p, ACT.Relu).then_inc(S["res"], 1)

                def sqrt2(n):
                    act.wait_ge(S["mv"], n + 1)
                    act.activation(std[:], mv[:, 1:2], ACT.Sqrt, bias=eps_col[:, 0:1],
                                   scale=1.0).then_inc(S["std"], 1)

                def norm2(n):
                    act.wait_ge(S["nmr"], n + 1)
                    act.wait_ge(S["scat"], n * 32)
                    act.wait_ge(S["xT"], n)
                    act.activation(xn2_t[:], x2_t[:], ACT.Identity, bias=nmr[:, 0:1],
                                   scale=rstd[:, 0:1]).then_inc(S["xn2"], 1)

                def xT_copy(n):
                    act.wait_ge(S["xT"], n + 1)
                    act.wait_ge(S["logit"], n)
                    act.activation(xT[:].rearrange("p k n -> p (k n)"), xT_p, ACT.Copy).then_inc(S["xTc"], 1)

                hooks = {1: [self_hi], 2: [agg_hi]}
                if l == 0:
                    hooks[11] = [relu]
                else:
                    hooks.update({11: [sqrt2], 12: [norm2], 14: [xT_copy]})
                layer(act, halves, hooks, tail=evac)

            def x_hi(q):
                act.wait_ge(M["xT"], q + 1)
                act.wait_ge(M["h"], q)
                act.activation(m_xT[:, 0].rearrange("p k n -> p (k n)"), mxT_p, ACT.Copy).then_inc(M["xHi"], 1)

            def h_hi(q):
                act.wait_ge(M["hT"], q + 1)
                act.wait_ge(M["y"], q)
                act.activation(m_hT[:, 0].rearrange("p k n -> p (k n)"), mhT_p, ACT.Copy).then_inc(M["hHi"], 1)

            def m_relu(q):
                act.wait_ge(M["h"], q + 1)
                act.wait_ge(M["hT"], q)
                act.activation(m_h[:], mh_p, ACT.Relu).then_inc(M["relu"], 1)

            def m_norm(q):
                act.wait_ge(M["mv"], q + 1)
                act.activation(m_std[:], m_mv[:, 1:2], ACT.Sqrt, bias=eps_col[:, 0:1],
                               scale=1.0).then_inc(M["std"], 1)
                act.wait_ge(M["b"], q + 1)
                act.wait_ge(M["gam"], q)
                act.activation(m_n[:], my_p, ACT.Identity, bias=m_b[:, 0:1],
                               scale=m_r[:, 0:1]).then_inc(M["norm"], 1)
                act.wait_ge(M["out"], q + 1)
                act.dma_start(y_d[bass.ds(q * P, P), :], m_y[:]).then_inc(M["store"], 16)

            act.wait_ge(s_cnt, CNT_DONE)
            x_hi(0)
            with act.Fori(0, NE // 2) as e2:
                for par in range(2):
                    e = e2 * 2 + par
                    q0 = value(act, tab_tiles[0:1, bass.ds(e, 1)], YT - 1)
                    q1 = value(act, tab_tiles[0:1, bass.ds(e + 1, 1)], YT - 1)
                    ql = value(act, tab_last[0:1, bass.ds(e, 1)], YT - 1)
                    m_relu(q0)
                    x_hi(q0 + 1)
                    with act.Fori(q0 + 1, q1) as q:
                        h_hi(q - 1)
                        m_relu(q)
                        x_hi(q + 1)
                        m_norm(q - 1)
                    h_hi(ql)
                    m_norm(ql)

            act.wait_ge(s_cnt, 1)
            act.activation(gate_e[:], gate_d[:], ACT.Exp).then_inc(s_gexp, 1)

        @block.vector
        def _(dve):
            kv = [0]

            def didv(ins, wait=False):
                kv[0] += 1
                ins.then_inc(s_constv, 1)
                if wait:
                    dve.wait_ge(s_constv, kv[0])

            dve.wait_ge(s_const, CONST)
            didv(dve.tensor_copy(iota[:], iota_i[:]))
            didv(dve.tensor_copy(tid[:], tid_i[:]))
            didv(dve.tensor_copy(gi[:], gi_i[:]))
            didv(dve.tensor_copy(rsel[:, 0:1], rseli[:, 0:1]))
            didv(dve.tensor_scalar(rsel[:, 1:2], rseli[:, 1:2], -2.0, 3.0, ALU.mult, ALU.add))
            didv(dve.tensor_copy(thr[:], thr_i[:]), wait=True)
            didv(dve.memset(thr[:, NT - 1:NT], float(LAST)), wait=True)
            didv(dve.tensor_scalar(thr_hi[:], thr[:], float(P), None, ALU.add))
            didv(dve.tensor_copy(start_col[:], thr[:]))
            didv(dve.memset(run[:], 0.0))
            didv(dve.memset(top2[:], 0.0), wait=True)
            assert kv[0] == CONSTV

            kt = [0]

            def t(ins, wait=True):
                kt[0] += 1
                ins.then_inc(s_tab, 1)
                if wait:
                    dve.wait_ge(s_tab, kt[0])

            def ln_stats(c):
                dve.wait_ge(s_ln_in[c % 3], 16 * (c // 3 + 1))
                for j in range(LN_ROWS):
                    i = dve.bn_stats(ln_bst[c % 2][:, j, :], ln_in[c % 3][:, j, :])
                i.then_inc(s_ln_st, 1)
                dve.wait_ge(s_ln_st, c + 1)
                if c >= 2:
                    dve.wait_ge(s_ln_out, c - 1)
                for j in range(LN_ROWS):
                    i = dve.bn_aggr(ln_mv[c % 2][:, j, :], ln_bst[c % 2][:, j, :])
                i.then_inc(s_ln_mv, 1)

            def ln_scale(c):
                dve.wait_ge(s_ln_std, c + 1)
                if c >= 2:
                    dve.wait_ge(s_ln_out, c - 1)
                dve.reciprocal(ln_r[c % 2][:], ln_std[c % 2][:]).then_inc(s_ln_r, 1)
                dve.wait_ge(s_ln_r, c + 1)
                dve.scalar_tensor_tensor(out=ln_b[c % 2][:], in0=ln_mv[c % 2][:, :, 0], scalar=-1.0,
                                         in1=ln_r[c % 2][:], op0=ALU.mult, op1=ALU.mult).then_inc(s_ln_b, 1)

            def tables():
                dve.wait_ge(s_edges, 96)
                t(dve.tensor_copy(ed_f[:, 0], ed_i[:, 0]), wait=False)
                t(dve.tensor_copy(ed_f[:, 1], ed_i[:, 1]))
                t(dve.tensor_reduce(out=t_max[:], in_=ed_f[:, 1], axis=AX.X, op=ALU.max), wait=False)
                t(dve.tensor_reduce(out=t_min[:], in_=ed_f[:, 1], axis=AX.X, op=ALU.min))
                over_g = lambda a: a.unsqueeze(1).to_broadcast([EP, NT, EB])
                over_b = lambda a: a[0:EP, :].unsqueeze(2).to_broadcast([EP, NT, EB])
                t(dve.tensor_tensor(cmp_m[:], over_g(t_max[:]), over_b(thr[:]), ALU.is_lt))
                t(dve.scalar_tensor_tensor(out=cmp_v[:], in0=cmp_m[:], scalar=float(ET), in1=over_g(tid[:]),
                                           op0=ALU.mult, op1=ALU.max))
                t(dve.tensor_reduce(out=first_c[:], in_=cmp_v[:], axis=AX.X, op=ALU.min))
                t(dve.tensor_tensor(cmp_m[:], over_g(t_min[:]), over_b(thr_hi[:]), ALU.is_lt))
                t(dve.tensor_tensor(cmp_v[:], cmp_m[:], over_g(tid[:]), ALU.mult))
                t(dve.tensor_tensor(cmp_v[:], cmp_v[:], cmp_m[:], ALU.add))
                t(dve.tensor_reduce(out=end_c[:], in_=cmp_v[:], axis=AX.X, op=ALU.max))

            def tables2():
                dve.wait_ge(s_tabT, 1)
                t(dve.tensor_reduce(out=first_g[:], in_=ps[0:NT, 4, 0:EP], axis=AX.X, op=ALU.min), wait=False)
                t(dve.tensor_reduce(out=end_g[:], in_=ps[0:NT, 4, P:P + EP], axis=AX.X, op=ALU.max))
                t(dve.tensor_tensor(span_g[:], end_g[:], first_g[:], ALU.subtract))
                t(dve.tensor_scalar(cmp_g[:], gi[:], span_g[:, 0:1], None, ALU.is_lt))
                t(dve.tensor_reduce(out=n_g[:], in_=cmp_g[:], axis=AX.X, op=ALU.add))
                t(dve.tensor_scalar(n_g2[:], n_g[:], 2.0, None, ALU.max))
                dve.wait_ge(s_tabT, 2)
                for j in range(2):
                    dstl = srcT if j == 0 else dstT
                    t(dve.tensor_copy(dstl[:, 0:4 * EP], ps[:, 2 * j, 0:4 * EP]), wait=False)
                    t(dve.tensor_copy(dstl[:, 4 * EP:ET], ps[:, 2 * j + 1, 0:3 * EP]), wait=False)
                dve.wait_ge(s_tabT, 3)
                t(dve.tensor_copy(tab_group[:], ps[0:1, 5, 0:NT + 1]), wait=False)
                t(dve.tensor_copy(tab_first[:], ps[0:1, 5, P:P + NT]))
                assert kt[0] == TAB_DONE

            ln_stats(0)
            for c in range(LN_CH):
                if c + 1 < LN_CH:
                    ln_stats(c + 1)
                ln_scale(c)
                if c == 1:
                    tables()
                if c == 4:
                    tables2()
                if c in WSPLIT_AT:
                    weights_lo(dve, WSPLIT_AT.index(c), WSPLIT_AT.index(c))

            dve.wait_ge(s_tab, TAB_DONE)
            for l in range(2):
                S = L[l]
                dve.wait_ge(s_ln_out, LN_CH)
                if l == 1:
                    dve.wait_ge(s_const2, 2)
                    dve.tensor_copy(ebase[:], ebase_i[:]).then_inc(s_cv2, 1)
                    dve.tensor_copy(ti[:], ti_i[:]).then_inc(s_cv2, 1)
                    dve.memset(zrow[:], 0.0).then_inc(s_cv2, 1)
                    dve.wait_ge(s_cv2, 3)
                    dve.tensor_copy(run[:], ebase[:]).then_inc(s_cv2, 1)
                    dve.wait_ge(s_cv2, 4)
                if l == 1:
                    weights_lo(dve, 2, 0)
                dve.sem_inc(S["lo"], G)

                def tile_iota(g, c0):
                    dve.wait_ge(S["lo"], c0 * G + G)
                    dve.tensor_scalar(iota_g[:], iota[:], start_col[:, bass.ds(g, 1)], None,
                                      ALU.add).then_inc(S["iota"], 1)
                    dve.wait_ge(S["iota"], g + 1)

                def select(g, c, t, hooks):
                    for k in range(G):
                        run_hooks(hooks, k)
                        if k % SELW == 0:
                            dve.wait_ge(S["seg"], c * G + (k + SELW))
                            dve.tensor_tensor(
                                sel[:, k:k + SELW, :], iota_g[:].unsqueeze(1).to_broadcast([P, SELW, P]),
                                dstT[:, bass.ds(t + k, SELW)].unsqueeze(2).to_broadcast([P, SELW, P]),
                                ALU.is_equal)
                        dve.wait_ge(L_rows[l][k], c * 16 + 16)
                        dve.wait_ge(S["hi"], c * G + (k + 1 + G))
                        dve.tensor_tensor(r_lo[:, k, :], rows[:, k, :], r_hi[:, k, :].bitcast(F32),
                                          ALU.subtract).then_inc(S["lo"], 1)
                    run_hooks(hooks, G)

                def degree(g):
                    dve.wait_ge(S["node"], g + 1)
                    dve.tensor_scalar(deg_m[:], deg_p[:, 0:1], 1.0, None, ALU.max).then_inc(S["rdeg0"], 1)
                    dve.wait_ge(S["rdeg0"], g + 1)
                    dve.reciprocal(rdeg[:, g:g + 1] if isinstance(g, int) else rdeg[:, bass.ds(g, 1)],
                                   deg_m[:]).then_inc(S["rdeg"], 1)

                def self_lo(n):
                    dve.wait_ge(S["selfHi"], n + 1)
                    dve.tensor_tensor(sT[:, 1].rearrange("p k n -> p (k n)"), sT_p,
                                      sT[:, 0].rearrange("p k n -> p (k n)").bitcast(F32),
                                      ALU.subtract).then_inc(S["selfLo"], 1)

                def agg_lo(n):
                    dve.wait_ge(S["aggHi"], n + 1)
                    dve.tensor_tensor(aT[:, 1].rearrange("p k n -> p (k n)"), aT_p,
                                      aT[:, 0].rearrange("p k n -> p (k n)").bitcast(F32),
                                      ALU.subtract).then_inc(S["aggLo"], 1)

                def residual(n):
                    dve.wait_ge(S["dense"], n + 1)
                    dve.wait_ge(S["xt"], n * 16 + 16)
                    dve.wait_ge(S["store"], n * 16)
                    dve.wait_ge(S["xn2"], n)
                    dve.scalar_tensor_tensor(out=x2_t[:], in0=dense_p, scalar=0.0, in1=x_t[:], op0=ALU.max,
                                             op1=ALU.add).then_inc(S["res"], 1)
                    dve.wait_ge(S["res"], n + 1)
                    dve.bn_stats(bst[:], x2_t[:]).then_inc(S["bst"], 1)
                    alone(dve, S["bst"], n + 1)
                    dve.bn_aggr(mv[:], bst[:]).then_inc(S["mv"], 1)

                def scales(n):
                    dve.wait_ge(S["std"], n + 1)
                    dve.reciprocal(rstd[:], std[:]).then_inc(S["rstd"], 1)
                    dve.wait_ge(S["rstd"], n + 1)
                    dve.scalar_tensor_tensor(out=nmr[:], in0=mv[:, 0:1], scalar=-1.0, in1=rstd[:],
                                             op0=ALU.mult, op1=ALU.mult).then_inc(S["nmr"], 1)

                def top_two(n):
                    one = (lambda a: a[:, :, n:n + 1]) if isinstance(n, int) else (lambda a: a[:, :, bass.ds(n, 1)])
                    dve.wait_ge(S["logit"], n + 1)
                    dve.tensor_copy(lg[:], lg_p[:, 0:NE]).then_inc(S["lg"], 1)
                    alone(dve, S["lg"], n + 1)
                    dve.max(mx8[:], lg[:]).then_inc(S["mx"], 1)
                    alone(dve, S["mx"], n + 1)
                    dve.max_index(ix8[:], mx8[:], lg[:]).then_inc(S["ix"], 1)
                    dve.tensor_copy(one(top2[:]), mx8[:, 0:2].unsqueeze(2))
                    dve.wait_ge(S["ix"], n + 1)
                    dve.tensor_copy(e01[:], ix8[:, 0:2]).then_inc(S["e01"], 1)
                    dve.wait_ge(S["e01"], n + 1)
                    for j in range(2):
                        dve.tensor_scalar(mask[:, j, :], iota[:, 0:NE], e01[:, j:j + 1], None,
                                          ALU.is_equal).then_inc(S[f"m{j}"], 1)
                    dve.wait_ge(S["m1"], n + 1)
                    dve.tensor_tensor(mask_s[:], mask[:, 0, :], mask[:, 1, :], ALU.add).then_inc(S["msum"], 1)

                def places(n):
                    dve.wait_ge(S["pref"], n + 1)
                    dve.tensor_tensor(place[:], run[:], pre_p[:, 0:NE], ALU.add).then_inc(S["place"], 1)
                    dve.wait_ge(S["place"], n + 1)
                    dve.tensor_tensor(run[:], run[:], pre_p[:, NE:2 * NE], ALU.add).then_inc(S["run"], 1)
                    dve.tensor_tensor(prod[:], mask[:], place[:].unsqueeze(1).to_broadcast([P, 2, NE]),
                                      ALU.mult).then_inc(S["prod"], 1)
                    dve.wait_ge(S["prod"], n + 1)
                    pf = posf[:, n, :] if isinstance(n, int) else posf[:, bass.ds(n, 1), :].rearrange("p a j -> p (a j)")
                    dve.tensor_reduce(out=pf, in_=prod[:], axis=AX.X, op=ALU.add).then_inc(S["pos"], 1)
                    dve.wait_ge(S["pos"], n + 1)
                    alone(dve, S["scat"], n * 32)
                    dve.tensor_copy(pos_now[:], pf).then_inc(S["posi"], 1)

                hooks = {1: [self_lo], 2: [agg_lo]}
                if l == 1:
                    hooks.update({10: [residual], 11: [scales], 15: [top_two], 17: [places]})
                layer(dve, select, hooks, opening=tile_iota, tail=degree if l == 0 else None)

            kc = [0]

            def cstep(ins):
                kc[0] += 1
                ins.then_inc(s_cnt, 1)
                dve.wait_ge(s_cnt, kc[0])

            dve.wait_ge(L[1]["posi"], NT)
            dve.wait_ge(L[1]["run"], NT)
            cstep(dve.tensor_tensor(gate_d[:], top2[:, 1, :], top2[:, 0, :], ALU.subtract))
            cstep(dve.tensor_copy(tab_rows[:], run[0:1, :]))
            cstep(dve.tensor_tensor(nrow[:], run[:], ebase[:], ALU.subtract))
            cstep(dve.tensor_tensor(ti_c[:], ti[:], nrow[:].unsqueeze(2).to_broadcast([P, NE, NT]), ALU.is_lt))
            cstep(dve.tensor_reduce(out=ntile[:], in_=ti_c[:], axis=AX.X, op=ALU.add))
            cstep(dve.tensor_scalar(ntile2[:], ntile[:], float(MIN_TILES), None, ALU.max))
            cstep(dve.memset(tcum[:], 0.0))
            for e in range(NE):
                cstep(dve.tensor_tensor(tcum[:, e + 1:e + 2], tcum[:, e:e + 1], ntile2[0:1, e:e + 1], ALU.add))
            cstep(dve.tensor_copy(tab_tiles[:], tcum[:]))
            cstep(dve.tensor_scalar(tab_last[:], tcum[:, 1:NE + 1], -1.0, None, ALU.add))
            assert kc[0] == CNT_DONE
            for i, ins in enumerate((
                    lambda: dve.tensor_scalar(shift[:], ntile2[:], float(P), float(REGION), ALU.mult, ALU.subtract),
                    lambda: dve.tensor_tensor(
                        pos_c[:], posf[:].rearrange("p n j -> p (n j)").unsqueeze(2).to_broadcast([P, 2 * NT, NE - 1]),
                        ebase[:, 1:NE].unsqueeze(1).to_broadcast([P, 2 * NT, NE - 1]), ALU.is_ge),
                    lambda: dve.tensor_tensor(
                        pos_c[:], pos_c[:], shift[:, 0:NE - 1].unsqueeze(1).to_broadcast([P, 2 * NT, NE - 1]),
                        ALU.mult),
                    lambda: dve.tensor_reduce(out=pos_s[:], in_=pos_c[:], axis=AX.X, op=ALU.add),
                    lambda: dve.tensor_tensor(posi[:].rearrange("p n j -> p (n j)"), pos_s[:],
                                              posf[:].rearrange("p n j -> p (n j)"), ALU.add))):
                ins().then_inc(s_place, 1)
                dve.wait_ge(s_place, i + 1)

            def x_lo(q):
                dve.wait_ge(M["xHi"], q + 1)
                dve.tensor_tensor(m_xT[:, 1].rearrange("p k n -> p (k n)"), mxT_p,
                                  m_xT[:, 0].rearrange("p k n -> p (k n)").bitcast(F32),
                                  ALU.subtract).then_inc(M["xLo"], 1)

            def h_lo(q):
                dve.wait_ge(M["hHi"], q + 1)
                dve.tensor_tensor(m_hT[:, 1].rearrange("p k n -> p (k n)"), mhT_p,
                                  m_hT[:, 0].rearrange("p k n -> p (k n)").bitcast(F32),
                                  ALU.subtract).then_inc(M["hLo"], 1)

            def y_norm(q, par):
                dve.wait_ge(M["y"], q + 1)
                dve.bn_stats(m_bst[:], my_p).then_inc(M["bst"], 1)
                alone(dve, M["bst"], q + 1)
                dve.bn_aggr(m_mv[:], m_bst[:]).then_inc(M["mv"], 1)
                dve.wait_ge(M["std"], q + 1)
                dve.reciprocal(m_r[:], m_std[:]).then_inc(M["r"], 1)
                dve.wait_ge(M["r"], q + 1)
                dve.scalar_tensor_tensor(out=m_b[:], in0=m_mv[:, 0:1], scalar=-1.0, in1=m_r[:],
                                         op0=ALU.mult, op1=ALU.mult).then_inc(M["b"], 1)
                dve.wait_ge(M["norm"], q + 1)
                dve.tensor_tensor(m_ng[:], m_n[:], gam[par][:], ALU.mult).then_inc(M["gam"], 1)
                dve.wait_ge(M["gam"], q + 1)
                dve.wait_ge(M["store"], q * 16)
                dve.tensor_tensor(m_y[:], m_ng[:], bet[par][:], ALU.add).then_inc(M["out"], 1)

            x_lo(0)
            with dve.Fori(0, NE // 2) as e2:
                for par in range(2):
                    e = e2 * 2 + par
                    q0 = value(dve, tab_tiles[0:1, bass.ds(e, 1)], YT - 1)
                    q1 = value(dve, tab_tiles[0:1, bass.ds(e + 1, 1)], YT - 1)
                    ql = value(dve, tab_last[0:1, bass.ds(e, 1)], YT - 1)
                    x_lo(q0 + 1)
                    dve.wait_ge(M["aff"], e * 32 + 32)
                    with dve.Fori(q0 + 1, q1) as q:
                        h_lo(q - 1)
                        x_lo(q + 1)
                        y_norm(q - 1, par)
                    h_lo(ql)
                    y_norm(ql, par)

            dve.wait_ge(s_gexp, 1)
            dve.tensor_scalar(gate_d[:], gate_e[:], 1.0, None, ALU.add).then_inc(s_gate, 1)
            dve.wait_ge(s_gate, 1)
            dve.reciprocal(gate[:, 0, :], gate_d[:]).then_inc(s_gate, 1)
            dve.wait_ge(s_gate, 2)
            dve.tensor_tensor(gate[:, 1, :], gate_e[:], gate[:, 0, :], ALU.mult).then_inc(s_gate, 1)
            dve.wait_ge(s_gate, 3)

            def combine(a):
                for j in range(CB):
                    n = a * CB + j
                    w = [gate[:, i, n:n + 1] if isinstance(n, int) else gate[:, i, bass.ds(n, 1)] for i in range(2)]
                    dve.wait_ge(s_cy[j], 32 * a + 32)
                    dve.wait_ge(s_cx[j], 16 * a + 16)
                    if not (isinstance(a, int) and a == 0):
                        dve.wait_ge(s_out, 16 * (n - CB + 1))
                    dve.scalar_tensor_tensor(out=c_t[:, j, :], in0=c_y[:, j, 0, :], scalar=w[0],
                                             in1=c_x[:, j, :], op0=ALU.mult, op1=ALU.add).then_inc(s_ct, 1)
                    dve.wait_ge(s_ct, n + 1)
                    dve.scalar_tensor_tensor(out=c_t[:, j, :], in0=c_y[:, j, 1, :], scalar=w[1],
                                             in1=c_t[:, j, :], op0=ALU.mult, op1=ALU.add).then_inc(s_cacc, 1)

            combine(0)
            with dve.Fori(1, NT // CB) as a:
                combine(a)

        @block.tensor
        def _(pe):
            pe.wait_ge(s_const, CONST)
            pe.wait_ge(s_tab, 11)
            pe.transpose(ps[0:NT, 4, 0:EP], first_c[:], ident[0:EP, 0:EP])
            pe.transpose(ps[0:NT, 4, P:P + EP], end_c[:], ident[0:EP, 0:EP]).then_inc(s_tabT, 1)
            for j in range(2):
                for b in range(EB):
                    i = pe.transpose(ps[:, 2 * j + b // 4, (b % 4) * EP:(b % 4 + 1) * EP], ed_f[:, j, b, :],
                                     ident[0:EP, 0:EP])
            i.then_inc(s_tabT, 1)
            pe.wait_ge(s_tab, 17)
            pe.matmul(ps[0:1, 5, 0:NT + 1], n_g2[:, 0:1], upper[0:NT, 0:NT + 1], start=True, stop=True)
            pe.matmul(ps[0:1, 5, P:P + NT], first_g[:, 0:1], ident[0:NT, 0:NT], start=True, stop=True) \
                .then_inc(s_tabT, 1)

            def product(out_ap, w, m, lhs, last=None, stop=False):
                for k in range(KC):
                    for a, b in ((0, 0), (1, 0), (0, 1)):
                        fin = k == KC - 1 and (a, b) == (0, 1)
                        i = pe.matmul(out_ap, lhs[:, a, k, :], w[:, m, b, k, :], start=False, stop=stop and fin)
                return i

            pe.wait_ge(s_tab, TAB_DONE)
            for l in range(2):
                S = L[l]
                pe.sem_inc(S["seg"], G)

                def opening(g, c0):
                    pe.wait_ge(S["evac"], g)
                    pe.matmul(agg_p, zero2[:], zero_row[:], start=True, stop=False)
                    if l == 0:
                        pe.matmul(deg_p[:, 0:2], zero2[:], zero_row[:, 0:2], start=True, stop=False)

                def sums(g, c, t, hooks):
                    for k in range(G):
                        run_hooks(hooks, k)
                        pe.wait_ge(S["lo"], c * G + (k + 1 + G))
                        if l == 0:
                            pe.matmul(deg_p[:, 0:2], sel[:, k, :], ones_col[:], start=False, stop=False)
                        pe.matmul(agg_p, sel[:, k, :], r_hi[:, k, :], start=False, stop=False)
                        pe.matmul(agg_p, sel[:, k, :], r_lo[:, k, :], start=False, stop=False).then_inc(S["seg"], 1)
                    run_hooks(hooks, G)

                def closing(g):
                    if l == 0:
                        pe.matmul(deg_p[:, 0:2], zero2[:], zero_row[:, 0:2], start=False, stop=True)
                    pe.matmul(agg_p, zero2[:], zero_row[:], start=False, stop=True).then_inc(S["node"], 1)

                def transposes(n):
                    pe.wait_ge(S["self"], n * 16 + 16)
                    pe.wait_ge(S["selfLo"], n)
                    for k in range(KC):
                        i = pe.transpose(sT_p[:, k * P:(k + 1) * P], self_t[:, k * P:(k + 1) * P], ident[:])
                    i.then_inc(S["selfT"], 1)
                    pe.wait_ge(S["evac"], n + 1)
                    pe.wait_ge(S["aggLo"], n)
                    for k in range(KC):
                        i = pe.transpose(aT_p[:, k * P:(k + 1) * P], agg_s[:, k * P:(k + 1) * P], ident[:])
                    i.then_inc(S["aggT"], 1)

                def dense_self(n):
                    pe.wait_ge(S["res"], n)
                    pe.wait_ge(s_wset, l + 1)
                    pe.matmul(dense_p, one2[:], bias[l][:, 0, :], start=True, stop=False)
                    pe.wait_ge(S["selfLo"], n + 1)
                    product(dense_p, wts[l], 1, sT)

                def dense_neigh(n):
                    pe.wait_ge(S["aggLo"], n + 1)
                    product(dense_p, wts[l], 0, aT, stop=True).then_inc(S["dense"], 1)

                def xT_t(n):
                    pe.wait_ge(S["xn2"], n + 1)
                    pe.wait_ge(S["xTc"], n)
                    for k in range(KC):
                        i = pe.transpose(xT_p[:, k * P:(k + 1) * P], xn2_t[:, k * P:(k + 1) * P], ident[:])
                    i.then_inc(S["xT"], 1)

                def logits(n):
                    pe.wait_ge(S["xTc"], n + 1)
                    pe.wait_ge(s_wg, 16)
                    pe.wait_ge(S["lg"], n)
                    for k in range(KC):
                        i = pe.matmul(lg_p[:, 0:NE], xT[:, k, :], wg_s[:, k, :], start=k == 0, stop=k == KC - 1)
                    i.then_inc(S["logit"], 1)

                def prefix(n):
                    pe.wait_ge(S["msum"], n + 1)
                    pe.wait_ge(S["run"], n)
                    pe.matmul(pre_p[:, 0:NE], upper[:], mask_s[:], start=True, stop=True)
                    pe.matmul(pre_p[:, NE:2 * NE], onesq[:], mask_s[:], start=True, stop=True).then_inc(S["pref"], 1)

                hooks = {0: [transposes], 2: [dense_self], 5: [dense_neigh]}
                if l == 1:
                    hooks.update({13: [xT_t], 15: [logits], 16: [prefix]})
                layer(pe, sums, hooks, opening=opening, tail=closing)

            def x_t_m(q):
                pe.wait_ge(M["x"], q * 16 + 16)
                pe.wait_ge(M["xLo"], q)
                for k in range(KC):
                    i = pe.transpose(mxT_p[:, k * P:(k + 1) * P], m_x[:, k * P:(k + 1) * P], ident[:])
                i.then_inc(M["xT"], 1)

            def mm1(q, par):
                pe.wait_ge(M["relu"], q)
                pe.matmul(mh_p, one2[:], bias[par][:, 0, :], start=True, stop=False)
                pe.wait_ge(M["xLo"], q + 1)
                product(mh_p, wts[par], 0, m_xT, stop=True).then_inc(M["h"], 1)

            def h_t_m(q):
                pe.wait_ge(M["relu"], q + 1)
                pe.wait_ge(M["hLo"], q)
                for k in range(KC):
                    i = pe.transpose(mhT_p[:, k * P:(k + 1) * P], m_h[:, k * P:(k + 1) * P], ident[:])
                i.then_inc(M["hT"], 1)

            def mm2(q, par):
                pe.wait_ge(M["norm"], q)
                pe.matmul(my_p, one2[:], bias[par][:, 1, :], start=True, stop=False)
                pe.wait_ge(M["hLo"], q + 1)
                product(my_p, wts[par], 1, m_hT, stop=True).then_inc(M["y"], 1)

            pe.wait_ge(s_cnt, CNT_DONE)
            x_t_m(0)
            with pe.Fori(0, NE // 2) as e2:
                for par in range(2):
                    e = e2 * 2 + par
                    q0 = value(pe, tab_tiles[0:1, bass.ds(e, 1)], YT - 1)
                    q1 = value(pe, tab_tiles[0:1, bass.ds(e + 1, 1)], YT - 1)
                    ql = value(pe, tab_last[0:1, bass.ds(e, 1)], YT - 1)
                    pe.wait_ge(s_wset, e + 3)
                    mm1(q0, par)
                    x_t_m(q0 + 1)
                    with pe.Fori(q0 + 1, q1) as q:
                        h_t_m(q - 1)
                        mm1(q, par)
                        x_t_m(q + 1)
                        mm2(q - 1, par)
                    h_t_m(ql)
                    mm2(ql, par)


_INS = ['x', 'src', 'dst', 'L0_gnn_W_self1', 'L0_gnn_W_neigh1', 'L0_gnn_b1', 'L0_gnn_W_self2', 'L0_gnn_W_neigh2',
        'L0_gnn_b2', 'L0_ffn_Wg', 'L0_ffn_W1', 'L0_ffn_b1', 'L0_ffn_W2', 'L0_ffn_b2', 'L0_ffn_gamma', 'L0_ffn_beta']


def kernel(**inputs):
    import concourse.bacc as bacc
    from concourse.bass_utils import run_bass_kernel_spmd

    nc = bacc.Bacc("TRN2", target_bir_lowering=False, num_devices=1)
    arrays, args = {}, []
    for name in _INS:
        a = np.ascontiguousarray(inputs[name])
        arrays[f"in_{name}"] = a
        args.append(nc.dram_tensor(f"in_{name}", a.shape, mybir.dt.from_np(a.dtype), kind="ExternalInput").ap())
    args.append(nc.dram_tensor("out_0", (N, D), F32, kind="ExternalOutput").ap())
    build(nc, *args)
    r = run_bass_kernel_spmd(nc, [arrays], core_ids=[0])
    return r.results[0]["out_0"]
```

```python
from contextlib import ExitStack

import numpy as np

import concourse.bass as bass
from concourse import mybir

F32 = mybir.dt.float32
F32R = mybir.dt.float32r
I32 = mybir.dt.int32
U32 = mybir.dt.uint32
ALU = mybir.AluOpType
ACT = mybir.ActivationFunctionType
AX = mybir.AxisListType

P = 128
N, D, E = 6250, 512, 100000
NE = 8
KC = D // P
NT = -(-N // P)
LAST = N - P
EPS = 1e-5

G = 9
EB, EP = 7, 112
ET = EB * EP
ETP = ET + 2 * G
FAR = 1.0e6
MAXG = -(-ET // G)
IDX_AT = {0: 5, 5: 4}
SELW = 3

LN_ROWS = 4
LN_CH = -(-N // (P * LN_ROWS))

WSPLIT_AT = (6, 10)
REGION = (NT + 1) * P
YT = 2 * NT + NE + 1
TQ = YT + 1
CB = 7


def start_of(g):
    return min(g * P, LAST)


def build(nc, x, src, dst, w_self1, w_neigh1, b1, w_self2, w_neigh2, b2, Wg, W1, eb1, W2, eb2, gamma, beta, out):
    xn_d = nc.dram_tensor("xn_scratch", (N, D), F32, kind="Internal").ap()
    h1_d = nc.dram_tensor("h1_scratch", (N, D), F32, kind="Internal").ap()
    x2_d = nc.dram_tensor("x2_scratch", (N, D), F32, kind="Internal").ap()
    disp_d = nc.dram_tensor("dispatch_scratch", (NE * REGION, D), F32, kind="Internal").ap()
    y_d = nc.dram_tensor("expert_out_scratch", (YT * P, D), F32, kind="Internal").ap()

    with ExitStack() as ctx:
        def sem(name):
            return ctx.enter_context(nc.semaphore(name))

        def sbc(c, name, shape, dt=F32):
            return c.enter_context(nc.sbuf_tensor(name, shape, dt))

        def sb(name, shape, dt=F32):
            return sbc(ctx, name, shape, dt)

        ident = sb("ident", [P, P])
        upper = sb("upper", [P, P])
        onesq = sb("onesq", [P, P])
        iota = sb("iota", [P, P])
        srcT = sb("srcT", [P, ETP], I32)
        dstT = sb("dstT", [P, ETP])
        start_col = sb("start_col", [P, NT])
        iota_g = sb("iota_g", [P, P])
        rdeg = sb("rdeg", [P, NT])
        zero2 = sb("zero2", [2, P], F32R)
        zero_row = sb("zero_row", [2, D], F32R)
        one2 = sb("one2", [2, P], F32R)
        ones_col = sb("ones_col", [P, 2], F32R)
        eps_col = sb("eps_col", [P, 1])
        rsel = sb("rsel", [2, 2])
        rseli = sb("rseli", [2, 2], I32)
        tab_first = sb("tab_first", [1, NT], I32)
        tab_group = sb("tab_group", [1, NT + 1], I32)
        tab_tiles = sb("tab_tiles", [1, NE + 1], I32)
        tab_end = sb("tab_end", [1, 2], I32)
        tab_row = sb("tab_row", [1, TQ], I32)
        tab_par = sb("tab_par", [1, TQ], I32)
        tab_set = sb("tab_set", [1, TQ], I32)
        tab_rows = sb("tab_rows", [1, NE], I32)
        wts_all = sb("wts", [P, 4, 2, KC, D], F32R)
        wts = [wts_all[:, 2 * i:2 * i + 2] for i in range(2)]
        w_raw = sb("w_raw", [P, 2, KC, D])
        bias_raw = sb("bias_raw", [2, 2, D])
        bias_t = sb("bias_t", [2, D])
        bias_u = sb("bias_u", [2, D])
        bias_all = sb("bias", [2, 4, D], F32R)
        bias = [bias_all[:, 2 * i:2 * i + 2] for i in range(2)]
        wg_s = sb("wg_s", [P, KC, NE])
        top2 = sb("top2", [P, 2, NT])
        posf = sb("posf", [P, NT, 2])
        posi = sb("posi", [P, NT, 2], I32)
        gate = sb("gate", [P, 2, NT])
        gate_e = sb("gate_e", [P, NT])
        gate_d = sb("gate_d", [P, NT])
        run = sb("run", [P, NE])

        with ExitStack() as c1:
            ln_in = [sbc(c1, f"ln_in{i}", [P, LN_ROWS, D]) for i in range(3)]
            ln_out = [sbc(c1, f"ln_out{i}", [P, LN_ROWS, D]) for i in range(3)]
            ln_bst = [sbc(c1, f"ln_bst{i}", [P, LN_ROWS, 6]) for i in range(2)]
            ln_mv = [sbc(c1, f"ln_mv{i}", [P, LN_ROWS, 2]) for i in range(2)]
            ln_std = [sbc(c1, f"ln_std{i}", [P, LN_ROWS]) for i in range(2)]
            ln_r = [sbc(c1, f"ln_r{i}", [P, LN_ROWS]) for i in range(2)]
            ln_b = [sbc(c1, f"ln_b{i}", [P, LN_ROWS]) for i in range(2)]
            ed_i = sbc(c1, "ed_i", [EP, 2, EB, P], I32)
            ed_f = sbc(c1, "ed_f", [EP, 2, EB, P])
            t_max = sbc(c1, "t_max", [EP, EB])
            t_min = sbc(c1, "t_min", [EP, EB])
            tid_i = sbc(c1, "tid_i", [EP, EB], I32)
            tid = sbc(c1, "tid", [EP, EB])
            thr_i = sbc(c1, "thr_i", [P, NT], I32)
            thr = sbc(c1, "thr", [P, NT])
            thr_hi = sbc(c1, "thr_hi", [P, NT])
            iota_i = sbc(c1, "iota_i", [P, P], I32)
            cmp_m = sbc(c1, "cmp_m", [EP, NT, EB])
            cmp_v = sbc(c1, "cmp_v", [EP, NT, EB])
            first_c = sbc(c1, "first_c", [EP, NT])
            end_c = sbc(c1, "end_c", [EP, NT])
            first_g = sbc(c1, "first_g", [NT, 1])
            end_g = sbc(c1, "end_g", [NT, 1])
            span_g = sbc(c1, "span_g", [NT, 1])
            gi_i = sbc(c1, "gi_i", [NT, MAXG], I32)
            gi = sbc(c1, "gi", [NT, MAXG])
            cmp_g = sbc(c1, "cmp_g", [NT, MAXG])
            n_g = sbc(c1, "n_g", [NT, 1])
            n_g2 = sbc(c1, "n_g2", [NT, 1])

        with ExitStack() as c2:
            rows = sbc(c2, "rows", [P, G, D])
            r_hi = sbc(c2, "r_hi", [P, G, D], F32R)
            r_lo = sbc(c2, "r_lo", [P, G, D], F32R)
            sel = sbc(c2, "sel", [P, G, P], F32R)
            idx = sbc(c2, "idx", [P, G], I32)
            agg_s = sbc(c2, "agg_s", [P, D])
            self_t = sbc(c2, "self_t", [P, D])
            aT = sbc(c2, "aT", [P, 2, KC, P], F32R)
            sT = sbc(c2, "sT", [P, 2, KC, P], F32R)
            h_t = sbc(c2, "h_t", [P, D])
            x_t = sbc(c2, "x_t", [P, D])
            x2_t = sbc(c2, "x2_t", [P, D])
            xn2_t = sbc(c2, "xn2_t", [P, D])
            xT = sbc(c2, "xT", [P, KC, P])
            deg_m = sbc(c2, "deg_m", [P, 1])
            bst = sbc(c2, "bst", [P, 6])
            mv = sbc(c2, "mv", [P, 2])
            std = sbc(c2, "std", [P, 1])
            rstd = sbc(c2, "rstd", [P, 1])
            nmr = sbc(c2, "nmr", [P, 1])
            lg = sbc(c2, "lg", [P, NE])
            mx8 = sbc(c2, "mx8", [P, NE])
            ix8 = sbc(c2, "ix8", [P, NE], U32)
            e01 = sbc(c2, "e01", [P, 2])
            mask = sbc(c2, "mask", [P, 2, NE])
            mask_s = sbc(c2, "mask_s", [P, NE])
            place = sbc(c2, "place", [P, NE])
            prod = sbc(c2, "prod", [P, 2, NE])
            pos_now = sbc(c2, "pos_now", [P, 2], I32)
            nrow = sbc(c2, "nrow", [P, NE])
            ti_i = sbc(c2, "ti_i", [P, NE, NT], I32)
            ti = sbc(c2, "ti", [P, NE, NT])
            ti_c = sbc(c2, "ti_c", [P, NE, NT])
            ntile = sbc(c2, "ntile", [P, NE])
            shift = sbc(c2, "shift", [P, NE])
            pos_c = sbc(c2, "pos_c", [P, 2 * NT, NE - 1])
            pos_s = sbc(c2, "pos_s", [P, 2 * NT])
            tcum = sbc(c2, "tcum", [1, NE + 1])
            tq_i = sbc(c2, "tq_i", [1, TQ], I32)
            tq = sbc(c2, "tq", [1, TQ])
            t_cmp, t_val = (rows[0:1, i:i + 2, :].rearrange("p a d -> p (a d)")[:, 0:TQ * NE]
                            .rearrange("p (q e) -> p q e", e=NE) for i in (0, 2))
            t_e = sbc(c2, "t_e", [1, TQ])
            t_in = sbc(c2, "t_in", [1, TQ])
            t_row = sbc(c2, "t_row", [1, TQ])
            sign = sbc(c2, "sign", [1, NE])
            ebase_i = sbc(c2, "ebase_i", [P, NE], I32)
            ebase = sbc(c2, "ebase", [P, NE])
            zrow = sbc(c2, "zrow", [P, D])

        with ExitStack() as c3:
            m_x = sbc(c3, "m_x", [P, D])
            m_xT = sbc(c3, "m_xT", [P, 2, KC, P], F32R)
            m_h = sbc(c3, "m_h", [P, D])
            m_hT = sbc(c3, "m_hT", [P, 2, KC, P], F32R)
            m_n = sbc(c3, "m_n", [P, D])
            m_ng = sbc(c3, "m_ng", [P, D])
            m_y = sbc(c3, "m_y", [P, D])
            m_bst = sbc(c3, "m_bst", [P, 6])
            m_mv = sbc(c3, "m_mv", [P, 2])
            m_std = sbc(c3, "m_std", [P, 1])
            m_r = sbc(c3, "m_r", [P, 1])
            m_b = sbc(c3, "m_b", [P, 1])
            gam = sbc(c3, "gam", [P, 2, D])
            bet = sbc(c3, "bet", [P, 2, D])

        with ExitStack() as c4:
            c_y = sbc(c4, "c_y", [P, CB, 2, D])
            c_x = sbc(c4, "c_x", [P, CB, D])
            c_t = sbc(c4, "c_t", [P, CB, D])
            c_idx = sbc(c4, "c_idx", [P, CB, 2], I32)

        ps = ctx.enter_context(nc.psum_tensor("ps", [P, 8, 512], F32))
        agg_p, deg_p, aT_p, sT_p, dense_p, xT_p, lg_p, pre_p = (ps[:, i, :] for i in range(8))
        mxT_p, mh_p, mhT_p, my_p = (ps[:, i, :] for i in range(4))

        s_const = sem("s_const")
        s_constv = sem("s_constv")
        s_ln_in = [sem(f"s_ln_in{i}") for i in range(3)]
        s_ln_st = sem("s_ln_st")
        s_ln_mv = sem("s_ln_mv")
        s_ln_std = sem("s_ln_std")
        s_ln_r = sem("s_ln_r")
        s_ln_b = sem("s_ln_b")
        s_ln_out = sem("s_ln_out")
        s_xn = sem("s_xn")
        s_pad = sem("s_pad")
        s_edges = sem("s_edges")
        s_tab = sem("s_tab")
        s_tabT = sem("s_tabT")
        s_raw = sem("s_raw")
        s_brow = sem("s_brow")
        s_raw_p = sem("s_raw_p")
        s_brow_p = sem("s_brow_p")
        s_split = sem("s_split")
        s_wset = sem("s_wset")
        s_wg = sem("s_wg")
        s_whi = sem("s_whi")
        s_wlo = sem("s_wlo")
        s_passed = sem("s_passed")
        s_bset = sem("s_bset")
        s_const2 = sem("s_const2")
        s_cv2 = sem("s_cv2")
        s_gate = sem("s_gate")
        s_place = sem("s_place")
        s_yzero = sem("s_yzero")

        names = ("iota idx hi lo seg node rdeg0 rdeg evac aggT aggHi aggLo self selfT selfHi "
                 "selfLo selfUsed dense res store xt bst mv std rstd nmr xn2 xT xTc logit lg mx ix e01 m0 m1 msum pref "
                 "place run prod pos posi scat").split()
        L = [{n: sem(f"s{l + 1}_{n}") for n in names if l == 1 or n not in
              ("xt bst mv std rstd nmr xn2 xT xTc logit lg mx ix e01 m0 m1 msum pref place run prod pos "
               "posi scat").split()} for l in range(2)]
        L_rows = [[sem(f"s{l + 1}_rows{k}") for k in range(G)] for l in range(2)]

        s_cnt = sem("s_cnt")
        s_gexp = sem("s_gexp")
        s_zero = sem("s_zero")
        M = {n: sem(f"m_{n}") for n in ("x xT xHi xLo h relu hT hHi hLo y bst mv std r b norm gam out "
                                        "store aff").split()}
        s_cidx = sem("s_cidx")
        s_cy = [sem(f"s_cy{j}") for j in range(CB)]
        s_cx = [sem(f"s_cx{j}") for j in range(CB)]
        s_ct = sem("s_ct")
        s_cacc = sem("s_cacc")
        s_cout = sem("s_cout")
        s_out = sem("s_out")

        CONST, CONSTV = 17, 11
        TAB_DONE = 23
        CNT_DONE = 28

        block = ctx.enter_context(nc.Block())

        def value(eng, cell, top):
            return eng.value_load(cell, min_val=0, max_val=top)

        def all_tiles(eng):
            return eng.value_load(tab_tiles[0:1, NE:NE + 1], min_val=2 * NT, max_val=YT - 1)

        def last_but_one(eng):
            return eng.value_load(tab_end[0:1, 0:1], min_val=2 * NT - 2, max_val=YT - 3)

        def weights_hi(act, n, par):
            act.wait_ge(s_raw, n * 32 + 32)
            for m in range(2):
                act.activation(wts[par][:, m, 0], w_raw[:, m], ACT.Copy).then_inc(s_whi, 1)

        def weights_lo(dve, n, par):
            for m in range(2):
                dve.wait_ge(s_whi, n * 2 + m + 1)
                dve.tensor_tensor(wts[par][:, m, 1], w_raw[:, m], wts[par][:, m, 0].bitcast(F32),
                                  ALU.subtract).then_inc(s_wlo, 1)

        def alone(eng, semaphore, v):
            eng.wait_ge(semaphore, v)
            eng.sem_inc(s_passed, 1)

        def within(v, top):
            return v if isinstance(v, int) else v.with_bounds(min_val=0, max_val=top)

        def layer(eng, group, hooks, opening=None, tail=None):
            back = max([d for fs in hooks.values() for _, d in fs] + [0])

            def tile(g):
                at = (lambda t, i: t[0:1, i:i + 1]) if isinstance(g, int) else (lambda t, i: t[0:1, bass.ds(i, 1)])
                c0 = value(eng, at(tab_group, g), NT * MAXG)
                c1 = value(eng, at(tab_group, g + 1), NT * MAXG)
                t0 = value(eng, at(tab_first, g), ET)
                steps = {k: [(f, g - d) for f, d in fs if not isinstance(g, int) or g >= d] for k, fs in hooks.items()}
                if opening:
                    opening(g, c0)
                group(g, c0, t0, {k: f for k, f in steps.items() if k < G})
                group(g, c0 + 1, t0 + G, {k - G: f for k, f in steps.items() if k >= G})
                with eng.If_lt(eng.to_reg(c0 + 2), eng.to_reg(c1)):
                    with eng.Fori(c0 + 2, c1) as c:
                        group(g, c, within(t0 + (c - c0) * G, ETP - G), {})
                if tail:
                    tail(g)

            for g in range(back + 1):
                tile(g)
            with eng.Fori(back + 1, NT) as g:
                tile(g)
            for g in range(NT, NT + back):
                for k in sorted(hooks):
                    for f, d in hooks[k]:
                        if g - d < NT:
                            f(g - d)

        def run_hooks(hooks, k):
            for f, n in hooks.get(k, []):
                f(n)

        def rows_at(t, n):
            return t[start_of(n):start_of(n) + P, :] if isinstance(n, int) else t[bass.ds(n * P, P), :]

        @block.sync
        def _(sp):
            def load_chunk(c):
                r0 = min(c * P * LN_ROWS, N - P * LN_ROWS)
                sp.dma_start(ln_in[c % 3][:], x[r0:r0 + P * LN_ROWS, :].rearrange("(p j) d -> p j d", p=P)) \
                    .then_inc(s_ln_in[c % 3], 16)

            def store_chunk(c):
                r0 = min(c * P * LN_ROWS, N - P * LN_ROWS)
                sp.wait_ge(s_ln_out, c + 1)
                if c == LN_CH - 1:
                    sp.wait_ge(s_xn, 16 * c)
                sp.dma_start(xn_d[r0:r0 + P * LN_ROWS, :].rearrange("(p j) d -> p j d", p=P),
                             ln_out[c % 3][:]).then_inc(s_xn, 16)

            def load_set(n, wa, wb, ba, bb):
                if not (isinstance(n, int) and n == 0):
                    sp.wait_ge(s_wset, n)
                sp.dma_start(w_raw[:, 0], wa.rearrange("(k p) n -> p k n", p=P)).then_inc(s_raw, 16)
                sp.dma_start(w_raw[:, 1], wb.rearrange("(k p) n -> p k n", p=P)).then_inc(s_raw, 16)
                for j, b in enumerate((ba, bb)):
                    sp.dma_start(bias_raw[:, j, :], b.to_broadcast([2, D])).then_inc(s_brow, 16)

            load_chunk(0)
            sp.wait_ge(s_pad, 2)
            full = (EB - 1) * EP * P
            tail_rows = (E - full) // P
            for j, lst in enumerate((src, dst)):
                sp.dma_start(ed_i[:, j, 0:EB - 1, :],
                             lst[0:full].rearrange("(b p e) -> p b e", p=EP, e=P)).then_inc(s_edges, 16)
                sp.dma_start(ed_i[0:tail_rows, j, EB - 1, :],
                             lst[full:full + tail_rows * P].rearrange("(p e) -> p e", e=P)).then_inc(s_edges, 16)
                sp.dma_start(ed_i[tail_rows:tail_rows + 1, j, EB - 1, 0:E - full - tail_rows * P],
                             lst[full + tail_rows * P:E].rearrange("(a e) -> a e", a=1)).then_inc(s_edges, 16)
            load_chunk(1)
            load_chunk(2)
            sp.dma_start(wg_s[:], Wg.rearrange("(k p) e -> p k e", p=P)).then_inc(s_wg, 16)
            brow = lambda b: b.rearrange("(a n) -> a n", a=1)
            for c in range(LN_CH):
                store_chunk(c)
                if c + 3 < LN_CH:
                    load_chunk(c + 3)
                if c == 2:
                    load_set(0, w_neigh1, w_self1, brow(b1), brow(b1))
                if c == 7:
                    load_set(1, w_neigh2, w_self2, brow(b2), brow(b2))

            for l, own, res_d, res in ((0, xn_d, h1_d, h_t), (1, h1_d, x2_d, x2_t)):
                S = L[l]
                if l == 0:
                    sp.wait_ge(s_xn, 16 * LN_CH)
                else:
                    load_set(2, W1[0], W2[0], eb1[0:1], eb2[0:1])
                    sp.wait_ge(L[0]["store"], 16 * NT)

                def load_tile(n):
                    if not (isinstance(n, int) and n == 0):
                        alone(sp, S["selfT"], n)
                        sp.wait_ge(S["self"], n * 16)
                    elif l == 1:
                        sp.wait_ge(L[0]["selfT"], NT)
                    sp.dma_start(self_t[:], rows_at(own, n)).then_inc(S["self"], 16)
                    if l == 1:
                        if not (isinstance(n, int) and n == 0):
                            sp.wait_ge(S["res"], n)
                            sp.wait_ge(S["xt"], n * 16)
                        sp.dma_start(x_t[:], rows_at(x, n)).then_inc(S["xt"], 16)

                def store_tile(n):
                    sp.wait_ge(S["res"], n + 1)
                    if isinstance(n, int):
                        sp.wait_ge(S["store"], 16 * n)
                    sp.dma_start(rows_at(res_d, n), res[:]).then_inc(S["store"], 16)

                load_tile(0)
                with sp.Fori(0, NT - 2) as n:
                    load_tile(n + 1)
                    store_tile(n)
                load_tile(NT - 1)
                sp.wait_ge(S["res"], NT - 1)
                sp.dma_start(res_d[(NT - 2) * P:(NT - 1) * P, :], res[:]).then_inc(S["store"], 16)
                store_tile(NT - 1)

            sp.wait_ge(L[1]["scat"], 32 * NT)
            sp.wait_ge(s_cnt, CNT_DONE)
            for e in range(NE):
                r = value(sp, tab_rows[0:1, e:e + 1], (NE - 1) * REGION + NT * P)
                sp.dma_start(disp_d[bass.ds(r, P), :], zrow[:]).then_inc(s_zero, 16)
            sp.wait_ge(s_zero, 16 * NE)

            def load_x(q):
                row = value(sp, tab_row[0:1, q:q + 1] if isinstance(q, int) else tab_row[0:1, bass.ds(q, 1)],
                            NE * REGION - P)
                if not (isinstance(q, int) and q == 0):
                    sp.wait_ge(M["xT"], q)
                sp.dma_start(m_x[:], disp_d[bass.ds(row, P), :]).then_inc(M["x"], 16)

            def store_y(q):
                alone(sp, M["out"], q + 2)
                sp.dma_start(y_d[q * P:(q + 1) * P, :] if isinstance(q, int) else y_d[bass.ds(q * P, P), :],
                             m_y[:]).then_inc(M["store"], 16)

            qT = all_tiles(sp)
            load_x(0)
            load_x(1)
            load_x(2)
            with sp.Fori(2, qT) as q:
                load_x(q + 1)
                store_y(q - 2)
            qe = last_but_one(sp)
            store_y(qe)
            store_y(qe + 1)
            alone(sp, M["store"], qT * 16)
            alone(sp, M["xLo"], qT + 1)

            def combine_loads(a):
                for j in range(CB):
                    n = a * CB + j
                    if not (isinstance(a, int) and a == 0):
                        alone(sp, s_ct, n - CB + 1)
                        alone(sp, s_cx[j], 16 * a)
                    sp.dma_start(c_x[:, j, :], rows_at(x2_d, n)).then_inc(s_cx[j], 16)

            def combine_stores(a):
                for j in range(CB):
                    n = a * CB + j
                    sp.wait_ge(s_cacc, n + 1)
                    if isinstance(n, int) and n == NT - 1:
                        sp.wait_ge(s_out, 16 * n)
                    sp.dma_start(rows_at(out, n), c_t[:, j, :]).then_inc(s_out, 16)

            combine_loads(0)
            with sp.Fori(0, NT // CB - 2) as a:
                combine_stores(a)
                combine_loads(a + 1)
            combine_stores(NT // CB - 2)
            combine_loads(NT // CB - 1)
            combine_stores(NT // CB - 1)
            sp.wait_ge(s_out, 16 * NT)

        @block.gpsimd
        def _(pool):
            k = [0]

            def did(ins, wait=False):
                k[0] += 1
                ins.then_inc(s_const, 1)
                if wait:
                    pool.wait_ge(s_const, k[0])

            pool.memset(ed_i[:, 1, EB - 1, :], int(FAR)).then_inc(s_pad, 1)
            pool.memset(ed_i[:, 0, EB - 1, :], 0).then_inc(s_pad, 1)
            did(pool.iota(iota_i[:], pattern=[[1, P]], base=0, channel_multiplier=0))
            did(pool.iota(thr_i[:], pattern=[[P, NT]], base=0, channel_multiplier=0))
            did(pool.iota(tid_i[:], pattern=[[EP, EB]], base=0, channel_multiplier=1))
            did(pool.iota(gi_i[:], pattern=[[G, MAXG]], base=0, channel_multiplier=0))
            did(pool.iota(rseli[:], pattern=[[1, 2]], base=0, channel_multiplier=1))
            did(pool.memset(eps_col[:], EPS))
            did(pool.memset(zero2[:].bitcast(F32), 0.0))
            did(pool.memset(one2[:].bitcast(F32), 1.0))
            did(pool.memset(ones_col[:].bitcast(F32), 1.0))
            did(pool.memset(onesq[:], 1.0))
            did(pool.memset(ident[:], 0.0), wait=True)
            did(pool.affine_select(out=ident[:], in_=ident[:], compare_op=ALU.not_equal, fill=1.0, base=0,
                                   pattern=[[-1, P]], channel_multiplier=1))
            did(pool.memset(upper[:], 1.0), wait=True)
            did(pool.affine_select(out=upper[:], in_=upper[:], compare_op=ALU.is_ge, fill=0.0, base=-1,
                                   pattern=[[1, P]], channel_multiplier=-1))
            did(pool.memset(srcT[:, ET:ETP], 0))
            did(pool.memset(dstT[:, ET:ETP], FAR))
            did(pool.memset(zero_row[:].bitcast(F32), 0.0))
            assert k[0] == CONST

            def split_set(n, par):
                early = isinstance(n, int) and n < 3
                if early:
                    pool.wait_ge(s_raw, n * 32 + 32)
                    pool.wait_ge(s_brow, n * 32 + 32)
                else:
                    alone(pool, s_raw_p, (n - 2) * 32)
                    alone(pool, s_brow_p, (n - 2) * 32)
                base = n * 10
                for m in range(2):
                    if early:
                        pool.wait_ge(s_wlo, n * 2 + m + 1)
                        pool.sem_inc(s_split, 2)
                    else:
                        pool.tensor_copy(wts[par][:, m, 0], w_raw[:, m]).then_inc(s_split, 1)
                        alone(pool, s_split, base + 5 * m + 1)
                        pool.tensor_tensor(wts[par][:, m, 1], w_raw[:, m], wts[par][:, m, 0].bitcast(F32),
                                           ALU.subtract).then_inc(s_split, 1)
                    pool.tensor_copy(bias[par][:, m, :], bias_raw[:, m, :]).then_inc(s_split, 1)
                    alone(pool, s_split, base + 5 * m + 3)
                    pool.tensor_scalar(bias_t[:], bias[par][:, m, :].bitcast(F32), rsel[:, 1:2], None,
                                       ALU.mult).then_inc(s_split, 1)
                    pool.tensor_scalar(bias_u[:], bias_raw[:, m, :], rsel[:, 0:1], None,
                                       ALU.mult).then_inc(s_split, 1)
                    alone(pool, s_split, base + 5 * m + 5)
                    pool.tensor_tensor(bias[par][:, m, :], bias_t[:], bias_u[:], ALU.add) \
                        .then_inc(s_wset if m else s_bset, 1)
                    if not m:
                        alone(pool, s_bset, n + 1)

            pool.wait_ge(s_constv, CONSTV)
            split_set(0, 0)
            split_set(1, 1)

            pool.wait_ge(s_tab, TAB_DONE)
            for l, rows_d in ((0, xn_d), (1, h1_d)):
                S = L[l]
                if l == 0:
                    pool.wait_ge(s_xn, 16 * LN_CH)
                else:
                    pool.wait_ge(L[0]["store"], 16 * NT)
                    pool.iota(ebase_i[:], pattern=[[REGION, NE]], base=0, channel_multiplier=0).then_inc(s_const2, 1)
                    pool.iota(ti_i[:], pattern=[[0, NE], [P, NT]], base=0, channel_multiplier=0).then_inc(s_const2, 1)
                    pool.iota(tq_i[:], pattern=[[1, TQ]], base=0, channel_multiplier=0).then_inc(s_const2, 1)

                def gathers(g, c, t, hooks):
                    for k in range(G):
                        run_hooks(hooks, k)
                        if k in IDX_AT:
                            w = IDX_AT[k]
                            alone(pool, S["hi"], c * G + (k + w))
                            alone(pool, S["lo"], c * G + (k + w))
                            pool.tensor_copy(idx[:, k:k + w], srcT[:, bass.ds(t + k, w)]).then_inc(S["idx"], 1)
                            alone(pool, S["idx"], c * len(IDX_AT) + (1 + (k > 0)))
                        pool.indirect_dma_start(
                            rows[:, k, :], None, rows_d,
                            bass.IndirectOffsetOnAxis(ap=idx[:, k:k + 1], axis=0)).then_inc(L_rows[l][k], 16)
                    run_hooks(hooks, G)

                def scatter(n):
                    alone(pool, S["posi"], n + 1)
                    for j in range(2):
                        pool.indirect_dma_start(
                            disp_d, bass.IndirectOffsetOnAxis(ap=pos_now[:, j:j + 1], axis=0),
                            xn2_t[:], None) \
                            .then_inc(S["scat"], 16)

                layer(pool, gathers, {16: [(scatter, 2)]} if l == 1 else {})

            def load_expert(n, e, par):
                at = (lambda t: t[e:e + 1]) if isinstance(e, int) else (lambda t: t[bass.ds(e, 1)])
                for m, w in enumerate((W1, W2)):
                    pool.dma_start(w_raw[:, m], at(w).rearrange("a (k p) n -> p (a k) n", p=P)).then_inc(s_raw_p, 16)
                for m, b in enumerate((eb1, eb2)):
                    pool.dma_start(bias_raw[:, m, :], at(b).to_broadcast([2, D])).then_inc(s_brow_p, 16)
                affine(e, par)

            def affine(e, par):
                at = (lambda t: t[e:e + 1]) if isinstance(e, int) else (lambda t: t[bass.ds(e, 1)])
                for t, d in ((gam, gamma), (bet, beta)):
                    pool.dma_start(t[:, par], at(d).to_broadcast([P, D])).then_inc(M["aff"], 16)

            pool.wait_ge(L[1]["evac"], NT)
            pool.wait_ge(L[1]["scat"], 32 * NT)
            pool.wait_ge(s_cnt, CNT_DONE)
            affine(0, 0)
            pool.wait_ge(M["aff"], 32)
            split_set(2, 0)
            load_expert(3, 1, 1)
            pool.wait_ge(L[1]["dense"], NT)
            pool.wait_ge(M["aff"], 64)
            split_set(3, 1)
            qT = all_tiles(pool)
            with pool.Fori(qT, YT) as j:
                pool.dma_start(y_d[bass.ds(j * P, P), :], zrow[:]).then_inc(s_yzero, 16)
            rest = pool.value_load(tab_end[0:1, 1:2], min_val=1, max_val=YT - 2 * NT)
            alone(pool, s_yzero, rest * 16)
            with pool.Fori(1, NE // 2) as e2:
                for par in range(2):
                    e = e2 * 2 + par
                    q = value(pool, tab_tiles[0:1, bass.ds(within(e - 1, NE), 1)], YT - 1)
                    alone(pool, M["y"], q + 1)
                    alone(pool, M["out"], q + 1)
                    load_expert(e + 2, e, par)
                    alone(pool, M["aff"], e * 32 + 32)
                    split_set(e + 2, par)

            qT = all_tiles(pool)
            alone(pool, M["store"], qT * 16)
            alone(pool, M["xLo"], qT + 1)
            pool.wait_ge(s_place, 4)

            def combine_gathers(a):
                for j in range(CB):
                    n = a * CB + j
                    if not (isinstance(a, int) and a == 0):
                        alone(pool, s_cacc, n - CB + 1)
                        alone(pool, s_cy[j], 32 * a)
                    pool.tensor_copy(c_idx[:, j, :], posi[:, n, :] if isinstance(n, int) else
                                     posi[:, bass.ds(n, 1), :].rearrange("p a j -> p (a j)")).then_inc(s_cidx, 1)
                    alone(pool, s_cidx, n + 1)
                    for i in range(2):
                        pool.indirect_dma_start(
                            c_y[:, j, i, :], None, y_d,
                            bass.IndirectOffsetOnAxis(ap=c_idx[:, j, i:i + 1], axis=0)).then_inc(s_cy[j], 16)

            combine_gathers(0)
            with pool.Fori(1, NT // CB) as a:
                combine_gathers(a)

        @block.scalar
        def _(act):
            act.wait_ge(s_const, CONST)

            def ln_sqrt(c):
                act.wait_ge(s_ln_mv, c + 1)
                act.activation(ln_std[c % 2][:], ln_mv[c % 2][:, :, 1], ACT.Sqrt, bias=eps_col[:, 0:1],
                               scale=1.0).then_inc(s_ln_std, 1)

            def ln_norm(c):
                act.wait_ge(s_ln_b, c + 1)
                if c >= 3:
                    act.wait_ge(s_xn, 16 * (c - 2))
                for j in range(LN_ROWS):
                    i = act.activation(ln_out[c % 3][:, j, :], ln_in[c % 3][:, j, :], ACT.Identity,
                                       bias=ln_b[c % 2][:, j:j + 1], scale=ln_r[c % 2][:, j:j + 1])
                i.then_inc(s_ln_out, 1)

            ln_sqrt(0)
            for c in range(LN_CH):
                if c + 1 < LN_CH:
                    ln_sqrt(c + 1)
                ln_norm(c)
                if c in WSPLIT_AT:
                    weights_hi(act, WSPLIT_AT.index(c), WSPLIT_AT.index(c))

            act.wait_ge(s_tab, TAB_DONE)
            for l in range(2):
                S = L[l]
                act.wait_ge(s_ln_out, LN_CH)
                if l == 1:
                    weights_hi(act, 2, 0)
                act.sem_inc(S["hi"], G)

                def halves(g, c, t, hooks):
                    for k in range(G):
                        run_hooks(hooks, k)
                        act.wait_ge(L_rows[l][k], c * 16 + 16)
                        act.wait_ge(S["seg"], c * G + (k + 1))
                        act.activation(r_hi[:, k, :], rows[:, k, :], ACT.Copy).then_inc(S["hi"], 1)
                    run_hooks(hooks, G)

                def evac(g):
                    act.wait_ge(S["node"], g + 1)
                    if l == 0:
                        act.wait_ge(S["rdeg"], g + 1)
                    act.wait_ge(S["aggT"], g)
                    act.activation(agg_s[:], agg_p, ACT.Identity,
                                   scale=rdeg[:, g:g + 1] if isinstance(g, int) else
                                   rdeg[:, bass.ds(g, 1)]).then_inc(S["evac"], 1)

                def self_hi(n):
                    act.wait_ge(S["selfT"], n + 1)
                    act.wait_ge(S["selfUsed"], n)
                    act.activation(sT[:, 0].rearrange("p k n -> p (k n)"), sT_p, ACT.Copy).then_inc(S["selfHi"], 1)

                def agg_hi(n):
                    act.wait_ge(S["aggT"], n + 1)
                    act.wait_ge(S["dense"], n)
                    act.activation(aT[:, 0].rearrange("p k n -> p (k n)"), aT_p, ACT.Copy).then_inc(S["aggHi"], 1)

                def relu(n):
                    act.wait_ge(S["dense"], n + 1)
                    act.wait_ge(S["store"], n * 16)
                    act.activation(h_t[:], dense_p, ACT.Relu).then_inc(S["res"], 1)

                def sqrt2(n):
                    act.wait_ge(S["mv"], n + 1)
                    act.activation(std[:], mv[:, 1:2], ACT.Sqrt, bias=eps_col[:, 0:1],
                                   scale=1.0).then_inc(S["std"], 1)

                def norm2(n):
                    act.wait_ge(S["nmr"], n + 1)
                    act.wait_ge(S["scat"], n * 32)
                    act.wait_ge(S["xT"], n)
                    act.activation(xn2_t[:], x2_t[:], ACT.Identity, bias=nmr[:, 0:1],
                                   scale=rstd[:, 0:1]).then_inc(S["xn2"], 1)

                def xT_copy(n):
                    act.wait_ge(S["xT"], n + 1)
                    act.wait_ge(S["logit"], n)
                    act.activation(xT[:].rearrange("p k n -> p (k n)"), xT_p, ACT.Copy).then_inc(S["xTc"], 1)

                hooks = {2: [(evac, 1)], 4: [(agg_hi, 1)], 11: [(self_hi, 0)]}
                if l == 0:
                    hooks[10] = [(relu, 1)]
                else:
                    hooks.update({12: [(sqrt2, 1)], 15: [(norm2, 1)], 17: [(xT_copy, 1)]})
                layer(act, halves, hooks)

            def x_hi(q):
                act.wait_ge(M["xT"], q + 1)
                act.wait_ge(M["h"], q)
                act.activation(m_xT[:, 0].rearrange("p k n -> p (k n)"), mxT_p, ACT.Copy).then_inc(M["xHi"], 1)

            def h_hi(q):
                act.wait_ge(M["hT"], q + 1)
                act.wait_ge(M["y"], q + 1)
                act.activation(m_hT[:, 0].rearrange("p k n -> p (k n)"), mhT_p, ACT.Copy).then_inc(M["hHi"], 1)

            def m_relu(q):
                act.wait_ge(M["h"], q + 1)
                act.wait_ge(M["hT"], q)
                act.activation(m_h[:], mh_p, ACT.Relu).then_inc(M["relu"], 1)

            def m_norm(q):
                act.wait_ge(M["mv"], q + 1)
                act.activation(m_std[:], m_mv[:, 1:2], ACT.Sqrt, bias=eps_col[:, 0:1],
                               scale=1.0).then_inc(M["std"], 1)
                act.wait_ge(M["b"], q + 1)
                act.wait_ge(M["gam"], q)
                act.activation(m_n[:], my_p, ACT.Identity, bias=m_b[:, 0:1],
                               scale=m_r[:, 0:1]).then_inc(M["norm"], 1)

            act.wait_ge(s_cnt, CNT_DONE)
            qT = all_tiles(act)
            x_hi(0)

            def tile_m(q):
                if not isinstance(q, int) or q >= 1:
                    h_hi(q - 1)
                if not isinstance(q, int) or q >= 2:
                    m_norm(q - 2)
                m_relu(q)
                x_hi(q + 1)

            for q in range(3):
                tile_m(q)
            with act.Fori(3, qT) as q:
                tile_m(q)
            qe = last_but_one(act)
            h_hi(qe + 1)
            m_norm(qe)
            m_norm(qe + 1)

            act.wait_ge(s_cnt, 1)
            act.activation(gate_e[:], gate_d[:], ACT.Exp).then_inc(s_gexp, 1)

        @block.vector
        def _(dve):
            kv = [0]

            def didv(ins, wait=False):
                kv[0] += 1
                ins.then_inc(s_constv, 1)
                if wait:
                    dve.wait_ge(s_constv, kv[0])

            dve.wait_ge(s_const, CONST)
            didv(dve.tensor_copy(iota[:], iota_i[:]))
            didv(dve.tensor_copy(tid[:], tid_i[:]))
            didv(dve.tensor_copy(gi[:], gi_i[:]))
            didv(dve.tensor_copy(rsel[:, 0:1], rseli[:, 0:1]))
            didv(dve.tensor_scalar(rsel[:, 1:2], rseli[:, 1:2], -2.0, 3.0, ALU.mult, ALU.add))
            didv(dve.tensor_copy(thr[:], thr_i[:]), wait=True)
            didv(dve.memset(thr[:, NT - 1:NT], float(LAST)), wait=True)
            didv(dve.tensor_scalar(thr_hi[:], thr[:], float(P), None, ALU.add))
            didv(dve.tensor_copy(start_col[:], thr[:]))
            didv(dve.memset(run[:], 0.0))
            didv(dve.memset(top2[:], 0.0), wait=True)
            assert kv[0] == CONSTV

            kt = [0]

            def t(ins, wait=True):
                kt[0] += 1
                ins.then_inc(s_tab, 1)
                if wait:
                    dve.wait_ge(s_tab, kt[0])

            def ln_stats(c):
                dve.wait_ge(s_ln_in[c % 3], 16 * (c // 3 + 1))
                for j in range(LN_ROWS):
                    i = dve.bn_stats(ln_bst[c % 2][:, j, :], ln_in[c % 3][:, j, :])
                i.then_inc(s_ln_st, 1)
                dve.wait_ge(s_ln_st, c + 1)
                if c >= 2:
                    dve.wait_ge(s_ln_out, c - 1)
                for j in range(LN_ROWS):
                    i = dve.bn_aggr(ln_mv[c % 2][:, j, :], ln_bst[c % 2][:, j, :])
                i.then_inc(s_ln_mv, 1)

            def ln_scale(c):
                dve.wait_ge(s_ln_std, c + 1)
                if c >= 2:
                    dve.wait_ge(s_ln_out, c - 1)
                dve.reciprocal(ln_r[c % 2][:], ln_std[c % 2][:]).then_inc(s_ln_r, 1)
                dve.wait_ge(s_ln_r, c + 1)
                dve.scalar_tensor_tensor(out=ln_b[c % 2][:], in0=ln_mv[c % 2][:, :, 0], scalar=-1.0,
                                         in1=ln_r[c % 2][:], op0=ALU.mult, op1=ALU.mult).then_inc(s_ln_b, 1)

            def tables():
                dve.wait_ge(s_edges, 96)
                t(dve.tensor_copy(ed_f[:, 0], ed_i[:, 0]), wait=False)
                t(dve.tensor_copy(ed_f[:, 1], ed_i[:, 1]))
                t(dve.tensor_reduce(out=t_max[:], in_=ed_f[:, 1], axis=AX.X, op=ALU.max), wait=False)
                t(dve.tensor_reduce(out=t_min[:], in_=ed_f[:, 1], axis=AX.X, op=ALU.min))
                over_g = lambda a: a.unsqueeze(1).to_broadcast([EP, NT, EB])
                over_b = lambda a: a[0:EP, :].unsqueeze(2).to_broadcast([EP, NT, EB])
                t(dve.tensor_tensor(cmp_m[:], over_g(t_max[:]), over_b(thr[:]), ALU.is_lt))
                t(dve.scalar_tensor_tensor(out=cmp_v[:], in0=cmp_m[:], scalar=float(ET), in1=over_g(tid[:]),
                                           op0=ALU.mult, op1=ALU.max))
                t(dve.tensor_reduce(out=first_c[:], in_=cmp_v[:], axis=AX.X, op=ALU.min))
                t(dve.tensor_tensor(cmp_m[:], over_g(t_min[:]), over_b(thr_hi[:]), ALU.is_lt))
                t(dve.tensor_tensor(cmp_v[:], cmp_m[:], over_g(tid[:]), ALU.mult))
                t(dve.tensor_tensor(cmp_v[:], cmp_v[:], cmp_m[:], ALU.add))
                t(dve.tensor_reduce(out=end_c[:], in_=cmp_v[:], axis=AX.X, op=ALU.max))

            def tables2():
                dve.wait_ge(s_tabT, 1)
                t(dve.tensor_reduce(out=first_g[:], in_=ps[0:NT, 4, 0:EP], axis=AX.X, op=ALU.min), wait=False)
                t(dve.tensor_reduce(out=end_g[:], in_=ps[0:NT, 4, P:P + EP], axis=AX.X, op=ALU.max))
                t(dve.tensor_tensor(span_g[:], end_g[:], first_g[:], ALU.subtract))
                t(dve.tensor_scalar(cmp_g[:], gi[:], span_g[:, 0:1], None, ALU.is_lt))
                t(dve.tensor_reduce(out=n_g[:], in_=cmp_g[:], axis=AX.X, op=ALU.add))
                t(dve.tensor_scalar(n_g2[:], n_g[:], 2.0, None, ALU.max))
                dve.wait_ge(s_tabT, 2)
                for j in range(2):
                    dstl = srcT if j == 0 else dstT
                    t(dve.tensor_copy(dstl[:, 0:4 * EP], ps[:, 2 * j, 0:4 * EP]), wait=False)
                    t(dve.tensor_copy(dstl[:, 4 * EP:ET], ps[:, 2 * j + 1, 0:3 * EP]), wait=False)
                dve.wait_ge(s_tabT, 3)
                t(dve.tensor_copy(tab_group[:], ps[0:1, 5, 0:NT + 1]), wait=False)
                t(dve.tensor_copy(tab_first[:], ps[0:1, 5, P:P + NT]))
                assert kt[0] == TAB_DONE

            ln_stats(0)
            for c in range(LN_CH):
                if c + 1 < LN_CH:
                    ln_stats(c + 1)
                ln_scale(c)
                if c == 1:
                    tables()
                if c == 4:
                    tables2()
                if c in WSPLIT_AT:
                    weights_lo(dve, WSPLIT_AT.index(c), WSPLIT_AT.index(c))

            dve.wait_ge(s_tab, TAB_DONE)
            for l in range(2):
                S = L[l]
                dve.wait_ge(s_ln_out, LN_CH)
                if l == 1:
                    dve.wait_ge(s_const2, 3)
                    dve.tensor_copy(ebase[:], ebase_i[:]).then_inc(s_cv2, 1)
                    dve.tensor_copy(ti[:], ti_i[:]).then_inc(s_cv2, 1)
                    dve.tensor_copy(tq[:], tq_i[:]).then_inc(s_cv2, 1)
                    dve.memset(zrow[:], 0.0).then_inc(s_cv2, 1)
                    for e in range(NE):
                        dve.memset(sign[:, e:e + 1], 1.0 - 2.0 * (e % 2)).then_inc(s_cv2, 1)
                    dve.wait_ge(s_cv2, 4 + NE)
                    dve.tensor_copy(run[:], ebase[:]).then_inc(s_cv2, 1)
                    dve.wait_ge(s_cv2, 5 + NE)
                if l == 1:
                    weights_lo(dve, 2, 0)
                dve.sem_inc(S["lo"], G)

                def tile_iota(g, c0):
                    dve.wait_ge(S["lo"], c0 * G + G)
                    dve.tensor_scalar(iota_g[:], iota[:], start_col[:, bass.ds(g, 1)], None,
                                      ALU.add).then_inc(S["iota"], 1)
                    dve.wait_ge(S["iota"], g + 1)

                def select(g, c, t, hooks):
                    for k in range(G):
                        run_hooks(hooks, k)
                        if k % SELW == 0:
                            dve.wait_ge(S["seg"], c * G + (k + SELW))
                            dve.tensor_tensor(
                                sel[:, k:k + SELW, :], iota_g[:].unsqueeze(1).to_broadcast([P, SELW, P]),
                                dstT[:, bass.ds(t + k, SELW)].unsqueeze(2).to_broadcast([P, SELW, P]),
                                ALU.is_equal)
                        dve.wait_ge(L_rows[l][k], c * 16 + 16)
                        dve.wait_ge(S["hi"], c * G + (k + 1 + G))
                        dve.tensor_tensor(r_lo[:, k, :], rows[:, k, :], r_hi[:, k, :].bitcast(F32),
                                          ALU.subtract).then_inc(S["lo"], 1)
                    run_hooks(hooks, G)

                def degree(g):
                    dve.wait_ge(S["node"], g + 1)
                    dve.tensor_scalar(deg_m[:], deg_p[:, 0:1], 1.0, None, ALU.max).then_inc(S["rdeg0"], 1)
                    dve.wait_ge(S["rdeg0"], g + 1)
                    dve.reciprocal(rdeg[:, g:g + 1] if isinstance(g, int) else rdeg[:, bass.ds(g, 1)],
                                   deg_m[:]).then_inc(S["rdeg"], 1)

                def self_lo(n):
                    dve.wait_ge(S["selfHi"], n + 1)
                    dve.tensor_tensor(sT[:, 1].rearrange("p k n -> p (k n)"), sT_p,
                                      sT[:, 0].rearrange("p k n -> p (k n)").bitcast(F32),
                                      ALU.subtract).then_inc(S["selfLo"], 1)

                def agg_lo(n):
                    dve.wait_ge(S["aggHi"], n + 1)
                    dve.tensor_tensor(aT[:, 1].rearrange("p k n -> p (k n)"), aT_p,
                                      aT[:, 0].rearrange("p k n -> p (k n)").bitcast(F32),
                                      ALU.subtract).then_inc(S["aggLo"], 1)

                def residual(n):
                    dve.wait_ge(S["dense"], n + 1)
                    dve.wait_ge(S["xt"], n * 16 + 16)
                    dve.wait_ge(S["store"], n * 16)
                    dve.wait_ge(S["xn2"], n)
                    dve.scalar_tensor_tensor(out=x2_t[:], in0=dense_p, scalar=0.0, in1=x_t[:], op0=ALU.max,
                                             op1=ALU.add).then_inc(S["res"], 1)
                    dve.wait_ge(S["res"], n + 1)
                    dve.bn_stats(bst[:], x2_t[:]).then_inc(S["bst"], 1)
                    alone(dve, S["bst"], n + 1)
                    dve.bn_aggr(mv[:], bst[:]).then_inc(S["mv"], 1)

                def scales(n):
                    dve.wait_ge(S["std"], n + 1)
                    dve.reciprocal(rstd[:], std[:]).then_inc(S["rstd"], 1)
                    dve.wait_ge(S["rstd"], n + 1)
                    dve.scalar_tensor_tensor(out=nmr[:], in0=mv[:, 0:1], scalar=-1.0, in1=rstd[:],
                                             op0=ALU.mult, op1=ALU.mult).then_inc(S["nmr"], 1)

                def top_two(n):
                    one = (lambda a: a[:, :, n:n + 1]) if isinstance(n, int) else (lambda a: a[:, :, bass.ds(n, 1)])
                    dve.wait_ge(S["logit"], n + 1)
                    dve.tensor_copy(lg[:], lg_p[:, 0:NE]).then_inc(S["lg"], 1)
                    alone(dve, S["lg"], n + 1)
                    dve.max(mx8[:], lg[:]).then_inc(S["mx"], 1)
                    alone(dve, S["mx"], n + 1)
                    dve.max_index(ix8[:], mx8[:], lg[:]).then_inc(S["ix"], 1)
                    dve.tensor_copy(one(top2[:]), mx8[:, 0:2].unsqueeze(2))
                    dve.wait_ge(S["ix"], n + 1)
                    dve.tensor_copy(e01[:], ix8[:, 0:2]).then_inc(S["e01"], 1)
                    dve.wait_ge(S["e01"], n + 1)
                    for j in range(2):
                        dve.tensor_scalar(mask[:, j, :], iota[:, 0:NE], e01[:, j:j + 1], None,
                                          ALU.is_equal).then_inc(S[f"m{j}"], 1)
                    dve.wait_ge(S["m1"], n + 1)
                    dve.tensor_tensor(mask_s[:], mask[:, 0, :], mask[:, 1, :], ALU.add).then_inc(S["msum"], 1)

                def places(n):
                    dve.wait_ge(S["pref"], n + 1)
                    dve.tensor_tensor(place[:], run[:], pre_p[:, 0:NE], ALU.add).then_inc(S["place"], 1)
                    dve.wait_ge(S["place"], n + 1)
                    dve.tensor_tensor(run[:], run[:], pre_p[:, NE:2 * NE], ALU.add).then_inc(S["run"], 1)
                    dve.tensor_tensor(prod[:], mask[:], place[:].unsqueeze(1).to_broadcast([P, 2, NE]),
                                      ALU.mult).then_inc(S["prod"], 1)
                    dve.wait_ge(S["prod"], n + 1)
                    pf = posf[:, n, :] if isinstance(n, int) else posf[:, bass.ds(n, 1), :].rearrange("p a j -> p (a j)")
                    dve.tensor_reduce(out=pf, in_=prod[:], axis=AX.X, op=ALU.add).then_inc(S["pos"], 1)
                    dve.wait_ge(S["pos"], n + 1)
                    alone(dve, S["scat"], n * 32)
                    dve.tensor_copy(pos_now[:], pf).then_inc(S["posi"], 1)

                hooks = {4: [(agg_lo, 1)], 12: [(self_lo, 0)]}
                if l == 0:
                    hooks[1] = [(degree, 1)]
                else:
                    hooks.update({10: [(residual, 1)], 12: [(self_lo, 0), (scales, 1)], 2: [(top_two, 2)],
                                  6: [(places, 2)]})
                layer(dve, select, hooks, opening=tile_iota)

            kc = [0]

            def cstep(ins):
                kc[0] += 1
                ins.then_inc(s_cnt, 1)
                dve.wait_ge(s_cnt, kc[0])

            dve.wait_ge(L[1]["posi"], NT)
            dve.wait_ge(L[1]["run"], NT)
            cstep(dve.tensor_tensor(gate_d[:], top2[:, 1, :], top2[:, 0, :], ALU.subtract))
            cstep(dve.tensor_copy(tab_rows[:], run[0:1, :]))
            cstep(dve.tensor_tensor(nrow[:], run[:], ebase[:], ALU.subtract))
            cstep(dve.tensor_tensor(ti_c[:], ti[:], nrow[:].unsqueeze(2).to_broadcast([P, NE, NT]), ALU.is_lt))
            cstep(dve.tensor_reduce(out=ntile[:], in_=ti_c[:], axis=AX.X, op=ALU.add))
            cstep(dve.memset(tcum[:], 0.0))
            for e in range(NE):
                cstep(dve.tensor_tensor(tcum[:, e + 1:e + 2], tcum[:, e:e + 1], ntile[0:1, e:e + 1], ALU.add))
            cstep(dve.tensor_copy(tab_tiles[:], tcum[:]))
            cstep(dve.tensor_scalar(tab_end[:, 0:1], tcum[:, NE:NE + 1], -2.0, None, ALU.add))
            cstep(dve.tensor_scalar(tab_end[:, 1:2], tcum[:, NE:NE + 1], -1.0, float(YT), ALU.mult, ALU.add))
            cstep(dve.tensor_scalar(shift[:], ntile[:], float(P), float(REGION), ALU.mult, ALU.subtract))
            over_q = lambda a: a.unsqueeze(1).to_broadcast([1, TQ, NE])
            cstep(dve.tensor_tensor(t_cmp, tq[:].unsqueeze(2).to_broadcast([1, TQ, NE]), over_q(tcum[:, 1:NE + 1]),
                                    ALU.is_ge))
            cstep(dve.tensor_reduce(out=t_e[:], in_=t_cmp, axis=AX.X, op=ALU.add))
            cstep(dve.tensor_scalar(tab_set[:], t_e[:], 3.0, None, ALU.add))
            cstep(dve.tensor_tensor(t_val, t_cmp, over_q(sign[:]), ALU.mult))
            cstep(dve.tensor_reduce(out=t_row[:], in_=t_val, axis=AX.X, op=ALU.add))
            cstep(dve.tensor_copy(tab_par[:], t_row[:]))
            cstep(dve.tensor_tensor(t_val, t_cmp, over_q(shift[0:1, :]), ALU.mult))
            cstep(dve.tensor_reduce(out=t_row[:], in_=t_val, axis=AX.X, op=ALU.add))
            cstep(dve.scalar_tensor_tensor(out=t_row[:], in0=tq[:], scalar=float(P), in1=t_row[:], op0=ALU.mult,
                                           op1=ALU.subtract))
            cstep(dve.scalar_tensor_tensor(out=tab_row[:], in0=t_e[:], scalar=float(NE), in1=t_row[:], op0=ALU.is_lt,
                                           op1=ALU.mult))
            assert kc[0] == CNT_DONE
            for i, ins in enumerate((
                    lambda: dve.tensor_tensor(
                        pos_c[:], posf[:].rearrange("p n j -> p (n j)").unsqueeze(2).to_broadcast([P, 2 * NT, NE - 1]),
                        ebase[:, 1:NE].unsqueeze(1).to_broadcast([P, 2 * NT, NE - 1]), ALU.is_ge),
                    lambda: dve.tensor_tensor(
                        pos_c[:], pos_c[:], shift[:, 0:NE - 1].unsqueeze(1).to_broadcast([P, 2 * NT, NE - 1]),
                        ALU.mult),
                    lambda: dve.tensor_reduce(out=pos_s[:], in_=pos_c[:], axis=AX.X, op=ALU.add),
                    lambda: dve.tensor_tensor(posi[:].rearrange("p n j -> p (n j)"), pos_s[:],
                                              posf[:].rearrange("p n j -> p (n j)"), ALU.add))):
                ins().then_inc(s_place, 1)
                dve.wait_ge(s_place, i + 1)

            def x_lo(q):
                dve.wait_ge(M["xHi"], q + 1)
                dve.tensor_tensor(m_xT[:, 1].rearrange("p k n -> p (k n)"), mxT_p,
                                  m_xT[:, 0].rearrange("p k n -> p (k n)").bitcast(F32),
                                  ALU.subtract).then_inc(M["xLo"], 1)

            def h_lo(q):
                dve.wait_ge(M["hHi"], q + 1)
                dve.tensor_tensor(m_hT[:, 1].rearrange("p k n -> p (k n)"), mhT_p,
                                  m_hT[:, 0].rearrange("p k n -> p (k n)").bitcast(F32),
                                  ALU.subtract).then_inc(M["hLo"], 1)

            def m_stats(q):
                dve.wait_ge(M["y"], q + 2)
                dve.bn_stats(m_bst[:], my_p).then_inc(M["bst"], 1)
                alone(dve, M["bst"], q + 1)
                dve.bn_aggr(m_mv[:], m_bst[:]).then_inc(M["mv"], 1)

            def m_scales(q):
                dve.wait_ge(M["std"], q + 1)
                dve.reciprocal(m_r[:], m_std[:]).then_inc(M["r"], 1)
                dve.wait_ge(M["r"], q + 1)
                dve.scalar_tensor_tensor(out=m_b[:], in0=m_mv[:, 0:1], scalar=-1.0, in1=m_r[:],
                                         op0=ALU.mult, op1=ALU.mult).then_inc(M["b"], 1)

            def m_affine(q, par, sets):
                alone(dve, s_wset, sets)
                at = lambda t: t[:, bass.ds(par, 1), :].rearrange("p a d -> p (a d)")
                dve.wait_ge(M["norm"], q + 1)
                dve.tensor_tensor(m_ng[:], m_n[:], at(gam), ALU.mult).then_inc(M["gam"], 1)
                dve.wait_ge(M["gam"], q + 1)
                dve.wait_ge(M["store"], q * 16)
                dve.tensor_tensor(m_y[:], m_ng[:], at(bet), ALU.add).then_inc(M["out"], 1)

            def of_tile(eng, table, q, top):
                return value(eng, table[0:1, q:q + 1] if isinstance(q, int) else table[0:1, bass.ds(q, 1)], top)

            dve.sem_inc(M["out"], 1)
            qT = all_tiles(dve)
            x_lo(0)

            def tile_m(q):
                if not isinstance(q, int) or q >= 2:
                    par = of_tile(dve, tab_par, q - 2, 1)
                    sets = of_tile(dve, tab_set, q - 2, NE + 3)
                    m_stats(q - 2)
                if not isinstance(q, int) or q >= 1:
                    h_lo(q - 1)
                if not isinstance(q, int) or q >= 2:
                    m_scales(q - 2)
                    m_affine(q - 2, par, sets)
                x_lo(q + 1)

            for q in range(3):
                tile_m(q)
            with dve.Fori(3, qT) as q:
                tile_m(q)
            qe = last_but_one(dve)
            for i in range(2):
                q = qe + i
                par = of_tile(dve, tab_par, q, 1)
                sets = of_tile(dve, tab_set, q, NE + 3)
                m_stats(q)
                if i == 0:
                    h_lo(qe + 1)
                m_scales(q)
                m_affine(q, par, sets)

            dve.wait_ge(s_gexp, 1)
            dve.tensor_scalar(gate_d[:], gate_e[:], 1.0, None, ALU.add).then_inc(s_gate, 1)
            dve.wait_ge(s_gate, 1)
            dve.reciprocal(gate[:, 0, :], gate_d[:]).then_inc(s_gate, 1)
            dve.wait_ge(s_gate, 2)
            dve.tensor_tensor(gate[:, 1, :], gate_e[:], gate[:, 0, :], ALU.mult).then_inc(s_gate, 1)
            dve.wait_ge(s_gate, 3)

            def combine(a):
                for j in range(CB):
                    n = a * CB + j
                    w = [gate[:, i, n:n + 1] if isinstance(n, int) else gate[:, i, bass.ds(n, 1)] for i in range(2)]
                    dve.wait_ge(s_cy[j], 32 * a + 32)
                    dve.wait_ge(s_cx[j], 16 * a + 16)
                    if not (isinstance(a, int) and a == 0):
                        dve.wait_ge(s_out, 16 * (n - CB + 1))
                    dve.scalar_tensor_tensor(out=c_t[:, j, :], in0=c_y[:, j, 0, :], scalar=w[0],
                                             in1=c_x[:, j, :], op0=ALU.mult, op1=ALU.add).then_inc(s_ct, 1)
                    dve.wait_ge(s_ct, n + 1)
                    dve.scalar_tensor_tensor(out=c_t[:, j, :], in0=c_y[:, j, 1, :], scalar=w[1],
                                             in1=c_t[:, j, :], op0=ALU.mult, op1=ALU.add).then_inc(s_cacc, 1)

            combine(0)
            with dve.Fori(1, NT // CB) as a:
                combine(a)

        @block.tensor
        def _(pe):
            pe.wait_ge(s_const, CONST)
            pe.wait_ge(s_tab, 11)
            pe.transpose(ps[0:NT, 4, 0:EP], first_c[:], ident[0:EP, 0:EP])
            pe.transpose(ps[0:NT, 4, P:P + EP], end_c[:], ident[0:EP, 0:EP]).then_inc(s_tabT, 1)
            for j in range(2):
                for b in range(EB):
                    i = pe.transpose(ps[:, 2 * j + b // 4, (b % 4) * EP:(b % 4 + 1) * EP], ed_f[:, j, b, :],
                                     ident[0:EP, 0:EP])
            i.then_inc(s_tabT, 1)
            pe.wait_ge(s_tab, 17)
            pe.matmul(ps[0:1, 5, 0:NT + 1], n_g2[:, 0:1], upper[0:NT, 0:NT + 1], start=True, stop=True)
            pe.matmul(ps[0:1, 5, P:P + NT], first_g[:, 0:1], ident[0:NT, 0:NT], start=True, stop=True) \
                .then_inc(s_tabT, 1)

            def product(out_ap, w, lhs, chunks, stop):
                for k in chunks:
                    for a, b in ((0, 0), (1, 0), (0, 1)):
                        i = pe.matmul(out_ap, lhs[:, a, k, :], w[:, b, k, :], start=False,
                                      stop=stop and k == chunks[-1] and (a, b) == (0, 1))
                return i

            pe.wait_ge(s_tab, TAB_DONE)
            for l in range(2):
                S = L[l]
                pe.sem_inc(S["seg"], G)

                def opening(g, c0):
                    pe.wait_ge(S["evac"], g)
                    pe.matmul(agg_p, zero2[:], zero_row[:], start=True, stop=False)
                    if l == 0:
                        pe.matmul(deg_p[:, 0:2], zero2[:], zero_row[:, 0:2], start=True, stop=False)

                def sums(g, c, t, hooks):
                    for k in range(G):
                        run_hooks(hooks, k)
                        pe.wait_ge(S["lo"], c * G + (k + 1 + G))
                        if l == 0:
                            pe.matmul(deg_p[:, 0:2], sel[:, k, :], ones_col[:], start=False, stop=False)
                        pe.matmul(agg_p, sel[:, k, :], r_hi[:, k, :], start=False, stop=False)
                        pe.matmul(agg_p, sel[:, k, :], r_lo[:, k, :], start=False, stop=False).then_inc(S["seg"], 1)
                    run_hooks(hooks, G)

                def closing(g):
                    if l == 0:
                        pe.matmul(deg_p[:, 0:2], zero2[:], zero_row[:, 0:2], start=False, stop=True)
                    pe.matmul(agg_p, zero2[:], zero_row[:], start=False, stop=True).then_inc(S["node"], 1)

                def self_t_t(n):
                    pe.wait_ge(S["self"], n * 16 + 16)
                    pe.wait_ge(S["selfLo"], n)
                    for k in range(KC):
                        i = pe.transpose(sT_p[:, k * P:(k + 1) * P], self_t[:, k * P:(k + 1) * P], ident[:])
                    i.then_inc(S["selfT"], 1)

                def agg_t(n):
                    pe.wait_ge(S["evac"], n + 1)
                    pe.wait_ge(S["aggLo"], n)
                    for k in range(KC):
                        i = pe.transpose(aT_p[:, k * P:(k + 1) * P], agg_s[:, k * P:(k + 1) * P], ident[:])
                    i.then_inc(S["aggT"], 1)

                def dense(k):
                    def step(n):
                        if k == 0:
                            pe.wait_ge(S["res"], n)
                            pe.wait_ge(s_wset, l + 1)
                            pe.matmul(dense_p, one2[:], bias[l][:, 0, :], start=True, stop=False)
                            pe.wait_ge(S["selfLo"], n + 1)
                        if k == KC:
                            pe.wait_ge(S["aggLo"], n + 1)
                        i = product(dense_p, wts[l][:, 1 - k // KC], sT if k < KC else aT, (k % KC,), k == 2 * KC - 1)
                        if k == KC - 1:
                            i.then_inc(S["selfUsed"], 1)
                        if k == 2 * KC - 1:
                            i.then_inc(S["dense"], 1)
                    return step

                def xT_t(n):
                    pe.wait_ge(S["xn2"], n + 1)
                    pe.wait_ge(S["xTc"], n)
                    for k in range(KC):
                        i = pe.transpose(xT_p[:, k * P:(k + 1) * P], xn2_t[:, k * P:(k + 1) * P], ident[:])
                    i.then_inc(S["xT"], 1)

                def logits(n):
                    pe.wait_ge(S["xTc"], n + 1)
                    pe.wait_ge(s_wg, 16)
                    pe.wait_ge(S["lg"], n)
                    for k in range(KC):
                        i = pe.matmul(lg_p[:, 0:NE], xT[:, k, :], wg_s[:, k, :], start=k == 0, stop=k == KC - 1)
                    i.then_inc(S["logit"], 1)

                def prefix(n):
                    pe.wait_ge(S["msum"], n + 1)
                    pe.wait_ge(S["run"], n)
                    pe.matmul(pre_p[:, 0:NE], upper[:], mask_s[:], start=True, stop=True)
                    pe.matmul(pre_p[:, NE:2 * NE], onesq[:], mask_s[:], start=True, stop=True).then_inc(S["pref"], 1)

                hooks = {k + 1: [(dense(k), 1)] for k in range(2 * KC)}
                hooks[0] = [(agg_t, 1)]
                hooks[9] = [(self_t_t, 0)]
                if l == 1:
                    hooks[3].append((prefix, 2))
                    hooks.update({14: [(xT_t, 1)], 17: [(logits, 1)]})
                layer(pe, sums, hooks, opening=opening, tail=closing)

            def x_t_m(q):
                pe.wait_ge(M["x"], q * 16 + 16)
                pe.wait_ge(M["xLo"], q)
                for k in range(KC):
                    i = pe.transpose(mxT_p[:, k * P:(k + 1) * P], m_x[:, k * P:(k + 1) * P], ident[:])
                i.then_inc(M["xT"], 1)

            def mm1(q, w):
                pe.wait_ge(M["relu"], q)
                pe.matmul(mh_p, one2[:], w[1][:, 0, :], start=True, stop=False)
                pe.wait_ge(M["xLo"], q + 1)
                product(mh_p, w[0][:, 0], m_xT, range(KC), True).then_inc(M["h"], 1)

            def h_t_m(q):
                pe.wait_ge(M["relu"], q + 1)
                pe.wait_ge(M["hLo"], q)
                for k in range(KC):
                    i = pe.transpose(mhT_p[:, k * P:(k + 1) * P], m_h[:, k * P:(k + 1) * P], ident[:])
                i.then_inc(M["hT"], 1)

            def mm2(q, w):
                pe.wait_ge(M["norm"], q)
                pe.matmul(my_p, one2[:], w[1][:, 1, :], start=True, stop=False)
                pe.wait_ge(M["hLo"], q + 1)
                product(my_p, w[0][:, 1], m_hT, range(KC), True).then_inc(M["y"], 1)

            def of_tile(table, q, top):
                return value(pe, table[0:1, q:q + 1] if isinstance(q, int) else table[0:1, bass.ds(q, 1)], top)

            def weights_of(q):
                par = of_tile(tab_par, q, 1)
                return wts_all[:, bass.ds(par * 2, 2)], bias_all[:, bass.ds(par * 2, 2)]

            pe.wait_ge(s_cnt, CNT_DONE)
            pe.sem_inc(M["y"], 1)
            qT = all_tiles(pe)
            x_t_m(0)

            def tile_m(q):
                sets, w = of_tile(tab_set, q, NE + 3), weights_of(q)
                if not isinstance(q, int) or q >= 1:
                    w_before = weights_of(q - 1)
                    h_t_m(q - 1)
                pe.wait_ge(s_wset, sets)
                mm1(q, w)
                x_t_m(q + 1)
                if not isinstance(q, int) or q >= 1:
                    mm2(q - 1, w_before)

            for q in range(2):
                tile_m(q)
            with pe.Fori(2, qT) as q:
                tile_m(q)
            ql = last_but_one(pe) + 1
            w = weights_of(ql)
            h_t_m(ql)
            mm2(ql, w)


_INS = ['x', 'src', 'dst', 'L0_gnn_W_self1', 'L0_gnn_W_neigh1', 'L0_gnn_b1', 'L0_gnn_W_self2', 'L0_gnn_W_neigh2',
        'L0_gnn_b2', 'L0_ffn_Wg', 'L0_ffn_W1', 'L0_ffn_b1', 'L0_ffn_W2', 'L0_ffn_b2', 'L0_ffn_gamma', 'L0_ffn_beta']


def kernel(**inputs):
    import concourse.bacc as bacc
    from concourse.bass_utils import run_bass_kernel_spmd

    nc = bacc.Bacc("TRN2", target_bir_lowering=False, num_devices=1)
    arrays, args = {}, []
    for name in _INS:
        a = np.ascontiguousarray(inputs[name])
        arrays[f"in_{name}"] = a
        args.append(nc.dram_tensor(f"in_{name}", a.shape, mybir.dt.from_np(a.dtype), kind="ExternalInput").ap())
    args.append(nc.dram_tensor("out_0", (N, D), F32, kind="ExternalOutput").ap())
    build(nc, *args)
    r = run_bass_kernel_spmd(nc, [arrays], core_ids=[0])
    return r.results[0]["out_0"]
```

```python
from contextlib import ExitStack

import numpy as np

import concourse.bass as bass
from concourse import mybir

F32 = mybir.dt.float32
F32R = mybir.dt.float32r
I32 = mybir.dt.int32
U32 = mybir.dt.uint32
ALU = mybir.AluOpType
ACT = mybir.ActivationFunctionType
AX = mybir.AxisListType

P = 128
N, D, E = 6250, 512, 100000
NE = 8
KC = D // P
NT = -(-N // P)
LAST = N - P
EPS = 1e-5

PACK = 1024
ST = 17
RING = 6
EB, EP = 7, 112
ET = EB * EP
ETP = ET + ST
FAR = 1.0e6
CHUNKS = {0: 6, 6: 6, 12: 5}
SELW = 3

LN_ROWS = 4
LN_CH = -(-N // (P * LN_ROWS))
LN_BUF = 4
LN_LEFT = N - (LN_CH - 1) * P * LN_ROWS
assert 0 < LN_LEFT <= P

WSPLIT_AT = 6
REGION = (NT + 1) * P
YT = 2 * NT + NE + 1
TQ = YT + 1
CB = 7
PRE = 3


def start_of(g):
    return min(g * P, LAST)


def build(nc, x, src, dst, w_self1, w_neigh1, b1, w_self2, w_neigh2, b2, Wg, W1, eb1, W2, eb2, gamma, beta, out):
    xn_d = nc.dram_tensor("xn_scratch", (N, D), F32, kind="Internal").ap()
    h1_d = nc.dram_tensor("h1_scratch", (N, D), F32, kind="Internal").ap()
    x2_d = nc.dram_tensor("x2_scratch", (N, D), F32, kind="Internal").ap()
    disp_d = nc.dram_tensor("dispatch_scratch", (NE * REGION, D), F32, kind="Internal").ap()
    y_d = nc.dram_tensor("expert_out_scratch", (YT * P, D), F32, kind="Internal").ap()

    with ExitStack() as ctx:
        def sem(name):
            return ctx.enter_context(nc.semaphore(name))

        def sbc(c, name, shape, dt=F32):
            return c.enter_context(nc.sbuf_tensor(name, shape, dt))

        def sb(name, shape, dt=F32):
            return sbc(ctx, name, shape, dt)

        ident = sb("ident", [P, P])
        upper = sb("upper", [P, P])
        row0 = sb("row0", [P, P])
        onesq = sb("onesq", [P, P])
        iota = sb("iota", [P, P])
        srcT = sb("srcT", [P, ETP], I32)
        dstT = sb("dstT", [P, ETP])
        start_col = sb("start_col", [P, NT + 1])
        iota_g = sb("iota_g", [P, 2, P])
        rdeg = sb("rdeg", [P, NT])
        zero2 = sb("zero2", [2, P], F32R)
        zero_row = sb("zero_row", [2, D], F32R)
        one2 = sb("one2", [2, P], F32R)
        ones_col = sb("ones_col", [P, 2], F32R)
        eps_col = sb("eps_col", [P, 1])
        rsel = sb("rsel", [2, 2])
        rseli = sb("rseli", [2, 2], I32)
        tab_tile = sb("tab_tile", [1, NT], I32)
        tab_next = sb("tab_next", [1, NT + 1], I32)
        tab_extra = sb("tab_extra", [1, NT + 1], I32)
        tab_tiles = sb("tab_tiles", [1, NE + 1], I32)
        tab_end = sb("tab_end", [1, 2], I32)
        tab_row = sb("tab_row", [1, TQ], I32)
        tab_use = sb("tab_use", [1, TQ], I32)
        tab_rows = sb("tab_rows", [1, NE], I32)
        wts_all = sb("wts", [P, 4, 2, KC, D], F32R)
        wts = [wts_all[:, 2 * i:2 * i + 2] for i in range(2)]
        w_raw = sb("w_raw", [P, 2, KC, D])
        bias_raw = sb("bias_raw", [2, 2, D])
        bias_t = sb("bias_t", [2, D])
        bias_u = sb("bias_u", [2, D])
        bias_all = sb("bias", [2, 4, D], F32R)
        bias = [bias_all[:, 2 * i:2 * i + 2] for i in range(2)]
        wg_s = sb("wg_s", [P, KC, NE])
        top2 = sb("top2", [P, 2, NT])
        posf = sb("posf", [P, NT, 2])
        posi = sb("posi", [P, NT, 2], I32)
        gate = sb("gate", [P, 2, NT])
        gate_e = sb("gate_e", [P, NT])
        gate_d = sb("gate_d", [P, NT])
        run = sb("run", [P, NE])

        with ExitStack() as c1:
            ln_in = [sbc(c1, f"ln_in{i}", [P, LN_ROWS, D]) for i in range(LN_BUF)]
            ln_out = [sbc(c1, f"ln_out{i}", [P, LN_ROWS, D]) for i in range(LN_BUF)]
            ln_bst = [sbc(c1, f"ln_bst{i}", [P, LN_ROWS, 6]) for i in range(2)]
            ln_mv = [sbc(c1, f"ln_mv{i}", [P, LN_ROWS, 2]) for i in range(2)]
            ln_std = [sbc(c1, f"ln_std{i}", [P, LN_ROWS]) for i in range(2)]
            ln_r = [sbc(c1, f"ln_r{i}", [P, LN_ROWS]) for i in range(2)]
            ln_b = [sbc(c1, f"ln_b{i}", [P, LN_ROWS]) for i in range(2)]
            ed_i = sbc(c1, "ed_i", [EP, 2, EB, P], I32)
            ed_f = sbc(c1, "ed_f", [EP, 2, EB, P])
            t_max = sbc(c1, "t_max", [EP, EB])
            t_min = sbc(c1, "t_min", [EP, EB])
            tid_i = sbc(c1, "tid_i", [EP, EB], I32)
            tid = sbc(c1, "tid", [EP, EB])
            thr_i = sbc(c1, "thr_i", [P, NT], I32)
            thr = sbc(c1, "thr", [P, NT])
            thr_hi = sbc(c1, "thr_hi", [P, NT])
            iota_i = sbc(c1, "iota_i", [P, P], I32)
            cmp_m = sbc(c1, "cmp_m", [EP, NT, EB])
            cmp_v = sbc(c1, "cmp_v", [EP, NT, EB])
            first_c = sbc(c1, "first_c", [EP, NT])
            end_c = sbc(c1, "end_c", [EP, NT])
            first_g = sbc(c1, "first_g", [NT, 1])
            end_g = sbc(c1, "end_g", [NT, 1])
            span_g = sbc(c1, "span_g", [NT, 1])
            n_g2 = sbc(c1, "n_g2", [NT, 1])
            f_row = sbc(c1, "f_row", [1, NT])
            n_row = sbc(c1, "n_row", [1, NT + 1])

        with ExitStack() as c2:
            rows = sbc(c2, "rows", [P, ST + 1, D])
            r_hi = sbc(c2, "r_hi", [P, RING, D], F32R)
            r_lo = sbc(c2, "r_lo", [P, RING, D], F32R)
            sel = sbc(c2, "sel", [P, RING, P], F32R)
            idx = sbc(c2, "idx", [P, ST + 1], I32)
            agg_s = sbc(c2, "agg_s", [P, D])
            self_t = sbc(c2, "self_t", [P, D])
            aT = sbc(c2, "aT", [P, 2, KC, P], F32R)
            sT = sbc(c2, "sT", [P, 2, KC, P], F32R)
            x_t = sbc(c2, "x_t", [P, D])
            x2_t = sbc(c2, "x2_t", [P, D])
            h_t = x2_t
            xn2_t = sbc(c2, "xn2_t", [P, D])
            xn2_s = sbc(c2, "xn2_s", [P, D])
            xT = sbc(c2, "xT", [P, KC, P])
            deg_m = sbc(c2, "deg_m", [P, 1])
            bst = sbc(c2, "bst", [P, 6])
            mv = sbc(c2, "mv", [P, 2])
            std = sbc(c2, "std", [P, 1])
            rstd = sbc(c2, "rstd", [P, 1])
            nmr = sbc(c2, "nmr", [P, 1])
            lg = sbc(c2, "lg", [P, NE])
            mx8 = sbc(c2, "mx8", [P, NE])
            ix8 = sbc(c2, "ix8", [P, NE], U32)
            e01 = sbc(c2, "e01", [P, 2])
            mask = sbc(c2, "mask", [P, 2, NE])
            prod = sbc(c2, "prod", [P, 2, NE])
            pos_now = sbc(c2, "pos_now", [P, 2], I32)
            nrow = sbc(c2, "nrow", [P, NE])
            ti_i = sbc(c2, "ti_i", [P, NE, NT], I32)
            ti = sbc(c2, "ti", [P, NE, NT])
            ntile = sbc(c2, "ntile", [P, NE])
            shift = sbc(c2, "shift", [P, NE])
            pos_c = sbc(c2, "pos_c", [P, 2 * NT, NE - 1])
            pos_s = sbc(c2, "pos_s", [P, 2 * NT])
            tcum = sbc(c2, "tcum", [1, NE + 1])
            tq_i = sbc(c2, "tq_i", [1, TQ], I32)
            tq = sbc(c2, "tq", [1, TQ])
            ti_c = rows[:, 4, 0:NE * NT].rearrange("p (e t) -> p e t", e=NE)
            t_cmp, t_val = (rows[0:1, i:i + 2, :].rearrange("p a d -> p (a d)")[:, 0:TQ * NE]
                            .rearrange("p (q e) -> p q e", e=NE) for i in (0, 2))
            t_e = sbc(c2, "t_e", [1, TQ])
            t_row = sbc(c2, "t_row", [1, TQ])
            ebase_i = sbc(c2, "ebase_i", [P, NE], I32)
            ebase = sbc(c2, "ebase", [P, NE])
            zrow = r_hi[:, 0, :].bitcast(F32)

        with ExitStack() as c3:
            m_x = sbc(c3, "m_x", [P, D])
            m_xT = sbc(c3, "m_xT", [P, 2, KC, P], F32R)
            m_h = sbc(c3, "m_h", [P, D])
            m_hT = sbc(c3, "m_hT", [P, 2, KC, P], F32R)
            m_n = sbc(c3, "m_n", [P, D])
            m_ng = sbc(c3, "m_ng", [P, D])
            m_y = sbc(c3, "m_y", [P, D])
            m_bst = sbc(c3, "m_bst", [P, 6])
            m_mv = sbc(c3, "m_mv", [P, 2])
            m_std = sbc(c3, "m_std", [P, 1])
            m_r = sbc(c3, "m_r", [P, 1])
            m_b = sbc(c3, "m_b", [P, 1])
            gam = sbc(c3, "gam", [P, 2, D])
            bet = sbc(c3, "bet", [P, 2, D])

        with ExitStack() as c4:
            c_y = sbc(c4, "c_y", [P, CB, 2, D])
            c_t = sbc(c4, "c_t", [P, CB, D])
            c_idx = sbc(c4, "c_idx", [P, CB, 2], I32)
            c_x = sbc(c4, "c_x", [P, CB * PRE, D])

        ps = ctx.enter_context(nc.psum_tensor("ps", [P, 8, 512], F32))
        aT_p, sT_p, dense_p, xT_p = (ps[:, i, :] for i in range(2, 6))
        lg_p, pre_p = ps[:, 6, 0:NE], ps[:, 7, 0:2 * NE]

        def agg_of(g):
            return ps[:, g % 2, :] if isinstance(g, int) else \
                ps[:, bass.ds(g % 2, 1), :].rearrange("p a d -> p (a d)")

        def deg_of(g):
            return ps[:, 6 + g % 2, 0:2] if isinstance(g, int) else \
                ps[:, bass.ds(g % 2 + 6, 1), 0:2].rearrange("p a d -> p (a d)")

        mxT_p, mh_p, mhT_p, my_p = (ps[:, i, :] for i in range(4))

        s_const = sem("s_const")
        s_constv = sem("s_constv")
        s_ln_in = [sem(f"s_ln_in{i}") for i in range(LN_BUF)]
        s_ln_st = sem("s_ln_st")
        s_ln_mv = sem("s_ln_mv")
        s_ln_std = sem("s_ln_std")
        s_ln_r = sem("s_ln_r")
        s_ln_b = sem("s_ln_b")
        s_ln_out = sem("s_ln_out")
        s_xn = [sem(f"s_xn{i}") for i in range(LN_BUF)]
        s_pad = sem("s_pad")
        s_edges = sem("s_edges")
        s_tab = sem("s_tab")
        s_tabT = sem("s_tabT")
        s_raw = sem("s_raw")
        s_brow = sem("s_brow")
        s_raw_p = sem("s_raw_p")
        s_brow_p = sem("s_brow_p")
        s_split = sem("s_split")
        s_wset = sem("s_wset")
        s_wg = sem("s_wg")
        s_whi = sem("s_whi")
        s_wlo = sem("s_wlo")
        s_bstep = sem("s_bstep")
        s_bset = sem("s_bset")
        s_passed = sem("s_passed")
        s_const2 = sem("s_const2")
        s_cv2 = sem("s_cv2")
        s_gate = sem("s_gate")
        s_place = sem("s_place")
        s_yzero = sem("s_yzero")

        names = ("iota idx idxx hi lo seg hix lox segx node rdeg0 rdeg evac aggT aggHi aggLo self selfT selfHi "
                 "selfLo selfUsed dense res store xt bst mv std rstd nmr xn2 xns xT xTc logit lg mx ix e01 mask pref "
                 "run prod pos posi scat").split()
        L = [{n: sem(f"s{l + 1}_{n}") for n in names if (n[:4] != "rdeg" if l else n not in
              ("xt bst mv std rstd nmr xn2 xns xT xTc logit lg mx ix e01 mask pref run prod pos "
               "posi scat").split())} for l in range(2)]
        s_rows = [sem(f"s_rows{k}") for k in range(ST)]
        L_rows = [s_rows + [sem(f"s{l + 1}_rows_loop")] for l in range(2)]

        s_cnt = sem("s_cnt")
        s_gexp = sem("s_gexp")
        s_zero = sem("s_zero")
        M = {n: sem(f"m_{n}") for n in ("x xT xHi xLo h relu hT hHi hLo y bst mv std r b norm gam out "
                                        "store aff").split()}
        s_cidx = sem("s_cidx")
        s_cy, CY0 = s_rows[0:CB], 2 * NT * 16
        s_cx = sem("s_cx")
        s_cx2 = sem("s_cx2")
        s_ct = sem("s_ct")
        s_cacc = sem("s_cacc")
        s_out = (s_ln_in + s_xn)[0:CB]
        OUT0 = [16 * len(range(i % LN_BUF, LN_CH, LN_BUF)) for i in range(CB)]

        CONST, CONSTV = 18, 11
        TAB_DONE = 26
        CNT_DONE = 27

        block = ctx.enter_context(nc.Block())

        def value(eng, cell, top):
            return eng.value_load(cell, min_val=0, max_val=top)

        def all_tiles(eng):
            return eng.value_load(tab_tiles[0:1, NE:NE + 1], min_val=2 * NT, max_val=YT - 1)

        def last_but_one(eng):
            return eng.value_load(tab_end[0:1, 0:1], min_val=2 * NT - 2, max_val=YT - 3)

        def weights_hi(act, n, par):
            act.wait_ge(s_raw, n * 32 + 32)
            for m in range(2):
                act.activation(wts[par][:, m, 0], w_raw[:, m], ACT.Copy).then_inc(s_whi, 1)

        def weights_lo(dve, n, par):
            for m in range(2):
                dve.wait_ge(s_whi, n * 2 + m + 1)
                dve.tensor_tensor(wts[par][:, m, 1], w_raw[:, m], wts[par][:, m, 0].bitcast(F32),
                                  ALU.subtract).then_inc(s_wlo, 1)

        def ln_part(t, c):
            return t[:] if c < LN_CH - 1 else t[0:LN_LEFT, 0:1]

        def ln_rows(c):
            return range(LN_ROWS if c < LN_CH - 1 else 1)

        def all_xn(eng):
            for i in range(LN_BUF):
                eng.wait_ge(s_xn[i], 16 * len(range(i, LN_CH, LN_BUF)))

        def biases(dve, n, par):
            dve.wait_ge(s_brow, n * 32 + 32)
            for m in range(2):
                at = n * 8 + m * 4
                dve.tensor_copy(bias[par][:, m, :], bias_raw[:, m, :]).then_inc(s_bstep, 1)
                dve.wait_ge(s_bstep, at + 1)
                dve.tensor_scalar(bias_t[:], bias[par][:, m, :].bitcast(F32), rsel[:, 1:2], None,
                                  ALU.mult).then_inc(s_bstep, 1)
                dve.tensor_scalar(bias_u[:], bias_raw[:, m, :], rsel[:, 0:1], None, ALU.mult).then_inc(s_bstep, 1)
                dve.wait_ge(s_bstep, at + 3)
                dve.tensor_tensor(bias[par][:, m, :], bias_t[:], bias_u[:], ALU.add).then_inc(s_bstep, 1)
            dve.wait_ge(s_bstep, (n + 1) * 8)
            dve.sem_inc(s_wset, 1)

        def alone(eng, semaphore, v):
            eng.wait_ge(semaphore, v)
            eng.sem_inc(s_passed, 1)

        def within(v, top):
            return v if isinstance(v, int) else v.with_bounds(min_val=0, max_val=top)

        def layer(eng, step, hooks, table, opening=None, tail=None, loop_end=None):
            back = max([d for fs in hooks.values() for _, d in fs] + [0])

            def tile(g):
                def cell(t, i):
                    return t[0:1, i:i + 1] if isinstance(g, int) else t[0:1, bass.ds(i, 1)]
                packed = value(eng, cell(table, g if table is tab_tile else g + 1), ET * PACK + ET)
                t0, n = within(packed // PACK, ET), within(packed % PACK, ET)
                if opening:
                    opening(g, t0)
                for k in range(ST + 1):
                    for f, d in hooks.get(k, []):
                        if not isinstance(g, int) or g >= d:
                            f(g - d)
                    if k < ST:
                        step(k, g, None, t0 + k)
                with eng.If_lt(eng.to_reg(0), eng.to_reg(n)):
                    x0 = value(eng, cell(tab_extra, g), NT * ET)
                    x1 = value(eng, cell(tab_extra, g + 1), NT * ET)
                    with eng.Fori(x0, x1) as x:
                        step(ST, g, x, within(t0 + ST + (x - x0), ETP - 1))
                    if loop_end:
                        loop_end(x1)
                if tail:
                    tail(g)

            for g in range(back + 1):
                tile(g)
            with eng.Fori(back + 1, NT) as g:
                tile(g)
            for g in range(NT, NT + back):
                for k in sorted(hooks):
                    for f, d in hooks[k]:
                        if g - d < NT:
                            f(g - d)

        def ring(k):
            return k % RING if k < ST else RING - 1

        def free_at(g, k):
            if k == ST:
                return g * ST + (ST // RING * RING + RING)
            if k >= RING:
                return g * ST + (k + 1)
            return g * ST + (RING + min(k - (ST % RING - 1), 0))

        def rows_at(t, n):
            return t[start_of(n):start_of(n) + P, :] if isinstance(n, int) else t[bass.ds(n * P, P), :]

        @block.sync
        def _(sp):
            def chunk_of(t, c):
                r0 = c * P * LN_ROWS
                return t[r0:r0 + P * LN_ROWS, :].rearrange("(p j) d -> p j d", p=P) if c < LN_CH - 1 else \
                    t[r0:N, :].rearrange("(p j) d -> p j d", j=1)

            def load_chunk(c):
                sp.dma_start(ln_part(ln_in[c % LN_BUF], c), chunk_of(x, c)).then_inc(s_ln_in[c % LN_BUF], 16)

            def store_chunk(c):
                sp.wait_ge(s_ln_out, c + 1)
                sp.dma_start(chunk_of(xn_d, c), ln_part(ln_out[c % LN_BUF], c)).then_inc(s_xn[c % LN_BUF], 16)

            def load_set(n, wa, wb, ba, bb):
                if not (isinstance(n, int) and n == 0):
                    sp.wait_ge(s_wset, n)
                sp.dma_start(w_raw[:, 0], wa.rearrange("(k p) n -> p k n", p=P)).then_inc(s_raw, 16)
                sp.dma_start(w_raw[:, 1], wb.rearrange("(k p) n -> p k n", p=P)).then_inc(s_raw, 16)
                for j, b in enumerate((ba, bb)):
                    sp.dma_start(bias_raw[:, j, :], b.to_broadcast([2, D])).then_inc(s_brow, 16)

            load_chunk(0)
            sp.wait_ge(s_pad, 2)
            full = (EB - 1) * EP * P
            tail_rows = (E - full) // P
            for j, lst in enumerate((src, dst)):
                sp.dma_start(ed_i[:, j, 0:EB - 1, :],
                             lst[0:full].rearrange("(b p e) -> p b e", p=EP, e=P)).then_inc(s_edges, 16)
                sp.dma_start(ed_i[0:tail_rows, j, EB - 1, :],
                             lst[full:full + tail_rows * P].rearrange("(p e) -> p e", e=P)).then_inc(s_edges, 16)
                sp.dma_start(ed_i[tail_rows:tail_rows + 1, j, EB - 1, 0:E - full - tail_rows * P],
                             lst[full + tail_rows * P:E].rearrange("(a e) -> a e", a=1)).then_inc(s_edges, 16)
            load_chunk(1)
            load_chunk(2)
            load_chunk(3)
            sp.dma_start(wg_s[:], Wg.rearrange("(k p) e -> p k e", p=P)).then_inc(s_wg, 16)
            brow = lambda b: b.rearrange("(a n) -> a n", a=1)
            for c in range(LN_CH):
                store_chunk(c)
                if c + LN_BUF < LN_CH:
                    load_chunk(c + LN_BUF)
                if c == 2:
                    load_set(0, w_neigh1, w_self1, brow(b1), brow(b1))
            load_set(1, w_neigh2, w_self2, brow(b2), brow(b2))

            for l, own, res_d, res in ((0, xn_d, h1_d, h_t), (1, h1_d, x2_d, x2_t)):
                S = L[l]
                if l == 0:
                    all_xn(sp)
                    load_set(2, W1[0], W2[0], eb1[0:1], eb2[0:1])
                else:
                    sp.wait_ge(L[0]["store"], 16 * NT)

                def load_tile(n):
                    if not (isinstance(n, int) and n == 0):
                        alone(sp, S["selfT"], n)
                        sp.wait_ge(S["self"], n * 16)
                    elif l == 1:
                        sp.wait_ge(L[0]["selfT"], NT)
                    sp.dma_start(self_t[:], rows_at(own, n)).then_inc(S["self"], 16)
                    if l == 1:
                        if not (isinstance(n, int) and n == 0):
                            sp.wait_ge(S["res"], n)
                            sp.wait_ge(S["xt"], n * 16)
                        sp.dma_start(x_t[:], rows_at(x, n)).then_inc(S["xt"], 16)

                def store_tile(n):
                    sp.wait_ge(S["res"], n + 1)
                    if isinstance(n, int):
                        sp.wait_ge(S["store"], 16 * n)
                    sp.dma_start(rows_at(res_d, n), res[:]).then_inc(S["store"], 16)

                load_tile(0)
                with sp.Fori(0, NT - 2) as n:
                    load_tile(n + 1)
                    store_tile(n)
                if l == 1:
                    load_set(3, W1[1], W2[1], eb1[1:2], eb2[1:2])
                load_tile(NT - 1)
                sp.wait_ge(S["res"], NT - 1)
                sp.dma_start(res_d[(NT - 2) * P:(NT - 1) * P, :], res[:]).then_inc(S["store"], 16)
                store_tile(NT - 1)

            sp.wait_ge(L[1]["scat"], 32 * NT)
            sp.wait_ge(s_cnt, 2)
            for e in range(NE):
                r = value(sp, tab_rows[0:1, e:e + 1], (NE - 1) * REGION + NT * P)
                sp.dma_start(disp_d[bass.ds(r, P), :], zrow).then_inc(s_zero, 16)
            sp.wait_ge(s_zero, 16 * NE)
            sp.wait_ge(s_cnt, CNT_DONE)

            def load_x(q):
                row = value(sp, tab_row[0:1, q:q + 1] if isinstance(q, int) else tab_row[0:1, bass.ds(q, 1)],
                            NE * REGION - P)
                if not (isinstance(q, int) and q == 0):
                    sp.wait_ge(M["xT"], q)
                sp.dma_start(m_x[:], disp_d[bass.ds(row, P), :]).then_inc(M["x"], 16)

            def store_y(q):
                alone(sp, M["out"], q + 2)
                sp.dma_start(y_d[q * P:(q + 1) * P, :] if isinstance(q, int) else y_d[bass.ds(q * P, P), :],
                             m_y[:]).then_inc(M["store"], 16)

            qT = all_tiles(sp)
            load_x(0)
            load_x(1)
            load_x(2)
            sp.wait_ge(s_place, 4)
            with sp.Fori(2, CB * PRE + 2) as q:
                load_x(q + 1)
                store_y(q - 2)
                sp.dma_start(c_x[:, bass.ds(q - 2, 1), :].rearrange("p a d -> p (a d)"),
                             rows_at(x2_d, q - 2)).then_inc(s_cx, 16)
            with sp.Fori(CB * PRE + 2, qT) as q:
                load_x(q + 1)
                store_y(q - 2)
            qe = last_but_one(sp)
            store_y(qe)
            store_y(qe + 1)
            alone(sp, M["store"], qT * 16)
            alone(sp, M["xLo"], qT + 1)
            sp.wait_ge(s_wset, NE + 2)

            def combine_loads(a):
                for j in range(CB):
                    n = a * CB + j
                    sp.wait_ge(s_ct, n - CB * PRE + 1)
                    sp.dma_start(c_x[:, n % (CB * PRE), :], rows_at(x2_d, n)).then_inc(s_cx2, 16)

            def combine_stores(a):
                for j in range(CB):
                    n = a * CB + j
                    sp.wait_ge(s_cacc, n + 1)
                    if n == NT - 1:
                        sp.wait_ge(s_out[j - 1], OUT0[j - 1] + 16 * (a + 1))
                    sp.dma_start(rows_at(out, n), c_t[:, j, :]).then_inc(s_out[j], 16)

            for a in range(NT // CB):
                combine_stores(a)
                if a + PRE < NT // CB:
                    if a > 0:
                        sp.wait_ge(s_cx2, 16 * CB * a)
                    combine_loads(a + PRE)
            for j in range(CB):
                sp.wait_ge(s_out[j], OUT0[j] + 16 * (NT // CB))

        @block.gpsimd
        def _(pool):
            k = [0]

            def did(ins, wait=False):
                k[0] += 1
                ins.then_inc(s_const, 1)
                if wait:
                    pool.wait_ge(s_const, k[0])

            pool.memset(ed_i[:, 1, EB - 1, :], int(FAR)).then_inc(s_pad, 1)
            pool.memset(ed_i[:, 0, EB - 1, :], 0).then_inc(s_pad, 1)
            did(pool.iota(iota_i[:], pattern=[[1, P]], base=0, channel_multiplier=0))
            did(pool.iota(thr_i[:], pattern=[[P, NT]], base=0, channel_multiplier=0))
            did(pool.iota(tid_i[:], pattern=[[EP, EB]], base=0, channel_multiplier=1))
            did(pool.iota(rseli[:], pattern=[[1, 2]], base=0, channel_multiplier=1))
            did(pool.memset(eps_col[:], EPS))
            did(pool.memset(zero2[:].bitcast(F32), 0.0))
            did(pool.memset(one2[:].bitcast(F32), 1.0))
            did(pool.memset(ones_col[:].bitcast(F32), 1.0))
            did(pool.memset(onesq[:], 1.0))
            did(pool.memset(row0[:], 0.0), wait=True)
            did(pool.memset(row0[0:1, :], 1.0))
            did(pool.memset(ident[:], 0.0), wait=True)
            did(pool.affine_select(out=ident[:], in_=ident[:], compare_op=ALU.not_equal, fill=1.0, base=0,
                                   pattern=[[-1, P]], channel_multiplier=1))
            did(pool.memset(upper[:], 1.0), wait=True)
            did(pool.affine_select(out=upper[:], in_=upper[:], compare_op=ALU.is_ge, fill=0.0, base=-1,
                                   pattern=[[1, P]], channel_multiplier=-1))
            did(pool.memset(srcT[:, ET:ETP], 0))
            did(pool.memset(dstT[:, ET:ETP], FAR))
            did(pool.memset(zero_row[:].bitcast(F32), 0.0))
            assert k[0] == CONST

            def split_set(n, par):
                alone(pool, s_raw_p, (n - 3) * 32)
                alone(pool, s_brow_p, (n - 3) * 32)
                base = (n - 4) * 10
                for m in range(2):
                    pool.tensor_copy(wts[par][:, m, 0], w_raw[:, m]).then_inc(s_split, 1)
                    alone(pool, s_split, base + (5 * m + 1))
                    pool.tensor_tensor(wts[par][:, m, 1], w_raw[:, m], wts[par][:, m, 0].bitcast(F32),
                                       ALU.subtract).then_inc(s_split, 1)
                    pool.tensor_copy(bias[par][:, m, :], bias_raw[:, m, :]).then_inc(s_split, 1)
                    alone(pool, s_split, base + (5 * m + 3))
                    pool.tensor_scalar(bias_t[:], bias[par][:, m, :].bitcast(F32), rsel[:, 1:2], None,
                                       ALU.mult).then_inc(s_split, 1)
                    pool.tensor_scalar(bias_u[:], bias_raw[:, m, :], rsel[:, 0:1], None,
                                       ALU.mult).then_inc(s_split, 1)
                    alone(pool, s_split, base + (5 * m + 5))
                    pool.tensor_tensor(bias[par][:, m, :], bias_t[:], bias_u[:], ALU.add) \
                        .then_inc(s_wset if m else s_bset, 1)
                    if not m:
                        alone(pool, s_bset, n - 3)

            pool.wait_ge(s_tab, TAB_DONE)
            all_xn(pool)
            pool.iota(ebase_i[:], pattern=[[REGION, NE]], base=0, channel_multiplier=0).then_inc(s_const2, 1)
            pool.iota(ti_i[:], pattern=[[0, NE], [P, NT]], base=0, channel_multiplier=0).then_inc(s_const2, 1)
            pool.iota(tq_i[:], pattern=[[1, TQ]], base=0, channel_multiplier=0).then_inc(s_const2, 1)
            for l, rows_d in ((0, xn_d), (1, h1_d)):
                S = L[l]
                if l == 1:
                    pool.wait_ge(L[0]["store"], 16 * NT)


                def gather(k, g, x, t):
                    if k in CHUNKS:
                        alone(pool, S["lo"], g * ST + (k + CHUNKS[k]))
                        alone(pool, S["idx"], g * len(CHUNKS) + (list(CHUNKS).index(k) + 1))
                    if k == ST:
                        alone(pool, S["lox"], x + 1)
                        pool.tensor_copy(idx[:, k:k + 1], srcT[:, bass.ds(t, 1)]).then_inc(S["idxx"], 1)
                        alone(pool, S["idxx"], x + 1)
                    pool.indirect_dma_start(
                        rows[:, k, :], None, rows_d,
                        bass.IndirectOffsetOnAxis(ap=idx[:, k:k + 1], axis=0)).then_inc(L_rows[l][k], 16)

                def scatter(n):
                    alone(pool, S["posi"], n + 1)
                    alone(pool, S["xns"], n + 1)
                    for j in range(2):
                        pool.indirect_dma_start(
                            disp_d, bass.IndirectOffsetOnAxis(ap=pos_now[:, j:j + 1], axis=0),
                            xn2_s[:], None) \
                            .then_inc(S["scat"], 16)

                layer(pool, gather, {11: [(scatter, 3)]} if l == 1 else {}, tab_tile)

            def load_expert(n, e, par):
                at = (lambda t: t[e:e + 1]) if isinstance(e, int) else (lambda t: t[bass.ds(e, 1)])
                for m, w in enumerate((W1, W2)):
                    pool.dma_start(w_raw[:, m], at(w).rearrange("a (k p) n -> p (a k) n", p=P)).then_inc(s_raw_p, 16)
                for m, b in enumerate((eb1, eb2)):
                    pool.dma_start(bias_raw[:, m, :], at(b).to_broadcast([2, D])).then_inc(s_brow_p, 16)
                affine(e, par)

            def affine(e, par):
                at = (lambda t: t[e:e + 1]) if isinstance(e, int) else (lambda t: t[bass.ds(e, 1)])
                for t, d in ((gam, gamma), (bet, beta)):
                    pool.dma_start(t[:, par], at(d).to_broadcast([P, D])).then_inc(M["aff"], 16)

            pool.wait_ge(s_cnt, CNT_DONE)
            pool.wait_ge(L[1]["evac"], NT)
            pool.wait_ge(L[1]["scat"], 32 * NT)
            affine(0, 0)
            affine(1, 1)
            qT = all_tiles(pool)
            with pool.Fori(qT, YT) as j:
                pool.dma_start(y_d[bass.ds(j * P, P), :], zrow).then_inc(s_yzero, 16)
            rest = pool.value_load(tab_end[0:1, 1:2], min_val=1, max_val=YT - 2 * NT)
            alone(pool, s_yzero, rest * 16)
            pool.wait_ge(s_wset, 4)
            with pool.Fori(1, NE // 2) as e2:
                for par in range(2):
                    e = e2 * 2 + par
                    q = value(pool, tab_tiles[0:1, bass.ds(within(e - 1, NE), 1)], YT - 1)
                    alone(pool, M["y"], q + 1)
                    alone(pool, M["out"], q + 1)
                    load_expert(e + 2, e, par)
                    alone(pool, M["aff"], e * 32 + 32)
                    split_set(e + 2, par)

            qT = all_tiles(pool)
            alone(pool, M["store"], qT * 16)
            alone(pool, M["xLo"], qT + 1)
            pool.wait_ge(s_place, 4)

            def combine_gathers(a):
                for j in range(CB):
                    n = a * CB + j
                    if not (isinstance(a, int) and a == 0):
                        alone(pool, s_cacc, n - CB + 1)
                        alone(pool, s_cy[j], 32 * a + CY0)
                    pool.tensor_copy(c_idx[:, j, :], posi[:, n, :] if isinstance(n, int) else
                                     posi[:, bass.ds(n, 1), :].rearrange("p a j -> p (a j)")).then_inc(s_cidx, 1)
                    alone(pool, s_cidx, n + 1)
                    for i in range(2):
                        pool.indirect_dma_start(
                            c_y[:, j, i, :], None, y_d,
                            bass.IndirectOffsetOnAxis(ap=c_idx[:, j, i:i + 1], axis=0)).then_inc(s_cy[j], 16)

            combine_gathers(0)
            with pool.Fori(1, NT // CB) as a:
                combine_gathers(a)

        @block.scalar
        def _(act):
            act.wait_ge(s_const, CONST)

            def ln_sqrt(c):
                act.wait_ge(s_ln_mv, c + 1)
                pj = ln_part(ln_mv[c % 2], c)
                act.activation(ln_std[c % 2][0:pj.shape[0], 0:pj.shape[1]], pj[:, :, 1], ACT.Sqrt,
                               bias=eps_col[0:pj.shape[0], 0:1], scale=1.0).then_inc(s_ln_std, 1)

            def ln_norm(c):
                act.wait_ge(s_ln_b, c + 1)
                if c >= LN_BUF:
                    act.wait_ge(s_xn[c % LN_BUF], 16 * (c // LN_BUF))
                for j in ln_rows(c):
                    pn = slice(0, P if c < LN_CH - 1 else LN_LEFT)
                    i = act.activation(ln_out[c % LN_BUF][pn, j, :], ln_in[c % LN_BUF][pn, j, :], ACT.Identity,
                                       bias=ln_b[c % 2][pn, j:j + 1], scale=ln_r[c % 2][pn, j:j + 1])
                i.then_inc(s_ln_out, 1)

            ln_sqrt(0)
            for c in range(LN_CH):
                if c + 1 < LN_CH:
                    ln_sqrt(c + 1)
                ln_norm(c)
                if c == WSPLIT_AT:
                    weights_hi(act, 0, 0)

            act.wait_ge(s_tab, TAB_DONE)
            for l in range(2):
                S = L[l]
                all_xn(act)
                first = value(act, tab_next[0:1, 0:1], ET * PACK) // PACK
                act.activation(idx[:, 0:ST], srcT[:, bass.ds(within(first, ET), ST)],
                               ACT.Copy).then_inc(S["idx"], len(CHUNKS))
                weights_hi(act, l + 1, 1 - l)
                first_next = [None]

                def next_tile(g, t):
                    first_next[0] = t

                def half(k, g, x, t):
                    if k < ST:
                        act.wait_ge(L_rows[l][k], (g + (l * NT + 1)) * 16)
                        act.wait_ge(S["seg"], free_at(g, k))
                    else:
                        act.wait_ge(L_rows[l][k], x * 16 + 16)
                        act.wait_ge(S["seg"], free_at(g, k))
                        act.wait_ge(S["segx"], x + 1)
                    act.activation(r_hi[:, ring(k), :], rows[:, k, :], ACT.Copy) \
                        .then_inc(S["hi"] if k < ST else S["hix"], 1)
                    for a, w in CHUNKS.items():
                        if k == a + w - 1 and k < ST:
                            act.activation(idx[:, a:a + w], srcT[:, bass.ds(first_next[0] + a, w)],
                                           ACT.Copy).then_inc(S["idx"], 1)

                def loop_end(x1):
                    alone(act, S["segx"], x1 + 1)

                def evac(g):
                    act.wait_ge(S["node"], g + 1)
                    if l == 0:
                        act.wait_ge(S["rdeg"], g + 1)
                    act.wait_ge(S["aggT"], g)
                    act.activation(agg_s[:], agg_of(g), ACT.Identity,
                                   scale=rdeg[:, g:g + 1] if isinstance(g, int) else
                                   rdeg[:, bass.ds(g, 1)]).then_inc(S["evac"], 1)

                def self_hi(n):
                    act.wait_ge(S["selfT"], n + 1)
                    act.wait_ge(S["selfUsed"], n)
                    act.activation(sT[:, 0].rearrange("p k n -> p (k n)"), sT_p, ACT.Copy).then_inc(S["selfHi"], 1)

                def agg_hi(n):
                    act.wait_ge(S["aggT"], n + 1)
                    act.wait_ge(S["dense"], n)
                    act.activation(aT[:, 0].rearrange("p k n -> p (k n)"), aT_p, ACT.Copy).then_inc(S["aggHi"], 1)

                def relu(n):
                    act.wait_ge(S["dense"], n + 1)
                    act.wait_ge(S["store"], n * 16)
                    act.activation(h_t[:], dense_p, ACT.Relu).then_inc(S["res"], 1)

                def sqrt2(n):
                    act.wait_ge(S["mv"], n + 1)
                    act.activation(std[:], mv[:, 1:2], ACT.Sqrt, bias=eps_col[:, 0:1],
                                   scale=1.0).then_inc(S["std"], 1)

                def norm2(n):
                    act.wait_ge(S["nmr"], n + 1)
                    act.wait_ge(S["xT"], n)
                    act.activation(xn2_t[:], x2_t[:], ACT.Identity, bias=nmr[:, 0:1],
                                   scale=rstd[:, 0:1]).then_inc(S["xn2"], 1)

                def norm2_again(n):
                    act.wait_ge(S["scat"], n * 32)
                    act.activation(xn2_s[:], x2_t[:], ACT.Identity, bias=nmr[:, 0:1],
                                   scale=rstd[:, 0:1]).then_inc(S["xns"], 1)

                def xT_copy(n):
                    act.wait_ge(S["xT"], n + 1)
                    act.wait_ge(S["logit"], n)
                    act.activation(xT[:].rearrange("p k n -> p (k n)"), xT_p, ACT.Copy).then_inc(S["xTc"], 1)

                hooks = {3: [(evac, 1)], 7: [(agg_hi, 1)], 15: [(self_hi, 0)]}
                if l == 0:
                    hooks[17] = [(relu, 1)]
                else:
                    hooks.update({4: [(sqrt2, 2)], 6: [(norm2, 2)], 10: [(xT_copy, 2)], 13: [(norm2_again, 2)]})
                layer(act, half, hooks, tab_next, opening=next_tile, loop_end=loop_end)

            def x_hi(q):
                act.wait_ge(M["xT"], q + 1)
                act.wait_ge(M["h"], q)
                act.activation(m_xT[:, 0].rearrange("p k n -> p (k n)"), mxT_p, ACT.Copy).then_inc(M["xHi"], 1)

            def h_hi(q):
                act.wait_ge(M["hT"], q + 1)
                act.wait_ge(M["y"], q + 1)
                act.activation(m_hT[:, 0].rearrange("p k n -> p (k n)"), mhT_p, ACT.Copy).then_inc(M["hHi"], 1)

            def m_relu(q):
                act.wait_ge(M["h"], q + 1)
                act.wait_ge(M["hT"], q)
                act.activation(m_h[:], mh_p, ACT.Relu).then_inc(M["relu"], 1)

            def m_norm(q):
                act.wait_ge(M["mv"], q + 1)
                act.activation(m_std[:], m_mv[:, 1:2], ACT.Sqrt, bias=eps_col[:, 0:1],
                               scale=1.0).then_inc(M["std"], 1)
                act.wait_ge(M["b"], q + 1)
                act.wait_ge(M["gam"], q)
                act.activation(m_n[:], my_p, ACT.Identity, bias=m_b[:, 0:1],
                               scale=m_r[:, 0:1]).then_inc(M["norm"], 1)

            act.wait_ge(s_cnt, CNT_DONE)
            qT = all_tiles(act)
            weights_hi(act, 3, 1)
            x_hi(0)

            def tile_m(q):
                if not isinstance(q, int) or q >= 1:
                    h_hi(q - 1)
                if not isinstance(q, int) or q >= 2:
                    m_norm(q - 2)
                m_relu(q)
                x_hi(q + 1)

            for q in range(3):
                tile_m(q)
            with act.Fori(3, qT) as q:
                tile_m(q)
            qe = last_but_one(act)
            h_hi(qe + 1)
            m_norm(qe)
            m_norm(qe + 1)

            act.wait_ge(s_cnt, 3)
            act.activation(gate_e[:], gate_d[:], ACT.Exp).then_inc(s_gexp, 1)

        @block.vector
        def _(dve):
            kv = [0]

            def didv(ins, wait=False):
                kv[0] += 1
                ins.then_inc(s_constv, 1)
                if wait:
                    dve.wait_ge(s_constv, kv[0])

            dve.wait_ge(s_const, CONST)
            didv(dve.tensor_copy(iota[:], iota_i[:]))
            didv(dve.tensor_copy(tid[:], tid_i[:]))
            didv(dve.tensor_copy(rsel[:, 0:1], rseli[:, 0:1]))
            didv(dve.tensor_scalar(rsel[:, 1:2], rseli[:, 1:2], -2.0, 3.0, ALU.mult, ALU.add))
            didv(dve.tensor_copy(thr[:], thr_i[:]), wait=True)
            didv(dve.memset(thr[:, NT - 1:NT], float(LAST)), wait=True)
            didv(dve.tensor_scalar(thr_hi[:], thr[:], float(P), None, ALU.add))
            didv(dve.tensor_copy(start_col[:, 0:NT], thr[:]))
            didv(dve.tensor_copy(start_col[:, NT:NT + 1], thr[:, 0:1]))
            didv(dve.memset(tab_next[:], 0))
            didv(dve.memset(top2[:], 0.0), wait=True)
            assert kv[0] == CONSTV

            kt = [0]

            def t(ins, wait=True):
                kt[0] += 1
                ins.then_inc(s_tab, 1)
                if wait:
                    dve.wait_ge(s_tab, kt[0])

            def ln_stats(c):
                dve.wait_ge(s_ln_in[c % LN_BUF], 16 * (c // LN_BUF + 1))
                pn = slice(0, P if c < LN_CH - 1 else LN_LEFT)
                for j in ln_rows(c):
                    i = dve.bn_stats(ln_bst[c % 2][pn, j, :], ln_in[c % LN_BUF][pn, j, :])
                i.then_inc(s_ln_st, 1)
                dve.wait_ge(s_ln_st, c + 1)
                if c >= 2:
                    dve.wait_ge(s_ln_out, c - 1)
                for j in ln_rows(c):
                    i = dve.bn_aggr(ln_mv[c % 2][pn, j, :], ln_bst[c % 2][pn, j, :])
                i.then_inc(s_ln_mv, 1)

            def ln_scale(c):
                dve.wait_ge(s_ln_std, c + 1)
                if c >= 2:
                    dve.wait_ge(s_ln_out, c - 1)
                std, r, b = (ln_part(t[c % 2], c) for t in (ln_std, ln_r, ln_b))
                dve.reciprocal(r, std).then_inc(s_ln_r, 1)
                dve.wait_ge(s_ln_r, c + 1)
                dve.scalar_tensor_tensor(out=b, in0=ln_part(ln_mv[c % 2], c)[:, :, 0], scalar=-1.0,
                                         in1=r, op0=ALU.mult, op1=ALU.mult).then_inc(s_ln_b, 1)

            def tables():
                dve.wait_ge(s_edges, 96)
                t(dve.tensor_copy(ed_f[:, 0], ed_i[:, 0]), wait=False)
                t(dve.tensor_copy(ed_f[:, 1], ed_i[:, 1]))
                t(dve.tensor_reduce(out=t_max[:], in_=ed_f[:, 1], axis=AX.X, op=ALU.max), wait=False)
                t(dve.tensor_reduce(out=t_min[:], in_=ed_f[:, 1], axis=AX.X, op=ALU.min))
                over_g = lambda a: a.unsqueeze(1).to_broadcast([EP, NT, EB])
                over_b = lambda a: a[0:EP, :].unsqueeze(2).to_broadcast([EP, NT, EB])
                t(dve.tensor_tensor(cmp_m[:], over_g(t_max[:]), over_b(thr[:]), ALU.is_lt))
                t(dve.scalar_tensor_tensor(out=cmp_v[:], in0=cmp_m[:], scalar=float(ET), in1=over_g(tid[:]),
                                           op0=ALU.mult, op1=ALU.max))
                t(dve.tensor_reduce(out=first_c[:], in_=cmp_v[:], axis=AX.X, op=ALU.min))
                t(dve.tensor_tensor(cmp_m[:], over_g(t_min[:]), over_b(thr_hi[:]), ALU.is_lt))
                t(dve.tensor_tensor(cmp_v[:], cmp_m[:], over_g(tid[:]), ALU.mult))
                t(dve.tensor_tensor(cmp_v[:], cmp_v[:], cmp_m[:], ALU.add))
                t(dve.tensor_reduce(out=end_c[:], in_=cmp_v[:], axis=AX.X, op=ALU.max))

            def tables2():
                dve.wait_ge(s_tabT, 1)
                t(dve.tensor_reduce(out=first_g[:], in_=ps[0:NT, 4, 0:EP], axis=AX.X, op=ALU.min), wait=False)
                t(dve.tensor_reduce(out=end_g[:], in_=ps[0:NT, 4, P:P + EP], axis=AX.X, op=ALU.max))
                t(dve.tensor_tensor(span_g[:], end_g[:], first_g[:], ALU.subtract))
                t(dve.tensor_scalar(n_g2[:], span_g[:], -float(ST), 0.0, ALU.add, ALU.max))
                dve.wait_ge(s_tabT, 2)
                for j in range(2):
                    dstl = srcT if j == 0 else dstT
                    t(dve.tensor_copy(dstl[:, 0:4 * EP], ps[:, 2 * j, 0:4 * EP]), wait=False)
                    t(dve.tensor_copy(dstl[:, 4 * EP:ET], ps[:, 2 * j + 1, 0:3 * EP]), wait=False)
                dve.wait_ge(s_tabT, 3)
                t(dve.tensor_copy(tab_extra[:], ps[0:1, 5, 0:NT + 1]), wait=False)
                t(dve.tensor_copy(f_row[:], ps[0:1, 5, P:P + NT]), wait=False)
                t(dve.tensor_copy(n_row[:, 0:NT], ps[0:1, 5, 2 * P:2 * P + NT]))
                t(dve.scalar_tensor_tensor(out=tab_tile[:], in0=f_row[:], scalar=float(PACK), in1=n_row[:, 0:NT],
                                           op0=ALU.mult, op1=ALU.add), wait=False)
                t(dve.tensor_scalar(tab_next[:, 0:1], f_row[:, 0:1], float(PACK), None, ALU.mult), wait=False)
                t(dve.scalar_tensor_tensor(out=tab_next[:, 1:NT], in0=f_row[:, 1:NT], scalar=float(PACK),
                                           in1=n_row[:, 0:NT - 1], op0=ALU.mult, op1=ALU.add), wait=False)
                t(dve.tensor_copy(tab_next[:, NT:NT + 1], n_row[:, NT - 1:NT]))
                assert kt[0] == TAB_DONE

            ln_stats(0)
            for c in range(LN_CH):
                if c + 1 < LN_CH:
                    ln_stats(c + 1)
                ln_scale(c)
                if c == 1:
                    tables()
                if c == 4:
                    tables2()
                if c == WSPLIT_AT:
                    weights_lo(dve, 0, 0)
                    biases(dve, 0, 0)

            dve.wait_ge(s_tab, TAB_DONE)
            for l in range(2):
                S = L[l]
                all_xn(dve)
                if l == 1:
                    dve.wait_ge(L[0]["lo"], NT * ST + ST)
                dve.sem_inc(S["lo"], ST)
                weights_lo(dve, l + 1, 1 - l)
                if l == 1:
                    dve.wait_ge(L[0]["dense"], NT)
                biases(dve, l + 1, 1 - l)
                if l == 1:
                    dve.wait_ge(L[0]["store"], 16 * NT)
                    dve.wait_ge(s_const2, 3)
                    dve.tensor_copy(ebase[:], ebase_i[:]).then_inc(s_cv2, 1)
                    dve.tensor_copy(ti[:], ti_i[:]).then_inc(s_cv2, 1)
                    dve.tensor_copy(tq[:], tq_i[:]).then_inc(s_cv2, 1)
                    dve.wait_ge(s_cv2, 1)
                    dve.tensor_copy(run[:], ebase[:]).then_inc(s_cv2, 1)
                    dve.wait_ge(s_cv2, 4)
                dve.sem_inc(S["lox"], 1)

                def of_tile(g):
                    return iota_g[:, g % 2, :] if isinstance(g, int) else \
                        iota_g[:, bass.ds(g % 2, 1), :].rearrange("p a j -> p (a j)")

                def tile_iota(g):
                    dve.tensor_scalar(of_tile(g), iota[:], start_col[:, g:g + 1] if isinstance(g, int) else
                                      start_col[:, bass.ds(g, 1)], None, ALU.add).then_inc(S["iota"], 1)

                def next_iota(g):
                    dve.wait_ge(S["lo"], g * ST + ST)
                    tile_iota(g + 1)

                def other_half(k, g, x, t):
                    if k % SELW == 0 or k == ST:
                        if k == 0:
                            dve.wait_ge(S["iota"], g + 1)
                        w = min(SELW, ST - k) if k < ST else 1
                        a = ring(k)
                        dve.wait_ge(S["seg"], free_at(g, k + w - 1 if k < ST else ST))
                        if k == ST:
                            dve.wait_ge(S["segx"], x + 1)
                        dve.tensor_tensor(
                            sel[:, a:a + w, :], of_tile(g).unsqueeze(1).to_broadcast([P, w, P]),
                            dstT[:, bass.ds(t, w)].unsqueeze(2).to_broadcast([P, w, P]), ALU.is_equal)
                    if k < ST:
                        dve.wait_ge(L_rows[l][k], (g + (l * NT + 1)) * 16)
                        dve.wait_ge(S["hi"], g * ST + (k + 1))
                    else:
                        dve.wait_ge(L_rows[l][k], x * 16 + 16)
                        dve.wait_ge(S["hix"], x + 1)
                    dve.tensor_tensor(r_lo[:, ring(k), :], rows[:, k, :], r_hi[:, ring(k), :].bitcast(F32),
                                      ALU.subtract).then_inc(S["lo"] if k < ST else S["lox"], 1)

                def loop_end(x1):
                    alone(dve, S["segx"], x1 + 1)

                def degree(g):
                    dve.wait_ge(S["node"], g + 1)
                    dve.tensor_scalar(deg_m[:], deg_of(g)[:, 0:1], 1.0, None, ALU.max).then_inc(S["rdeg0"], 1)

                def over_degree(g):
                    dve.wait_ge(S["rdeg0"], g + 1)
                    dve.reciprocal(rdeg[:, g:g + 1] if isinstance(g, int) else rdeg[:, bass.ds(g, 1)],
                                   deg_m[:]).then_inc(S["rdeg"], 1)

                def self_lo(n):
                    dve.wait_ge(S["selfHi"], n + 1)
                    dve.tensor_tensor(sT[:, 1].rearrange("p k n -> p (k n)"), sT_p,
                                      sT[:, 0].rearrange("p k n -> p (k n)").bitcast(F32),
                                      ALU.subtract).then_inc(S["selfLo"], 1)

                def agg_lo(n):
                    dve.wait_ge(S["aggHi"], n + 1)
                    dve.tensor_tensor(aT[:, 1].rearrange("p k n -> p (k n)"), aT_p,
                                      aT[:, 0].rearrange("p k n -> p (k n)").bitcast(F32),
                                      ALU.subtract).then_inc(S["aggLo"], 1)

                def residual(n):
                    dve.wait_ge(S["dense"], n + 1)
                    dve.wait_ge(S["xt"], n * 16 + 16)
                    dve.wait_ge(S["store"], n * 16)
                    dve.wait_ge(S["xns"], n)
                    dve.scalar_tensor_tensor(out=x2_t[:], in0=dense_p, scalar=0.0, in1=x_t[:], op0=ALU.max,
                                             op1=ALU.add).then_inc(S["res"], 1)

                def stats(n):
                    dve.wait_ge(S["res"], n + 1)
                    dve.bn_stats(bst[:], x2_t[:]).then_inc(S["bst"], 1)

                def moments(n):
                    alone(dve, S["bst"], n + 1)
                    dve.bn_aggr(mv[:], bst[:]).then_inc(S["mv"], 1)

                def scale(n):
                    dve.wait_ge(S["std"], n + 1)
                    dve.reciprocal(rstd[:], std[:]).then_inc(S["rstd"], 1)

                def offset(n):
                    dve.wait_ge(S["rstd"], n + 1)
                    dve.scalar_tensor_tensor(out=nmr[:], in0=mv[:, 0:1], scalar=-1.0, in1=rstd[:],
                                             op0=ALU.mult, op1=ALU.mult).then_inc(S["nmr"], 1)

                def logits(n):
                    dve.wait_ge(S["logit"], n + 1)
                    dve.tensor_copy(lg[:], lg_p).then_inc(S["lg"], 1)

                def largest(n):
                    alone(dve, S["lg"], n + 1)
                    dve.max(mx8[:], lg[:]).then_inc(S["mx"], 1)

                def experts(n):
                    alone(dve, S["mx"], n + 1)
                    dve.max_index(ix8[:], mx8[:], lg[:]).then_inc(S["ix"], 1)

                def numbers(n):
                    one = (lambda a: a[:, :, n:n + 1]) if isinstance(n, int) else (lambda a: a[:, :, bass.ds(n, 1)])
                    dve.tensor_copy(one(top2[:]), mx8[:, 0:2].unsqueeze(2))
                    dve.wait_ge(S["ix"], n + 1)
                    dve.tensor_copy(e01[:], ix8[:, 0:2]).then_inc(S["e01"], 1)

                def masks(n):
                    dve.wait_ge(S["e01"], n + 1)
                    dve.wait_ge(S["pref"], n)
                    dve.tensor_tensor(mask[:], iota[:, 0:NE].unsqueeze(1).to_broadcast([P, 2, NE]),
                                      e01[:].unsqueeze(2).to_broadcast([P, 2, NE]), ALU.is_equal) \
                        .then_inc(S["mask"], 1)

                def places(n):
                    dve.wait_ge(S["pref"], n + 1)
                    dve.tensor_tensor(prod[:], mask[:], pre_p[:, 0:NE].unsqueeze(1).to_broadcast([P, 2, NE]),
                                      ALU.mult).then_inc(S["prod"], 1)
                    dve.tensor_copy(run[:], pre_p[:, NE:2 * NE]).then_inc(S["run"], 1)

                def of_node(n):
                    return posf[:, n, :] if isinstance(n, int) else posf[:, bass.ds(n, 1), :].rearrange("p a j -> p (a j)")

                def positions(n):
                    dve.wait_ge(S["prod"], n + 1)
                    dve.tensor_reduce(out=of_node(n), in_=prod[:], axis=AX.X, op=ALU.add).then_inc(S["pos"], 1)

                def scatter_to(n):
                    dve.wait_ge(S["pos"], n + 1)
                    alone(dve, S["scat"], n * 32)
                    dve.tensor_copy(pos_now[:], of_node(n)).then_inc(S["posi"], 1)

                hooks = {7: [(agg_lo, 1)], 8: [(next_iota, 0)], 15: [(self_lo, 0)]}
                if l == 0:
                    hooks.update({1: [(degree, 1)], 2: [(over_degree, 1)]})
                else:
                    hooks.update({16: [(residual, 1)], 17: [(stats, 1)], 0: [(moments, 2)], 4: [(scale, 2)],
                                  5: [(offset, 2)], 11: [(logits, 2)], 12: [(largest, 2)], 13: [(experts, 2)],
                                  14: [(numbers, 2)], 1: [(places, 3)], 2: [(positions, 3)], 3: [(scatter_to, 3)]})
                    hooks[15].append((masks, 2))
                tile_iota(0)
                layer(dve, other_half, hooks, tab_tile, loop_end=loop_end)

            kc = [0]

            def cstep(ins):
                kc[0] += 1
                ins.then_inc(s_cnt, 1)
                dve.wait_ge(s_cnt, kc[0])

            dve.wait_ge(L[1]["posi"], NT)
            dve.wait_ge(L[1]["run"], NT)
            cstep(dve.memset(zrow, 0.0))
            cstep(dve.tensor_copy(tab_rows[:], run[0:1, :]))
            cstep(dve.tensor_tensor(gate_d[:], top2[:, 1, :], top2[:, 0, :], ALU.subtract))
            cstep(dve.tensor_tensor(nrow[:], run[:], ebase[:], ALU.subtract))
            cstep(dve.tensor_tensor(ti_c, ti[:], nrow[:].unsqueeze(2).to_broadcast([P, NE, NT]), ALU.is_lt))
            cstep(dve.tensor_reduce(out=ntile[:], in_=ti_c, axis=AX.X, op=ALU.add))
            cstep(dve.memset(tcum[:], 0.0))
            for e in range(NE):
                cstep(dve.tensor_tensor(tcum[:, e + 1:e + 2], tcum[:, e:e + 1], ntile[0:1, e:e + 1], ALU.add))
            cstep(dve.tensor_copy(tab_tiles[:], tcum[:]))
            cstep(dve.tensor_scalar(tab_end[:, 0:1], tcum[:, NE:NE + 1], -2.0, None, ALU.add))
            cstep(dve.tensor_scalar(tab_end[:, 1:2], tcum[:, NE:NE + 1], -1.0, float(YT), ALU.mult, ALU.add))
            cstep(dve.tensor_scalar(shift[:], ntile[:], float(P), float(REGION), ALU.mult, ALU.subtract))
            over_q = lambda a: a.unsqueeze(1).to_broadcast([1, TQ, NE])
            cstep(dve.tensor_tensor(t_cmp, tq[:].unsqueeze(2).to_broadcast([1, TQ, NE]), over_q(tcum[:, 1:NE + 1]),
                                    ALU.is_ge))
            cstep(dve.tensor_reduce(out=t_e[:], in_=t_cmp, axis=AX.X, op=ALU.add))
            cstep(dve.tensor_scalar(tab_use[:, 0:1], t_e[:, 0:1], float(PACK), None, ALU.mult))
            cstep(dve.scalar_tensor_tensor(out=tab_use[:, 1:TQ], in0=t_e[:, 1:TQ], scalar=float(PACK),
                                           in1=t_e[:, 0:TQ - 1], op0=ALU.mult, op1=ALU.add))
            cstep(dve.tensor_tensor(t_val, t_cmp, over_q(shift[0:1, :]), ALU.mult))
            cstep(dve.tensor_reduce(out=t_row[:], in_=t_val, axis=AX.X, op=ALU.add))
            cstep(dve.scalar_tensor_tensor(out=t_row[:], in0=tq[:], scalar=float(P), in1=t_row[:], op0=ALU.mult,
                                           op1=ALU.subtract))
            cstep(dve.scalar_tensor_tensor(out=tab_row[:], in0=t_e[:], scalar=float(NE), in1=t_row[:], op0=ALU.is_lt,
                                           op1=ALU.mult))
            assert kc[0] == CNT_DONE
            for i, ins in enumerate((
                    lambda: dve.tensor_tensor(
                        pos_c[:], posf[:].rearrange("p n j -> p (n j)").unsqueeze(2).to_broadcast([P, 2 * NT, NE - 1]),
                        ebase[:, 1:NE].unsqueeze(1).to_broadcast([P, 2 * NT, NE - 1]), ALU.is_ge),
                    lambda: dve.tensor_tensor(
                        pos_c[:], pos_c[:], shift[:, 0:NE - 1].unsqueeze(1).to_broadcast([P, 2 * NT, NE - 1]),
                        ALU.mult),
                    lambda: dve.tensor_reduce(out=pos_s[:], in_=pos_c[:], axis=AX.X, op=ALU.add),
                    lambda: dve.tensor_tensor(posi[:].rearrange("p n j -> p (n j)"), pos_s[:],
                                              posf[:].rearrange("p n j -> p (n j)"), ALU.add))):
                ins().then_inc(s_place, 1)
                dve.wait_ge(s_place, i + 1)

            def x_lo(q):
                dve.wait_ge(M["xHi"], q + 1)
                dve.tensor_tensor(m_xT[:, 1].rearrange("p k n -> p (k n)"), mxT_p,
                                  m_xT[:, 0].rearrange("p k n -> p (k n)").bitcast(F32),
                                  ALU.subtract).then_inc(M["xLo"], 1)

            def h_lo(q):
                dve.wait_ge(M["hHi"], q + 1)
                dve.tensor_tensor(m_hT[:, 1].rearrange("p k n -> p (k n)"), mhT_p,
                                  m_hT[:, 0].rearrange("p k n -> p (k n)").bitcast(F32),
                                  ALU.subtract).then_inc(M["hLo"], 1)

            def m_stats(q):
                dve.wait_ge(M["y"], q + 2)
                dve.bn_stats(m_bst[:], my_p).then_inc(M["bst"], 1)
                alone(dve, M["bst"], q + 1)
                dve.bn_aggr(m_mv[:], m_bst[:]).then_inc(M["mv"], 1)

            def m_scales(q):
                dve.wait_ge(M["std"], q + 1)
                dve.reciprocal(m_r[:], m_std[:]).then_inc(M["r"], 1)
                dve.wait_ge(M["r"], q + 1)
                dve.scalar_tensor_tensor(out=m_b[:], in0=m_mv[:, 0:1], scalar=-1.0, in1=m_r[:],
                                         op0=ALU.mult, op1=ALU.mult).then_inc(M["b"], 1)

            def m_affine(q, e):
                alone(dve, s_wset, e + 3)
                at = lambda t: t[:, bass.ds(e % 2, 1), :].rearrange("p a d -> p (a d)")
                dve.wait_ge(M["norm"], q + 1)
                dve.tensor_tensor(m_ng[:], m_n[:], at(gam), ALU.mult).then_inc(M["gam"], 1)
                dve.wait_ge(M["gam"], q + 1)
                dve.wait_ge(M["store"], q * 16)
                dve.tensor_tensor(m_y[:], m_ng[:], at(bet), ALU.add).then_inc(M["out"], 1)

            def expert_before(q):
                cell = tab_use[0:1, q:q + 1] if isinstance(q, int) else tab_use[0:1, bass.ds(q, 1)]
                return within(value(dve, cell, (PACK + 1) * NE) % PACK, NE - 1)

            dve.sem_inc(M["out"], 1)
            qT = all_tiles(dve)
            weights_lo(dve, 3, 1)
            biases(dve, 3, 1)
            x_lo(0)
            dve.wait_ge(M["aff"], 64)

            def tile_m(q):
                if not isinstance(q, int) or q >= 2:
                    e = expert_before(q - 1)
                    m_stats(q - 2)
                if not isinstance(q, int) or q >= 1:
                    h_lo(q - 1)
                if not isinstance(q, int) or q >= 2:
                    m_scales(q - 2)
                    m_affine(q - 2, e)
                x_lo(q + 1)

            for q in range(3):
                tile_m(q)
            with dve.Fori(3, qT) as q:
                tile_m(q)
            qe = last_but_one(dve)
            for i in range(2):
                q = qe + i
                e = expert_before(q + 1)
                m_stats(q)
                if i == 0:
                    h_lo(qe + 1)
                m_scales(q)
                m_affine(q, e)

            dve.wait_ge(s_gexp, 1)
            dve.tensor_scalar(gate_d[:], gate_e[:], 1.0, None, ALU.add).then_inc(s_gate, 1)
            dve.wait_ge(s_gate, 1)
            dve.reciprocal(gate[:, 0, :], gate_d[:]).then_inc(s_gate, 1)
            dve.wait_ge(s_gate, 2)
            dve.tensor_tensor(gate[:, 1, :], gate_e[:], gate[:, 0, :], ALU.mult).then_inc(s_gate, 1)
            dve.wait_ge(s_gate, 3)

            def combine(a, ahead):
                for j in range(CB):
                    n = a * CB + j
                    w = [gate[:, i, n:n + 1] if isinstance(n, int) else gate[:, i, bass.ds(n, 1)] for i in range(2)]
                    dve.wait_ge(s_cy[j], 32 * a + (32 + CY0))
                    if j == 0 and ahead:
                        dve.wait_ge(s_cx, 16 * CB * PRE)
                    elif j == 0:
                        dve.wait_ge(s_cx2, 16 * CB * a - 16 * CB * (PRE - 1))
                    if not (isinstance(a, int) and a == 0):
                        dve.wait_ge(s_out[j], 16 * a + OUT0[j])
                    dve.scalar_tensor_tensor(out=c_t[:, j, :], in0=c_y[:, j, 0, :], scalar=w[0],
                                             in1=x2_of(n if ahead else n % (CB * PRE)), op0=ALU.mult, op1=ALU.add).then_inc(s_ct, 1)
                    dve.wait_ge(s_ct, n + 1)
                    dve.scalar_tensor_tensor(out=c_t[:, j, :], in0=c_y[:, j, 1, :], scalar=w[1],
                                             in1=c_t[:, j, :], op0=ALU.mult, op1=ALU.add).then_inc(s_cacc, 1)

            def x2_of(slot):
                return c_x[:, slot, :] if isinstance(slot, int) else \
                    c_x[:, bass.ds(slot, 1), :].rearrange("p a d -> p (a d)")

            combine(0, True)
            with dve.Fori(1, PRE) as a:
                combine(a, True)
            for a in range(PRE, NT // CB):
                combine(a, False)

        @block.tensor
        def _(pe):
            pe.wait_ge(s_const, CONST)
            pe.wait_ge(s_tab, 11)
            pe.transpose(ps[0:NT, 4, 0:EP], first_c[:], ident[0:EP, 0:EP])
            pe.transpose(ps[0:NT, 4, P:P + EP], end_c[:], ident[0:EP, 0:EP]).then_inc(s_tabT, 1)
            for j in range(2):
                for b in range(EB):
                    i = pe.transpose(ps[:, 2 * j + b // 4, (b % 4) * EP:(b % 4 + 1) * EP], ed_f[:, j, b, :],
                                     ident[0:EP, 0:EP])
            i.then_inc(s_tabT, 1)
            pe.wait_ge(s_tab, 15)
            pe.matmul(ps[0:1, 5, 0:NT + 1], n_g2[:, 0:1], upper[0:NT, 0:NT + 1], start=True, stop=True)
            pe.matmul(ps[0:1, 5, 2 * P:2 * P + NT], n_g2[:, 0:1], ident[0:NT, 0:NT], start=True, stop=True)
            pe.matmul(ps[0:1, 5, P:P + NT], first_g[:, 0:1], ident[0:NT, 0:NT], start=True, stop=True) \
                .then_inc(s_tabT, 1)

            def product(out_ap, w, lhs, chunks, stop):
                for k in chunks:
                    for a, b in ((0, 0), (1, 0), (0, 1)):
                        i = pe.matmul(out_ap, lhs[:, a, k, :], w[:, b, k, :], start=False,
                                      stop=stop and k == chunks[-1] and (a, b) == (0, 1))
                return i

            pe.wait_ge(s_tab, TAB_DONE)
            for l in range(2):
                S = L[l]
                pe.sem_inc(S["seg"], RING)
                pe.sem_inc(S["segx"], 1)

                def opening(g, t0):
                    if not (isinstance(g, int) and g < 2):
                        pe.wait_ge(S["evac"], g - 1)
                    pe.matmul(agg_of(g), zero2[:], zero_row[:], start=True, stop=False)
                    if l == 0:
                        pe.matmul(deg_of(g), zero2[:], zero_row[:, 0:2], start=True, stop=False)

                def sums(k, g, x, t):
                    a = ring(k)
                    if k < ST:
                        pe.wait_ge(S["lo"], g * ST + (k + 1 + ST))
                    else:
                        pe.wait_ge(S["lox"], x + 2)
                    if l == 0:
                        pe.matmul(deg_of(g), sel[:, a, :], ones_col[:], start=False, stop=False)
                    pe.matmul(agg_of(g), sel[:, a, :], r_hi[:, a, :], start=False, stop=False)
                    pe.matmul(agg_of(g), sel[:, a, :], r_lo[:, a, :], start=False, stop=False) \
                        .then_inc(S["seg"] if k < ST else S["segx"], 1)

                def closing(g):
                    if l == 0:
                        pe.matmul(deg_of(g), zero2[:], zero_row[:, 0:2], start=False, stop=True)
                    pe.matmul(agg_of(g), zero2[:], zero_row[:], start=False, stop=True).then_inc(S["node"], 1)

                def self_t_t(n):
                    pe.wait_ge(S["self"], n * 16 + 16)
                    pe.wait_ge(S["selfLo"], n)
                    for k in range(KC):
                        i = pe.transpose(sT_p[:, k * P:(k + 1) * P], self_t[:, k * P:(k + 1) * P], ident[:])
                    i.then_inc(S["selfT"], 1)

                def agg_t(n):
                    pe.wait_ge(S["evac"], n + 1)
                    pe.wait_ge(S["aggLo"], n)
                    for k in range(KC):
                        i = pe.transpose(aT_p[:, k * P:(k + 1) * P], agg_s[:, k * P:(k + 1) * P], ident[:])
                    i.then_inc(S["aggT"], 1)

                def dense(k):
                    def step(n):
                        if k == 0:
                            pe.wait_ge(S["res"], n)
                            pe.wait_ge(s_wset, l + 1)
                            pe.matmul(dense_p, one2[:], bias[l][:, 0, :], start=True, stop=False)
                            pe.wait_ge(S["selfLo"], n + 1)
                        if k == KC:
                            pe.wait_ge(S["aggLo"], n + 1)
                        i = product(dense_p, wts[l][:, 1 - k // KC], sT if k < KC else aT, (k % KC,), k == 2 * KC - 1)
                        if k == KC - 1:
                            i.then_inc(S["selfUsed"], 1)
                        if k == 2 * KC - 1:
                            i.then_inc(S["dense"], 1)
                    return step

                def xT_t(n):
                    pe.wait_ge(S["xn2"], n + 1)
                    pe.wait_ge(S["xTc"], n)
                    for k in range(KC):
                        i = pe.transpose(xT_p[:, k * P:(k + 1) * P], xn2_t[:, k * P:(k + 1) * P], ident[:])
                    i.then_inc(S["xT"], 1)

                def logits(n):
                    pe.wait_ge(S["xTc"], n + 1)
                    pe.wait_ge(s_wg, 16)
                    pe.wait_ge(S["lg"], n)
                    for k in range(KC):
                        i = pe.matmul(lg_p, xT[:, k, :], wg_s[:, k, :], start=k == 0, stop=k == KC - 1)
                    i.then_inc(S["logit"], 1)

                def prefix(n):
                    pe.wait_ge(S["mask"], n + 1)
                    pe.wait_ge(S["run"], n)
                    for c, before in ((0, upper), (NE, onesq)):
                        pe.matmul(pre_p[:, c:c + NE], row0[:], run[:], start=True, stop=False)
                        for j in range(2):
                            i = pe.matmul(pre_p[:, c:c + NE], before[:], mask[:, j, :], start=False, stop=j == 1)
                    i.then_inc(S["pref"], 1)

                if l == 1:
                    pe.wait_ge(s_cv2, 4)
                    pe.wait_ge(L[0]["rdeg0"], NT)
                hooks = {2 * k: [(dense(k), 1)] for k in range(2 * KC)}
                hooks[3] = [(agg_t, 1)]
                hooks[11] = [(self_t_t, 0)]
                if l == 1:
                    hooks.update({5: [(xT_t, 2)], 9: [(logits, 2)], 17: [(prefix, 2)]})
                layer(pe, sums, hooks, tab_tile, opening=opening, tail=closing)

            def x_t_m(q):
                pe.wait_ge(M["x"], q * 16 + 16)
                pe.wait_ge(M["xLo"], q)
                for k in range(KC):
                    i = pe.transpose(mxT_p[:, k * P:(k + 1) * P], m_x[:, k * P:(k + 1) * P], ident[:])
                i.then_inc(M["xT"], 1)

            def mm1(q, w):
                pe.wait_ge(M["relu"], q)
                pe.matmul(mh_p, one2[:], w[1][:, 0, :], start=True, stop=False)
                pe.wait_ge(M["xLo"], q + 1)
                product(mh_p, w[0][:, 0], m_xT, range(KC), True).then_inc(M["h"], 1)

            def h_t_m(q):
                pe.wait_ge(M["relu"], q + 1)
                pe.wait_ge(M["hLo"], q)
                for k in range(KC):
                    i = pe.transpose(mhT_p[:, k * P:(k + 1) * P], m_h[:, k * P:(k + 1) * P], ident[:])
                i.then_inc(M["hT"], 1)

            def mm2(q, w):
                pe.wait_ge(M["norm"], q)
                pe.matmul(my_p, one2[:], w[1][:, 1, :], start=True, stop=False)
                pe.wait_ge(M["hLo"], q + 1)
                product(my_p, w[0][:, 1], m_hT, range(KC), True).then_inc(M["y"], 1)

            def weights_of(e):
                par = e % 2
                return wts_all[:, bass.ds(par * 2, 2)], bias_all[:, bass.ds(par * 2, 2)]

            def experts_of(q):
                cell = tab_use[0:1, q:q + 1] if isinstance(q, int) else tab_use[0:1, bass.ds(q, 1)]
                packed = value(pe, cell, (PACK + 1) * NE)
                return within(packed // PACK, NE), within(packed % PACK, NE - 1)

            pe.wait_ge(s_cnt, CNT_DONE)
            pe.sem_inc(M["y"], 1)
            qT = all_tiles(pe)
            x_t_m(0)

            def tile_m(q):
                e, e_before = experts_of(q)
                if not isinstance(q, int) or q >= 1:
                    h_t_m(q - 1)
                pe.wait_ge(s_wset, e + 3)
                mm1(q, weights_of(e))
                x_t_m(q + 1)
                if not isinstance(q, int) or q >= 1:
                    mm2(q - 1, weights_of(e_before))

            for q in range(2):
                tile_m(q)
            with pe.Fori(2, qT) as q:
                tile_m(q)
            ql = last_but_one(pe) + 1
            w = weights_of(experts_of(ql)[0])
            h_t_m(ql)
            mm2(ql, w)


_INS = ['x', 'src', 'dst', 'L0_gnn_W_self1', 'L0_gnn_W_neigh1', 'L0_gnn_b1', 'L0_gnn_W_self2', 'L0_gnn_W_neigh2',
        'L0_gnn_b2', 'L0_ffn_Wg', 'L0_ffn_W1', 'L0_ffn_b1', 'L0_ffn_W2', 'L0_ffn_b2', 'L0_ffn_gamma', 'L0_ffn_beta']


def kernel(**inputs):
    import concourse.bacc as bacc
    from concourse.bass_utils import run_bass_kernel_spmd

    nc = bacc.Bacc("TRN2", target_bir_lowering=False, num_devices=1)
    arrays, args = {}, []
    for name in _INS:
        a = np.ascontiguousarray(inputs[name])
        arrays[f"in_{name}"] = a
        args.append(nc.dram_tensor(f"in_{name}", a.shape, mybir.dt.from_np(a.dtype), kind="ExternalInput").ap())
    args.append(nc.dram_tensor("out_0", (N, D), F32, kind="ExternalOutput").ap())
    build(nc, *args)
    r = run_bass_kernel_spmd(nc, [arrays], core_ids=[0])
    return r.results[0]["out_0"]
```
